# Optimizing a Trainium2 kernel written in Bass

```python
import numpy as np
import jax
import jax.numpy as jnp

def _softmax(x, axis=-1):
    return jax.nn.softmax(x, axis=axis)

def _gelu(x):
    return jax.nn.gelu(x, approximate=True)

def _silu(x):
    return jax.nn.silu(x)

def _sigmoid(x):
    return jax.nn.sigmoid(x)

def _layernorm(x, axis=-1, eps=1e-05):
    m = jnp.mean(x, axis=axis, keepdims=True)
    v = jnp.var(x, axis=axis, keepdims=True)
    return (x - m) / jnp.sqrt(v + eps)

def _scatter_add(tgt, idx, src, axis=0):
    return tgt.at[idx].add(src)

def _segment_sum(src, seg, n):
    return jax.ops.segment_sum(src, seg, n)
kernel_name = 'mk_flamingo_gated_d2_seqx_r4_470475'

def setup_inputs(seed: int=0):
    np.random.seed(seed)
    _w = jnp.asarray

    def _rec_inputs():
        import jax
        import jax.numpy as jnp
        _rk = jax.random.key(seed)
        x = 7.22e-05 + 1 * jax.random.normal(jax.random.fold_in(_rk, 1), (4, 512, 256), jnp.float32)
        _lenS = 512 - jax.random.randint(jax.random.fold_in(_rk, 7), (4,), 0, max(1, 512 // 4) + 1, jnp.int32)
        _lenS2 = 512 - jax.random.randint(jax.random.fold_in(_rk, 8), (4,), 0, max(1, 512 // 4) + 1, jnp.int32)
        _ctx_1024P = jax.random.normal(jax.random.fold_in(_rk, 11), (4, 16, 256), jnp.float32)
        _ctx_1024c = jax.random.dirichlet(jax.random.fold_in(_rk, 511), 0.3 * jnp.ones((16,), jnp.float32), (4, 512))
        _ctx_1024t = jnp.einsum('bsk,bkd->bsd', _ctx_1024c, _ctx_1024P)
        _ctx_1024t = _ctx_1024t * jax.lax.rsqrt(jnp.mean(jnp.square(_ctx_1024t)) + 1e-12) * 0.953939
        ctx_1024 = 4.13588e-05 + 0.999923 * (_ctx_1024t + 0.3 * jax.random.normal(jax.random.fold_in(_rk, 611), (4, 512, 256), jnp.float32))
        _g = jax.random.normal(jax.random.fold_in(_rk, 9001), (2, 2), jnp.float32)
        _g = jnp.sign(_g) * jnp.maximum(jnp.abs(_g), 1.0) + (_g == 0) * 1.0
        g_xattn = _g[0]
        g_ffn = _g[1]
        return (x, ctx_1024, g_xattn, g_ffn)
    x, ctx_1024, g_xattn, g_ffn = _rec_inputs()

    def _L0_xattn_setup():
        import jax, jax.numpy as jnp
        import numpy as np
        D_MODEL = 256
        NUM_HEADS = 16
        D_K = D_MODEL // NUM_HEADS
        key = jax.random.key(seed)
        ks = jax.random.split(key, 7)
        B, S = (4, 512)
        scale = 1.0 / np.sqrt(D_MODEL)
        return {'query': jax.random.normal(ks[0], (B, S, D_MODEL), dtype=jnp.float32), 'key': jax.random.normal(ks[1], (B, S, D_MODEL), dtype=jnp.float32), 'value': jax.random.normal(ks[2], (B, S, D_MODEL), dtype=jnp.float32), 'W_q': jax.random.normal(ks[3], (D_MODEL, D_MODEL), dtype=jnp.float32) * scale, 'W_k': jax.random.normal(ks[4], (D_MODEL, D_MODEL), dtype=jnp.float32) * scale, 'W_v': jax.random.normal(ks[5], (D_MODEL, D_MODEL), dtype=jnp.float32) * scale, 'W_o': jax.random.normal(ks[6], (D_MODEL, D_MODEL), dtype=jnp.float32) * scale}
    _L0_xattn_all = _L0_xattn_setup()
    _L0_xattn_in = {k: v for k, v in _L0_xattn_all.items() if k in ('W_q', 'W_k', 'W_v', 'W_o')}
    del _L0_xattn_all

    def _L0_ffn_setup():
        import jax, jax.numpy as jnp
        import numpy as np
        SL, BS, HS, FF, E, TOPK = (512, 2, 256, 1024, 8, 2)
        key = jax.random.key(seed)
        ks = jax.random.split(key, 6)
        T = SL * BS
        x = jax.random.normal(ks[0], (SL, BS, HS), jnp.float32)
        scores = jax.random.uniform(ks[1], (T, E), jnp.float32)
        expert_weights = jax.random.uniform(ks[2], (T, TOPK), jnp.float32)
        expert_indices = jax.random.randint(ks[3], (T, TOPK), 0, E, jnp.int32)
        w1 = jax.random.normal(ks[4], (E, HS, FF), jnp.float32) * (1.0 / np.sqrt(HS))
        w2 = jax.random.normal(ks[5], (E, FF, HS), jnp.float32) * (1.0 / np.sqrt(FF))
        bias = jnp.zeros((HS,), jnp.float32)
        return dict(x=x, scores=scores, expert_weights=expert_weights, expert_indices=expert_indices, w1=w1, w2=w2, bias=bias)
    _L0_ffn_all = _L0_ffn_setup()
    _L0_ffn_in = {k: v for k, v in _L0_ffn_all.items() if k in ('scores', 'expert_weights', 'expert_indices', 'w1', 'w2', 'bias')}
    del _L0_ffn_all

    def _L1_xattn_setup():
        import jax, jax.numpy as jnp
        import numpy as np
        NUM_HEADS = 16
        D_MODEL = 256
        D_K = D_MODEL // NUM_HEADS

        def _split_heads(x):
            B, S, _ = x.shape
            return x.reshape(B, S, NUM_HEADS, D_K).transpose(0, 2, 1, 3)
        key = jax.random.key(seed)
        ks = jax.random.split(key, 11)
        B, S = (2, 512)
        s = 1.0 / np.sqrt(D_MODEL)
        return {'Q': jax.random.normal(ks[0], (B, S, D_MODEL), jnp.float32), 'K': jax.random.normal(ks[1], (B, S, D_MODEL), jnp.float32), 'V': jax.random.normal(ks[2], (B, S, D_MODEL), jnp.float32), 'Wq': jax.random.normal(ks[3], (D_MODEL, D_MODEL), jnp.float32) * s, 'bq': jnp.zeros((D_MODEL,), jnp.float32), 'Wk': jax.random.normal(ks[4], (D_MODEL, D_MODEL), jnp.float32) * s, 'bk': jnp.zeros((D_MODEL,), jnp.float32), 'Wv': jax.random.normal(ks[5], (D_MODEL, D_MODEL), jnp.float32) * s, 'bv': jnp.zeros((D_MODEL,), jnp.float32), 'Wo': jax.random.normal(ks[6], (D_MODEL, D_MODEL), jnp.float32) * s, 'bo': jnp.zeros((D_MODEL,), jnp.float32)}
    _L1_xattn_all = _L1_xattn_setup()
    _L1_xattn_in = {k: v for k, v in _L1_xattn_all.items() if k in ('Wq', 'bq', 'Wk', 'bk', 'Wv', 'bv', 'Wo', 'bo')}
    del _L1_xattn_all

    def _L1_ffn_setup():
        import jax, jax.numpy as jnp
        import numpy as np
        BLOCK = 32
        W_BITS = 4
        ACT_BITS = 16

        def act_qdq(x):
            qmax = 2.0 ** (ACT_BITS - 1) - 1.0
            scale = jnp.maximum(jnp.max(jnp.abs(x)) / qmax, 1e-12)
            return jnp.clip(jnp.round(x / scale), -qmax - 1.0, qmax) * scale

        def fixed_qdq_u16(x):
            scale = 1.0 / 65536.0
            return jnp.clip(jnp.round(x / scale), 0.0, 65535.0) * scale

        def lpbq_dequant(w):
            O, I = w.shape
            qmax = 2.0 ** (W_BITS - 1) - 1.0
            wb = w.reshape(O, I // BLOCK, BLOCK)
            s = jnp.maximum(jnp.max(jnp.abs(wb), axis=-1, keepdims=True) / qmax, 1e-12)
            wq = jnp.clip(jnp.round(wb / s), -qmax - 1.0, qmax) * s
            return wq.reshape(O, I)
        key = jax.random.key(seed)
        k1, k2, k3, k4 = jax.random.split(key, 4)
        B, S, H, I = (2, 1024, 256, 768)
        x = jax.random.normal(k1, (B, S, H), jnp.float32)
        w_gate = jax.random.normal(k2, (I, H), jnp.float32) * 0.02
        w_up = jax.random.normal(k3, (I, H), jnp.float32) * 0.02
        w_down = jax.random.normal(k4, (H, I), jnp.float32) * 0.02
        return {'x': x, 'w_gate': w_gate, 'w_up': w_up, 'w_down': w_down}
    _L1_ffn_all = _L1_ffn_setup()
    _L1_ffn_in = {k: v for k, v in _L1_ffn_all.items() if k in ('w_gate', 'w_up', 'w_down')}
    del _L1_ffn_all
    return {'x': x, 'ctx_1024': ctx_1024, 'g_xattn': g_xattn, 'g_ffn': g_ffn, 'L0_xattn_W_q': _L0_xattn_in['W_q'], 'L0_xattn_W_k': _L0_xattn_in['W_k'], 'L0_xattn_W_v': _L0_xattn_in['W_v'], 'L0_xattn_W_o': _L0_xattn_in['W_o'], 'L0_ffn_scores': _L0_ffn_in['scores'], 'L0_ffn_expert_weights': _L0_ffn_in['expert_weights'], 'L0_ffn_expert_indices': _L0_ffn_in['expert_indices'], 'L0_ffn_w1': _L0_ffn_in['w1'], 'L0_ffn_w2': _L0_ffn_in['w2'], 'L0_ffn_bias': _L0_ffn_in['bias'], 'L1_xattn_Wq': _L1_xattn_in['Wq'], 'L1_xattn_bq': _L1_xattn_in['bq'], 'L1_xattn_Wk': _L1_xattn_in['Wk'], 'L1_xattn_bk': _L1_xattn_in['bk'], 'L1_xattn_Wv': _L1_xattn_in['Wv'], 'L1_xattn_bv': _L1_xattn_in['bv'], 'L1_xattn_Wo': _L1_xattn_in['Wo'], 'L1_xattn_bo': _L1_xattn_in['bo'], 'L1_ffn_w_gate': _L1_ffn_in['w_gate'], 'L1_ffn_w_up': _L1_ffn_in['w_up'], 'L1_ffn_w_down': _L1_ffn_in['w_down']}

def reference(x, ctx_1024, g_xattn, g_ffn, L0_xattn_W_q, L0_xattn_W_k, L0_xattn_W_v, L0_xattn_W_o, L0_ffn_scores, L0_ffn_expert_weights, L0_ffn_expert_indices, L0_ffn_w1, L0_ffn_w2, L0_ffn_bias, L1_xattn_Wq, L1_xattn_bq, L1_xattn_Wk, L1_xattn_bk, L1_xattn_Wv, L1_xattn_bv, L1_xattn_Wo, L1_xattn_bo, L1_ffn_w_gate, L1_ffn_w_up, L1_ffn_w_down):
    import jax
    import jax.numpy as jnp

    def _L0_xattn_ref(query, key, value, W_q, W_k, W_v, W_o):
        import jax, jax.numpy as jnp
        import numpy as np
        D_MODEL = 256
        NUM_HEADS = 16
        D_K = D_MODEL // NUM_HEADS
        B, S, _ = query.shape

        def proj(x, W):
            return (x @ W.T).reshape(B, S, NUM_HEADS, D_K).transpose(0, 2, 1, 3)
        Q = proj(query, W_q)
        K = proj(key, W_k)
        V = proj(value, W_v)
        scores = jnp.einsum('bhqd,bhkd->bhqk', Q, K) / jnp.sqrt(jnp.float32(D_K))
        attn = jax.nn.softmax(scores, axis=-1)
        out = jnp.einsum('bhqk,bhkd->bhqd', attn, V)
        out = out.transpose(0, 2, 1, 3).reshape(B, S, D_MODEL)
        return out @ W_o.T

    def _L0_ffn_ref(x, scores, expert_weights, expert_indices, w1, w2, bias):
        import jax, jax.numpy as jnp
        import numpy as np
        SL, BS, HS, FF, E, TOPK = (512, 2, 256, 1024, 8, 2)
        sl, bs, hs = x.shape
        n_exp = w1.shape[0]
        top_k = expert_indices.shape[-1]
        xf = x.reshape(-1, hs)
        flat_idx = expert_indices.reshape(-1)
        flat_w = expert_weights.reshape(-1)
        order = jnp.argsort(flat_idx)
        tok = order // top_k
        tokens_per_expert = jnp.bincount(flat_idx, length=n_exp).astype(jnp.int32)
        xs = xf[tok]
        h = jax.nn.gelu(jax.lax.ragged_dot(xs, w1, tokens_per_expert), approximate=False)
        ys = jax.lax.ragged_dot(h, w2, tokens_per_expert)
        ys = ys * flat_w[order][:, None]
        out = jnp.zeros_like(xf).at[tok].add(ys)
        return out.reshape(sl, bs, hs) + bias

    def _L1_xattn_ref(Q, K, V, Wq, bq, Wk, bk, Wv, bv, Wo, bo):
        import jax, jax.numpy as jnp
        import numpy as np
        NUM_HEADS = 16
        D_MODEL = 256
        D_K = D_MODEL // NUM_HEADS

        def _split_heads(x):
            B, S, _ = x.shape
            return x.reshape(B, S, NUM_HEADS, D_K).transpose(0, 2, 1, 3)
        q = _split_heads(Q @ Wq + bq)
        k = _split_heads(K @ Wk + bk)
        v = _split_heads(V @ Wv + bv)
        scores = jnp.einsum('bhqd,bhkd->bhqk', q, k) / jnp.sqrt(jnp.asarray(D_K, q.dtype))
        attn = jax.nn.softmax(scores, axis=-1)
        out = jnp.einsum('bhqk,bhkd->bhqd', attn, v)
        B, H, S, Dk = out.shape
        combined = out.transpose(0, 2, 1, 3).reshape(B, S, H * Dk)
        return combined @ Wo + bo

    def _L1_ffn_ref(x, w_gate, w_up, w_down):
        import jax, jax.numpy as jnp
        import numpy as np
        BLOCK = 32
        W_BITS = 4
        ACT_BITS = 16

        def act_qdq(x):
            qmax = 2.0 ** (ACT_BITS - 1) - 1.0
            scale = jnp.maximum(jnp.max(jnp.abs(x)) / qmax, 1e-12)
            return jnp.clip(jnp.round(x / scale), -qmax - 1.0, qmax) * scale

        def fixed_qdq_u16(x):
            scale = 1.0 / 65536.0
            return jnp.clip(jnp.round(x / scale), 0.0, 65535.0) * scale

        def lpbq_dequant(w):
            O, I = w.shape
            qmax = 2.0 ** (W_BITS - 1) - 1.0
            wb = w.reshape(O, I // BLOCK, BLOCK)
            s = jnp.maximum(jnp.max(jnp.abs(wb), axis=-1, keepdims=True) / qmax, 1e-12)
            wq = jnp.clip(jnp.round(wb / s), -qmax - 1.0, qmax) * s
            return wq.reshape(O, I)
        x = act_qdq(x)
        up = act_qdq(x @ lpbq_dequant(w_up).T)
        gate = act_qdq(x @ lpbq_dequant(w_gate).T)
        sig = fixed_qdq_u16(jax.nn.sigmoid(gate))
        gate = act_qdq(gate * sig)
        o = act_qdq(gate * up)
        return o @ lpbq_dequant(w_down).T
    x = x + jnp.tanh(g_xattn[0]) * _L0_xattn_ref(_layernorm(x, axis=-1), ctx_1024, ctx_1024, L0_xattn_W_q, L0_xattn_W_k, L0_xattn_W_v, L0_xattn_W_o)
    x = x + jnp.tanh(g_ffn[0]) * _L0_ffn_ref(_layernorm(x, axis=-1), L0_ffn_scores, L0_ffn_expert_weights, L0_ffn_expert_indices, L0_ffn_w1, L0_ffn_w2, L0_ffn_bias)
    x = x + jnp.tanh(g_xattn[1]) * _L1_xattn_ref(_layernorm(x, axis=-1), ctx_1024, ctx_1024, L1_xattn_Wq, L1_xattn_bq, L1_xattn_Wk, L1_xattn_bk, L1_xattn_Wv, L1_xattn_bv, L1_xattn_Wo, L1_xattn_bo)
    x = x + jnp.tanh(g_ffn[1]) * _L1_ffn_ref(_layernorm(x, axis=-1), L1_ffn_w_gate, L1_ffn_w_up, L1_ffn_w_down)
    return x

_drawn_inputs = setup_inputs


def setup_inputs(seed=0):
    import zlib

    import numpy as np

    out = dict(_drawn_inputs(seed))
    spreads = {'g_ffn': (-1.0, 0.6),
     'L0_ffn_bias': (0.0, 0.1),
     'L1_xattn_bq': (0.0, 0.5),
     'L1_xattn_bk': (0.0, 0.8),
     'L1_xattn_bv': (0.0, 0.1),
     'L1_xattn_bo': (0.0, 0.1)}
    factors = {'L1_ffn_w_gate': 2.723}
    for name, (base, spread) in spreads.items():
        noise = np.random.default_rng([zlib.crc32(name.encode()), seed]).standard_normal(out[name].shape)
        drawn = base * np.exp(spread * noise) if base else spread * noise
        out[name] = jnp.asarray(drawn.astype(out[name].dtype))
    for name, factor in factors.items():
        out[name] = (out[name] * factor).astype(out[name].dtype)
    return out
```

```python
from contextlib import ExitStack

import numpy as np

import concourse.bass as bass
from concourse import mybir

F32 = mybir.dt.float32
BF16 = mybir.dt.bfloat16
I32 = mybir.dt.int32
U32 = mybir.dt.uint32
ALU = mybir.AluOpType
ACT = mybir.ActivationFunctionType
AX = mybir.AxisListType

P = 128
D = 256
KC = D // P
B, S = 4, 512
NT = B * S // P
TB = S // P
H, DK = 16, 16
G = 4
NG = H // G
E = 8
FF = 1024
FC = FF // P
ROUTED = 8
TOPK = 2
SLOT_TILES = ROUTED * TOPK + E - 1
QF = 768
QC = QF // P
BLOCK = 32
EPS = 1e-5
PARTS = 3
ROWS = 6 * DK
Q_RUNS = [(0, 3), (3, 2), (5, 1)]
K_RUNS = [(0, 3), (3, 2), (5, 1)]
MAGIC = 1.5 * 2.0 ** 23
QMAX = 32767.0
TINY = 1e-12
A_MAX, S_X, F_X, S_U, F_U, S_G, F_G, S_2, F_2, S_O, F_O, OUT_F, UNIT, T0, T1 = (0, *range(2, 16))
PIECES = QC * 2
PIECE_ORDER = [2 * c + half for half in range(2) for c in range(QC)]


def build_program(nc, io, out):
    with ExitStack() as ctx:
        def sb(name, shape, dt=F32):
            return ctx.enter_context(nc.sbuf_tensor(name, shape, dt))

        def sem(name):
            return ctx.enter_context(nc.semaphore(name))

        PS = ctx.enter_context(nc.psum_tensor("PS", [P, 8, 512], F32))
        BIG = sb("BIG", [P, 32768])
        KSt = sb("KSt", [P, 4 * G * S], BF16)
        Pt = sb("Pt", [P, 4096])
        X = sb("X", [P, NT, D])
        VS = sb("VS", [P, NG, TB, G, DK + 1])
        OT = sb("OT", [P, 2, S])
        WO = sb("WO", [P, KC, D])
        identf = sb("identf", [P, P])
        identb = sb("identb", [P, P], BF16)
        upper = sb("upper", [P, P])
        ones = sb("ones", [P, P])
        gates = sb("gates", [P, 4])
        tg = sb("tg", [P, 4])
        bias_row = sb("bias_row", [P, D])
        stats = sb("stats", [P, NT, 6])
        mv = sb("mv", [P, NT, 2])
        ve = sb("ve", [P, NT])
        sd = sb("sd", [P, NT])
        nw1 = sb("nw1", [P, NT])
        nw2 = sb("nw2", [P, NT])
        rstd = sb("rstd", [P, NT])
        MX = sb("MX", [P, 2, TB, G])
        MP = sb("MP", [P, TB, PARTS, G], BF16)
        MD = sb("MD", [P, TB, G])
        MR = sb("MR", [PARTS * G, 2, S], BF16)
        rden = sb("rden", [P, TB, G])
        pos_i = sb("pos_i", [P, TOPK, ROUTED], U32)
        ew = sb("ew", [P, ROUTED, TOPK])
        expert_i = sb("expert_i", [1, SLOT_TILES + 1], I32)
        zrow = sb("zrow", [P, D])
        magic = sb("magic", [P, 1])
        idx = sb("idx", [P, ROUTED, TOPK], I32)
        idxf = sb("idxf", [P, ROUTED, TOPK])
        hot = sb("hot", [P, ROUTED, TOPK, E])
        slots = sb("slots", [P, ROUTED, E])
        totals = sb("totals", [P, ROUTED, E])
        before = sb("before", [P, ROUTED, E])
        place = sb("place", [P, ROUTED, E])
        picked = sb("picked", [P, ROUTED, E])
        posf = sb("posf", [P, TOPK, ROUTED])
        rt = [sb(f"rt{i}", [P, E]) for i in range(4)]
        rti = [sb(f"rti{i}", [P, E], I32) for i in range(2)]
        upto = sb("upto", [P, E])
        ex = [sb(f"ex{i}", [1, SLOT_TILES + 1]) for i in range(2)]
        tile_no = sb("tile_no", [P, SLOT_TILES + 1], I32)
        tile_f = sb("tile_f", [P, SLOT_TILES + 1])
        sc = sb("sc", [P, 16])
        cm = sb("cm", [P, 2])
        cmx = sb("cmx", [P, 64])
        one = sb("one", [1, 2])
        ws = sb("ws", [P, 3, QC * D // BLOCK])

        W1 = BIG[:, 0:E * KC * FF]
        W2 = BIG[:, E * KC * FF:2 * E * KC * FF]
        QS = BIG[:, 28672:32768].bitcast(BF16).rearrange("p (g h t) -> p g h t", g=NG, h=G)
        KS = KSt[:, :].rearrange("p (g h t) -> p g h t", g=NG, h=G)
        OALL = BIG[:, 24576:28672].rearrange("p (i n) -> p i n", i=NT)
        at = 4608
        CT = BIG[:, at:at + 4096].rearrange("p (c t) -> p c t", c=KC); at += 4096
        XNT = BIG[:, at:at + 1024].rearrange("p (c t) -> p c t", c=KC); at += 1024
        PT = BIG[:, at:at + 3072].bitcast(BF16).rearrange("p (j r t) -> p j r t", j=4, r=PARTS); at += 3072
        VB = BIG[:, at:at + TB * H * (DK + 1)].rearrange("p (t h d) -> p t h d", t=TB, h=H); at += TB * H * (DK + 1)
        RB = BIG[:, at:at + 1024].rearrange("p (j t) -> p j t", j=2); at += 1024
        AW = BIG[:, at:at + 1536].rearrange("p (c n) -> p c n", c=3 * KC); at += 1536
        BV = BIG[:, at:at + D]; at += D
        BQK = BIG[:, at:at + 4]; at += 4
        TGBO = BIG[:, at:at + D]; at += D
        assert at <= 24576
        XN = Pt[:, :].rearrange("p (i n) -> p i n", i=NT)
        PP = Pt[:, :].rearrange("p (q h t) -> p q h t", q=4, h=2)

        qk_dram = nc.dram_tensor("qk_parts", (2, 2, B, PARTS, D, S), BF16).ap()
        v_dram = nc.dram_tensor("v_rows", (2, B, NG, P, TB, G, DK + 1), F32).ap()
        xs_dram = nc.dram_tensor("slot_rows", ((SLOT_TILES + 1) * P, D), F32).ap()
        ys_dram = nc.dram_tensor("slot_results", ((SLOT_TILES + 1) * P, D), F32).ap()

        x_in = [sem(f"x_in{b}") for b in range(B)]
        gates_in = sem("gates_in")
        aw_in = sem("aw_in")
        wo_in = sem("wo_in")
        ct_in = sem("ct_in")
        consts = sem("consts")
        tg_ready = sem("tg_ready")
        ln_var = sem("ln_var")
        ln_sd = sem("ln_sd")
        xn_ready = sem("xn_ready")
        dve_link = sem("dve_link")
        tr_done = sem("tr_done")
        xnt_evac = sem("xnt_evac")
        qk_done = sem("qk_done")
        hi_done = sem("hi_done")
        r_done = sem("r_done")
        mid_done = sem("mid_done")
        lo_done = sem("lo_done")
        part_out = [sem(f"part_out{j}") for j in range(4)]
        v_done = sem("v_done")
        v_taken = sem("v_taken")
        v_out = sem("v_out")
        q_stack = [sem(f"q_stack{g}") for g in range(NG)]
        v_stack = [sem(f"v_stack{g}") for g in range(NG)]
        max_done = sem("max_done")
        max_taken = sem("max_taken")
        max_link = sem("max_link")
        max_parts = sem("max_parts")
        max_turned = sem("max_turned")
        max_copied = sem("max_copied")
        max_rows = [sem(f"max_rows{g}") for g in range(NG)]
        st_done = sem("st_done")
        exp_done = sem("exp_done")
        pv_done = sem("pv_done")
        ot_ready = sem("ot_ready")
        ot_turned = sem("ot_turned")
        rden_ready = sem("rden_ready")
        o_ready = sem("o_ready")
        pv_zero = sem("pv_zero")
        tro_done = sem("tro_done")
        on_evac = sem("on_evac")
        out_done = sem("out_done")
        x_upd = sem("x_upd")
        biased = sem("biased")
        idx_in = sem("idx_in")
        gp_consts = sem("gp_consts")
        ones_rows = sem("ones_rows")
        tg_bias = sem("tg_bias")
        gate_int = sem("gate_int")
        m_magic = sem("m_magic")
        o_int = sem("o_int")
        onehots = sem("onehots")
        ranks = sem("ranks")
        routed = sem("routed")
        zeroed = sem("zeroed")
        scattered = sem("scattered")
        w_in = sem("w_in")
        xs_in = [sem(f"xs_in{q}") for q in range(2)]
        xs_turned = sem("xs_turned")
        xst_ready = sem("xst_ready")
        h_done = sem("h_done")
        gelu_done = sem("gelu_done")
        ht_turned = sem("ht_turned")
        ht_ready = sem("ht_ready")
        y_done = sem("y_done")
        ys_ready = sem("ys_ready")
        ys_out = [sem(f"ys_out{q}") for q in range(2)]
        gathered = [sem(f"gathered{i}") for i in range(ROUTED)]
        combined = sem("combined")
        qw_in = sem("qw_in")
        qw_ready = sem("qw_ready")
        qwt_turned = sem("qwt_turned")
        qwt_ready = sem("qwt_ready")
        col_max = sem("col_max")
        max_col_turned = sem("max_col_turned")
        max_one = sem("max_one")
        max_spread = sem("max_spread")
        nx_magic = sem("nx_magic")
        nx_ready = sem("nx_ready")
        nx_turned = sem("nx_turned")
        nxt_ready = sem("nxt_ready")
        ug_done = sem("ug_done")
        ug_copied = sem("ug_copied")
        ug_max = sem("ug_max")
        scales = sem("scales")
        q_magic = sem("q_magic")
        q_clip = sem("q_clip")
        sig_done = sem("sig_done")
        prod_done = sem("prod_done")
        dn_done = sem("dn_done")
        y_final = sem("y_final")
        stored = sem("stored")

        block = ctx.enter_context(nc.Block())


        def moe_buffers():
            k32 = KSt[:, :].bitcast(F32)
            return dict(
                xs=k32[:, 0:512].rearrange("p (q n) -> p q n", q=2),
                xst=k32[:, 512:1024].rearrange("p (q n) -> p q n", q=2),
                ys=k32[:, 1024:1536].rearrange("p (q n) -> p q n", q=2),
                h=Pt[:, 0:2048].rearrange("p (q n) -> p q n", q=2),
                ht=Pt[:, 2048:4096].rearrange("p (q c n) -> p q c n", q=2, c=FC),
                got=Pt[:, :].rearrange("p (k i n) -> p k i n", k=TOPK, i=ROUTED),
            )

        def quant_buffers():
            return dict(
                raw=BIG[:, 24576:24576 + 3 * QC * D],
                wt=BIG[:, 0:3 * QC * D],
                up=BIG[:, 4608:16896].rearrange("p (c t) -> p c t", c=QC),
                gate=BIG[:, 16896:29184].rearrange("p (c t) -> p c t", c=QC),
                xt=KSt[:, :].bitcast(F32).rearrange("p (c t) -> p c t", c=KC),
                sig=Pt[:, 0:2048].rearrange("p (q n) -> p q n", q=2),
            )

        M = moe_buffers()
        Q = quant_buffers()

        def bank(i, k=1):
            return PS[:, i:i + k, :].rearrange("p a b -> p (a b)")

        ST = [bank(0, 2), bank(2, 2)]
        SM = [bank(4), bank(5)]
        PV = bank(6)
        MISC = bank(7)

        linked = [0]

        def link(eng, ins):
            linked[0] += 1
            ins.then_inc(dve_link, 1)
            eng.wait_ge(dve_link, linked[0])

        def wait(eng, s, value):
            if not isinstance(value, int) or value > 0:
                eng.wait_ge(s, value)

        def over_batches(eng, layer, body):
            body(B * layer, True, False)
            with eng.Fori(B * layer + 1, B * layer + B - 1) as n:
                body(n, False, False)
            body(B * layer + B - 1, False, True)

        def over_tiles(eng, body):
            with eng.Fori(0, (SLOT_TILES - 3) // 2) as m:
                for q in range(2):
                    body(m, q, None)
            for t in range(SLOT_TILES - 3, SLOT_TILES):
                body(t // 2, t % 2, t)

        assert SLOT_TILES % 2 == 1
        
        def piece(ap, i):
            return ap[:, i // 2, i % 2 * 1024:i % 2 * 1024 + 1024]

        def ug_place(k):
            return Q["gate" if k % 2 else "up"][:, k // 2 % QC, k // (2 * QC) * S:k // (2 * QC) * S + S]

        def clip_count(what, i):
            order = []
            for j in range(PIECES + 1):
                order += [("gate", j), ("up", j)] * (j < PIECES) + [("sig", j - 1)] * (j > 0)
            return 4 + order.index((what, i)) + 1

        NORM_BASE = [0, NT, NT + ROUTED, 2 * NT + ROUTED]

        @block.sync
        def _(sp):
            def load_layer(layer):
                sp.dma_start(AW, io["attn_w"][layer, 0:3].rearrange("w (c p) n -> p (w c) n", p=P)).then_inc(aw_in, 16)
                sp.dma_start(BQK, io["attn_bqk"][layer]).then_inc(aw_in, 16)
                sp.dma_start(BV, io["attn_bvo"][layer, 0].partition_broadcast(P)).then_inc(aw_in, 16)
                sp.dma_start(TGBO, io["attn_bvo"][layer, 1].partition_broadcast(P)).then_inc(aw_in, 16)
                for c in range(KC):
                    sp.dma_start(CT[:, c, :], io["ctx_t"][c * P:(c + 1) * P, :]).then_inc(ct_in, 16)

            def prep(layer):
                for b in range(B):
                    n = B * layer + b
                    for j in range(4):
                        which, c = 1 - j // 2, j % 2
                        if j == 2:
                            sp.wait_ge(v_taken, 2 * (n + 1))
                            for g in range(NG):
                                sp.dma_start(v_dram[layer, b, g], VB[:, :, G * g:G * g + G, :]).then_inc(v_out, 16)
                        sp.wait_ge(lo_done, 4 * n + j + 1)
                        sp.dma_start(qk_dram[layer, which, b, :, c * P:(c + 1) * P, :].rearrange("r p t -> p r t"),
                                     PT[:, j, :, :]).then_inc(part_out[j], 16)

            def load_stack(layer, b, g):
                rows = slice(g * G * DK, (g + 1) * G * DK)
                for first, k, part in ((0, 3, 0), (3, 2, 1), (5, 1, 2)):
                    dst = slice(first * DK, (first + k) * DK)
                    q = qk_dram[layer, 0, b, part, rows, :].rearrange("(d h) t -> d (h t)", h=G)
                    sp.dma_start(QS[dst, g, :, :].rearrange("p h t -> p (h t)"),
                                 q.unsqueeze(0).to_broadcast([k, DK, G * S])).then_inc(q_stack[g], 16)
                    kk = qk_dram[layer, 1, b, 0:k, rows, :].rearrange("r (d h) t -> r d (h t)", h=G)
                    sp.dma_start(KS[dst, g, :, :].rearrange("p h t -> p (h t)"), kk).then_inc(q_stack[g], 16)

            def load_v(layer, b, g):
                sp.dma_start(VS[:, g], v_dram[layer, b, g]).then_inc(v_stack[g], 16)

            def load_max_rows(g):
                sp.dma_start(QS[ROWS:ROWS + PARTS, g, :, :], MR[:, g % 2, :]).then_inc(max_rows[g], 16)

            def attention(layer):
                for j in range(4):
                    sp.wait_ge(part_out[j], 16 * B * (layer + 1))
                sp.wait_ge(v_out, 16 * NG * B * (layer + 1))
                for g in range(NG):
                    load_stack(layer, 0, g)
                    load_v(layer, 0, g)
                sp.wait_ge(max_copied, NG * B * layer + 1)
                load_max_rows(0)

                def batch(n, first, last):
                    for g in range(NG):
                        s = NG * n + g
                        if not (last and g == NG - 1):
                            sp.wait_ge(max_copied, s + 2)
                            load_max_rows((g + 1) % NG)
                        if not last:
                            sp.wait_ge(st_done, 8 * (s + 1))
                            load_stack(layer, n + 1 - B * layer, g)
                            sp.wait_ge(pv_done, 4 * (s + 1))
                            load_v(layer, n + 1 - B * layer, g)
                over_batches(sp, layer, batch)

            sp.dma_start(gates[:, :], io["gates"].partition_broadcast(P)).then_inc(gates_in, 16)
            for b in range(B):
                sp.dma_start(X[:, TB * b:TB * b + TB, :],
                             io["x"][b].rearrange("(i p) n -> p i n", p=P)).then_inc(x_in[b], 16)
            load_layer(0)
            sp.dma_start(WO[:, :, :], io["attn_w"][0, 3].rearrange("(c p) n -> p c n", p=P)).then_inc(wo_in, 16)
            sp.dma_start(ew[:, :, :], io["expert_weights"].rearrange("(i p) k -> p i k", p=P)).then_inc(idx_in, 16)
            sp.dma_start(idx[:, :, :], io["expert_indices"].rearrange("(i p) k -> p i k", p=P)).then_inc(idx_in, 16)
            sp.dma_start(bias_row[:, :], io["moe_bias"].partition_broadcast(P)).then_inc(idx_in, 16)
            prep(0)
            attention(0)

            sp.wait_ge(out_done, NT)
            sp.dma_start(WO[:, :, :], io["attn_w"][1, 3].rearrange("(c p) n -> p c n", p=P)).then_inc(wo_in, 16)

            def load_slots(m, q, t):
                if t is None or t >= 2:
                    sp.wait_ge(xs_turned, 2 * m + q - 1)
                sp.dma_start(M["xs"][:, q, :], slot_tile(xs_dram, m, q)).then_inc(xs_in[q], 16)

            def store_results(m, q):
                sp.wait_ge(ys_ready, 2 * m + q + 1)
                sp.dma_start(slot_tile(ys_dram, m, q), M["ys"][:, q, :]).then_inc(ys_out[q], 16)

            def slot_tile(dram, m, q):
                return dram.rearrange("(m q p) n -> m q p n", q=2, p=P)[m, q]

            sp.wait_ge(scattered, 16 * TOPK * ROUTED)
            load_slots(0, 0, 0)
            load_slots(0, 1, 1)
            with sp.Fori(0, (SLOT_TILES - 3) // 2) as m:
                for q in range(2):
                    load_slots(m + 1, q, None)
                    store_results(m, q)
            t = SLOT_TILES - 1
            load_slots(t // 2, t % 2, t)
            for t in range(SLOT_TILES - 3, SLOT_TILES):
                store_results(t // 2, t % 2)

            sp.wait_ge(y_done, SLOT_TILES)
            load_layer(1)
            prep(1)
            attention(1)

            sp.wait_ge(tro_done, 2 * NT)
            raw = Q["raw"]
            sp.dma_start(raw[:, 0:QC * D].rearrange("p (c n) -> p c n", c=QC),
                         io["w_gate"].rearrange("(c p) n -> p c n", p=P)).then_inc(qw_in, 16)
            sp.dma_start(raw[:, QC * D:2 * QC * D].rearrange("p (c n) -> p c n", c=QC),
                         io["w_up"].rearrange("(c p) n -> p c n", p=P)).then_inc(qw_in, 16)
            sp.dma_start(raw[:, 2 * QC * D:].rearrange("p (c n) -> p c n", c=KC),
                         io["w_down"].rearrange("(c p) n -> p c n", p=P)).then_inc(qw_in, 16)
            for i in range(NT):
                sp.wait_ge(y_final, i + 1)
                sp.dma_start(out[i // TB, (i % TB) * P:(i % TB + 1) * P, :], X[:, i, :]).then_inc(stored, 16)
            sp.wait_ge(stored, 16 * NT)

        @block.gpsimd
        def _(gp):
            gp.memset(identf[:, :], 0.0).then_inc(gp_consts, 1)
            gp.memset(upper[:, :], 1.0).then_inc(gp_consts, 1)
            gp.memset(ones[:, :], 1.0).then_inc(gp_consts, 1)
            gp.memset(zrow[:, :], 0.0).then_inc(gp_consts, 1)
            gp.memset(magic[:, :], MAGIC).then_inc(gp_consts, 1)
            gp.memset(VB[:, :, :, DK:DK + 1], 1.0).then_inc(gp_consts, 1)
            gp.iota(tile_no[:, :], pattern=[[1, SLOT_TILES + 1]], base=0, channel_multiplier=0).then_inc(gp_consts, 1)
            gp.wait_ge(gp_consts, 7)
            gp.affine_select(out=identf[:, :], in_=identf[:, :], compare_op=ALU.not_equal, fill=1.0, base=0,
                             pattern=[[-1, P]], channel_multiplier=1).then_inc(consts, 1)
            gp.affine_select(out=upper[:, :], in_=upper[:, :], compare_op=ALU.is_gt, fill=0.0, base=0,
                             pattern=[[1, P]], channel_multiplier=-1).then_inc(consts, 1)
            gp.wait_ge(consts, 1)
            gp.tensor_copy(identb[:, :], identf[:, :]).then_inc(consts, 1)
            gp.wait_ge(consts, 3)
            gp.memset(KS[ROWS:ROWS + PARTS, :, :, :], 1.0).then_inc(ones_rows, 1)
            gp.wait_ge(ones_rows, 1)

            def prep(layer):
                for n in range(B * layer, B * layer + B):
                    for j in range(4):
                        gp.wait_ge(mid_done, 4 * n + j + 1)
                        gp.tensor_tensor(PT[:, j, 2, :], RB[:, j % 2, :], PT[:, j, 1, :],
                                         ALU.subtract).then_inc(lo_done, 1)

            prep(0)
            gp.dma_start(xs_dram.rearrange("(t p) n -> p t n", p=P),
                         zrow[:, :].unsqueeze(1).to_broadcast([P, SLOT_TILES + 1, D])).then_inc(zeroed, 16)

            def load_w1(e):
                gp.dma_start(W1[:, e * KC * FF:(e + 1) * KC * FF].rearrange("p (c n) -> p c n", c=KC),
                             io["w1"][e].rearrange("(c p) n -> p c n", p=P)).then_inc(w_in, 16)

            def load_w2(e):
                gp.dma_start(W2[:, e * FC * D:(e + 1) * FC * D].rearrange("p (c n) -> p c n", c=FC),
                             io["w2"][e].rearrange("(c p) n -> p c n", p=P)).then_inc(w_in, 16)

            gp.wait_ge(aw_in, 64)
            for j in range(4):
                gp.wait_ge(part_out[j], 16 * B)
            gp.wait_ge(v_out, 16 * NG * B)
            gp.wait_ge(qk_done, 4 * B)
            for e in range(E):
                load_w1(e)
            for e in range(4):
                load_w2(e)
            gp.wait_ge(st_done, 8 * NG * B)
            for e in (6, 7):
                load_w2(e)
            gp.wait_ge(tro_done, NT)
            for e in (4, 5):
                load_w2(e)

            gp.wait_ge(routed, 1)
            gp.wait_ge(zeroed, 16)
            for i in range(ROUTED):
                gp.wait_ge(xn_ready, NORM_BASE[1] + i + 1)
                for k in range(TOPK):
                    gp.indirect_dma_start(out=xs_dram[:, :],
                                          out_offset=bass.IndirectOffsetOnAxis(ap=pos_i[:, k, i:i + 1], axis=0),
                                          in_=XN[:, i, :], in_offset=None).then_inc(scattered, 16)
            gp.wait_ge(tg_bias, 1)
            for i in range(NT):
                if i == 0:
                    gp.wait_ge(x_upd, NT)
                gp.tensor_tensor(X[:, i, :], X[:, i, :], bias_row[:, :], ALU.add).then_inc(biased, 1)
            gp.wait_ge(ys_out[0], 16 * ((SLOT_TILES + 1) // 2))
            gp.wait_ge(ys_out[1], 16 * (SLOT_TILES // 2))
            for i in range(ROUTED):
                for k in range(TOPK):
                    gp.indirect_dma_start(out=M["got"][:, k, i, :], out_offset=None, in_=ys_dram[0:SLOT_TILES * P, :],
                                          in_offset=bass.IndirectOffsetOnAxis(ap=pos_i[:, k, i:i + 1], axis=0),
                                          ).then_inc(gathered[i], 16)

            gp.wait_ge(y_done, SLOT_TILES)
            gp.wait_ge(ys_out[0], 16 * ((SLOT_TILES + 1) // 2))
            gp.memset(VB[:, :, :, DK:DK + 1], 1.0).then_inc(gp_consts, 1)
            gp.wait_ge(gp_consts, 8)
            gp.memset(KS[ROWS:ROWS + PARTS, :, :, :], 1.0).then_inc(ones_rows, 1)
            gp.wait_ge(ones_rows, 2)
            prep(1)
            gp.wait_ge(tg_bias, 2)
            gp.wait_ge(xn_ready, NORM_BASE[3])
            for i in range(NT):
                gp.tensor_tensor(X[:, i, :], X[:, i, :], bias_row[:, :], ALU.add).then_inc(biased, 1)

            def clip(ap, low, high, ready, value):
                gp.wait_ge(ready, value)
                gp.tensor_scalar(ap, ap, MAGIC + high, MAGIC + low, ALU.min, ALU.max).then_inc(q_clip, 1)

            for i in range(4):
                clip(Pt[:, i * 1024:(i + 1) * 1024], -QMAX - 1.0, QMAX, q_magic, i + 1)
            for i in range(PIECES + 1):
                if i < PIECES:
                    clip(piece(Q["gate"], i), -QMAX - 1.0, QMAX, q_magic, 4 + 2 * i + 1)
                    clip(piece(Q["up"], i), -QMAX - 1.0, QMAX, q_magic, 4 + 2 * i + 2)
                if i > 0:
                    clip(Q["sig"][:, (i - 1) % 2, :], 0.0, 65535.0, m_magic, i)
            for i in range(PIECES):
                clip(piece(Q["gate"], i), -QMAX - 1.0, QMAX, q_magic, 4 + 2 * PIECES + i + 1)
            for i in range(PIECES):
                clip(piece(Q["gate"], PIECE_ORDER[i]), -QMAX - 1.0, QMAX, q_magic, 4 + 3 * PIECES + i + 1)

        @block.scalar
        def _(act):
            act.wait_ge(gates_in, 16)
            act.wait_ge(gp_consts, 7)
            act.activation(tg[:, :], gates[:, :], ACT.Tanh).then_inc(tg_ready, 1)

            def norm(k):
                act.wait_ge(ln_var, k + 1)
                act.activation(sd[:, :], ve[:, :], ACT.Sqrt).then_inc(ln_sd, 1)

            def prep(layer):
                act.wait_ge(aw_in, 64 * (layer + 1))
                for n in range(B * layer, B * layer + B):
                    for c in range(KC):
                        act.wait_ge(tr_done, KC * n + c + 1)
                        wait(act, qk_done, 4 * n)
                        act.activation(XNT[:, c, :], bank(c), ACT.Copy).then_inc(xnt_evac, 1)
                    for j in range(4):
                        which, c = 1 - j // 2, j % 2
                        act.wait_ge(qk_done, 4 * n + j + 1)
                        wait(act, part_out[j], 16 * n)
                        act.activation(PT[:, j, 0, :], bank(2 + j), ACT.Identity,
                                       bias=BQK[:, 2 * which + c:2 * which + c + 1]).then_inc(hi_done, 1)

            def copy_out(s, q):
                act.wait_ge(pv_done, 4 * (s + 1))
                wait(act, ot_turned, s - 1)
                act.activation(OT[:, q, :], PV, ACT.Copy).then_inc(ot_ready, 1)

            def copy_max(n, g):
                act.wait_ge(max_turned, NG * n + g + 1)
                wait(act, max_rows[(g + 2) % NG], 16 * (n + g // 2))
                act.activation(MR[:, g % 2, :], MISC[0:PARTS * G, 0:S // 2].bitcast(BF16),
                               ACT.Copy).then_inc(max_copied, 1)

            def attention(layer):
                copy_max(B * layer, 0)

                def batch(n, first, last):
                    for g in range(NG):
                        s = NG * n + g
                        for kc in range(TB):
                            u = 4 * s + kc
                            for half in range(2):
                                act.wait_ge(st_done, 2 * u + half + 1)
                                wait(act, pv_done, u - 1)
                                act.activation(PP[:, 2 * (kc % 2) + half, :, :].rearrange("p h t -> p (h t)"),
                                               ST[half], ACT.Exp, scale=DK ** -0.5).then_inc(exp_done, 1)
                            if kc == 0 and not (first and g == 0):
                                copy_out(s - 1, (g + 1) % 2)
                            if kc == 1 and not (last and g == NG - 1):
                                copy_max(n + (g + 1) // NG, (g + 1) % NG)
                over_batches(act, layer, batch)
                copy_out(NG * B * (layer + 1) - 1, 1)

            def tail(layer):
                for i in range(NT):
                    t = NT * layer + i
                    act.wait_ge(tro_done, t + 1)
                    wait(act, out_done, t - 1)
                    act.activation(OT[:, i % 2, 0:D], bank(i % 2)[:, 0:D], ACT.Copy).then_inc(on_evac, 1)

            norm(0)
            prep(0)
            attention(0)
            tail(0)
            norm(1)

            def expert_tile(m, q, t):
                if t is None or t + 1 < SLOT_TILES:
                    gelu(m, q, 1, t)
                act.wait_ge(y_done, 2 * m + q + 1)
                act.activation(M["ys"][:, q, :], bank(4 + q)[:, 0:D], ACT.Copy).then_inc(ys_ready, 1)

            def gelu(m, q, ahead, t):
                nq = (q + ahead) % 2
                for half in range(2):
                    act.wait_ge(h_done, 2 * (2 * m + q + ahead) + half + 1)
                    act.activation(M["h"][:, nq, half * 512:half * 512 + 512], bank(half),
                                   ACT.Gelu).then_inc(gelu_done, 1)

            gelu(0, 0, 0, 0)
            expert_tile(0, 0, 0)
            expert_tile(0, 1, 1)
            with act.Fori(1, (SLOT_TILES - 3) // 2) as m:
                for q in range(2):
                    act.wait_ge(ys_out[q], 16 * m)
                    expert_tile(m, q, None)
            for t in range(SLOT_TILES - 3, SLOT_TILES):
                act.wait_ge(ys_out[t % 2], 16 * (t // 2))
                expert_tile(t // 2, t % 2, t)

            norm(2)
            prep(1)
            attention(1)
            tail(1)
            norm(3)

            act.wait_ge(scales, 1)
            for i in range(4):
                ap = Pt[:, i * 1024:(i + 1) * 1024]
                act.activation(ap, ap, ACT.Identity, scale=sc[:, F_X:F_X + 1], bias=magic[:, :]).then_inc(q_magic, 1)
            for i in range(NT // 4):
                for c in range(KC):
                    act.wait_ge(nx_turned, 2 * i + c + 1)
                    act.activation(Q["xt"][:, c, i * 512:i * 512 + 512], bank(6 + c), ACT.Copy).then_inc(nxt_ready, 1)
            for k in range(2 * QC * B):
                act.wait_ge(ug_done, k + 1)
                act.activation(ug_place(k), bank(k % 4), ACT.Copy).then_inc(ug_copied, 1)
            act.wait_ge(scales, 2)
            for i in range(PIECES + 1):
                if i < PIECES:
                    for which, f in (("gate", F_G), ("up", F_U)):
                        ap = piece(Q[which], i)
                        act.activation(ap, ap, ACT.Identity, scale=sc[:, f:f + 1], bias=magic[:, :]).then_inc(q_magic, 1)
                if i > 0:
                    j = i - 1
                    act.wait_ge(gate_int, j + 1)
                    wait(act, prod_done, j - 1)
                    act.activation(Q["sig"][:, j % 2, :], piece(Q["gate"], j), ACT.Sigmoid,
                                   scale=sc[:, S_G:S_G + 1]).then_inc(sig_done, 1)
            for r, f in ((0, F_2), (1, F_O)):
                act.wait_ge(scales, 3 + r)
                for i in range(PIECES):
                    ap = piece(Q["gate"], PIECE_ORDER[i] if r else i)
                    act.activation(ap, ap, ACT.Identity, scale=sc[:, f:f + 1], bias=magic[:, :]).then_inc(q_magic, 1)

        @block.vector
        def _(dve):
            def routing():
                dve.wait_ge(idx_in, 48)
                dve.wait_ge(gp_consts, 7)
                dve.tensor_copy(tile_f[:, :], tile_no[:, :])
                link(dve, dve.tensor_copy(idxf[:, :, :], idx[:, :, :]))
                for e in range(E):
                    last = dve.tensor_scalar(hot[:, :, :, e], idxf[:, :, :], float(e), None, ALU.is_equal)
                link(dve, last)
                dve.tensor_tensor(slots[:, :, :], hot[:, :, 0, :], hot[:, :, 1, :], ALU.add).then_inc(onehots, 1)
                dve.wait_ge(ranks, 1)
                dve.memset(before[:, 0, :], 0.0)
                link(dve, dve.tensor_copy(totals[:, :, :].rearrange("p i e -> p (i e)"), bank(1)[:, 0:ROUTED * E]))
                for i in range(1, ROUTED):
                    link(dve, dve.tensor_tensor(before[:, i, :], before[:, i - 1, :], totals[:, i - 1, :], ALU.add))
                link(dve, dve.tensor_tensor(rt[0][:, :], before[:, ROUTED - 1, :], totals[:, ROUTED - 1, :], ALU.add))
                link(dve, dve.tensor_scalar(rti[0][:, :], rt[0][:, :], float(P - 1), None, ALU.add))
                link(dve, dve.tensor_scalar(rti[1][:, :], rti[0][:, :], 7, None, ALU.arith_shift_right))
                link(dve, dve.tensor_copy(rt[1][:, :], rti[1][:, :]))
                link(dve, dve.tensor_copy(upto[:, 0:1], rt[1][:, 0:1]))
                for e in range(1, E):
                    link(dve, dve.tensor_tensor(upto[:, e:e + 1], upto[:, e - 1:e], rt[1][:, e:e + 1], ALU.add))
                link(dve, dve.tensor_tensor(rt[2][:, :], upto[:, :], rt[1][:, :], ALU.subtract))
                link(dve, dve.tensor_scalar(rt[3][:, :], rt[2][:, :], float(P), None, ALU.mult))
                link(dve, dve.tensor_tensor(place[:, :, :].rearrange("p i e -> p (i e)"), bank(0)[:, 0:ROUTED * E],
                                            before[:, :, :].rearrange("p i e -> p (i e)"), ALU.add))
                link(dve, dve.tensor_tensor(place[:, :, :], place[:, :, :],
                                            rt[3][:, :].unsqueeze(1).to_broadcast([P, ROUTED, E]), ALU.add))
                for k in range(TOPK):
                    link(dve, dve.tensor_tensor(picked[:, :, :], place[:, :, :], hot[:, :, k, :], ALU.mult))
                    link(dve, dve.tensor_reduce(posf[:, k, :], picked[:, :, :], AX.X, ALU.add))
                    if k == 0:
                        link(dve, dve.tensor_tensor(place[:, :, :], place[:, :, :], hot[:, :, 0, :], ALU.add))
                dve.tensor_copy(pos_i[:, :, :], posf[:, :, :])
                link(dve, dve.memset(ex[0][:, :], 0.0))
                for e in range(E):
                    link(dve, dve.scalar_tensor_tensor(ex[(e + 1) % 2][:, :], tile_f[0:1, :], upto[0:1, e:e + 1],
                                                       ex[e % 2][:, :], ALU.is_ge, ALU.add))
                link(dve, dve.tensor_scalar(ex[1][:, :], ex[0][:, :], float(E - 1), None, ALU.min))
                dve.tensor_copy(expert_i[:, :], ex[1][:, :]).then_inc(routed, 1)

            def norm(k, tiles):
                for i in range(tiles):
                    if k == 0 and i % TB == 0:
                        dve.wait_ge(x_in[i // TB], 16)
                    last = dve.bn_stats(stats[:, i, :], X[:, i, :])
                link(dve, last)
                for i in range(tiles):
                    last = dve.bn_aggr(mv[:, i, :], stats[:, i, :])
                link(dve, last)
                dve.tensor_scalar(ve[:, :], mv[:, :, 1], EPS, None, ALU.add).then_inc(ln_var, 1)
                dve.wait_ge(ln_sd, k + 1)
                link(dve, dve.reciprocal(nw1[:, :], sd[:, :]))
                link(dve, dve.tensor_tensor(nw2[:, :], ve[:, :], nw1[:, :], ALU.mult))
                link(dve, dve.tensor_tensor(nw1[:, :], nw2[:, :], sd[:, :], ALU.add))
                link(dve, dve.tensor_scalar(nw2[:, :], nw1[:, :], 0.5, None, ALU.mult))
                link(dve, dve.reciprocal(rstd[:, :], nw2[:, :]))
                for i in range(tiles):
                    dve.tensor_scalar(XN[:, i, :], X[:, i, :], mv[:, i, 0:1], rstd[:, i:i + 1],
                                      ALU.subtract, ALU.mult).then_inc(xn_ready, 1)

            def prep(layer):
                dve.wait_ge(aw_in, 64 * (layer + 1))
                dve.wait_ge(gp_consts, 7 + layer)
                for n in range(B * layer, B * layer + B):
                    for j in range(4):
                        which, c = 1 - j // 2, j % 2
                        if j == 2:
                            for t2 in range(2):
                                dve.wait_ge(v_done, 2 * n + t2 + 1)
                                wait(dve, v_out, 16 * NG * n)
                                for t in range(2):
                                    last = dve.tensor_tensor(
                                        VB[:, 2 * t2 + t, :, 0:DK],
                                        bank(6 + t2)[:, t * D:t * D + D].rearrange("p (h d) -> p h d", h=H),
                                        BV.rearrange("p (h d) -> p h d", h=H), ALU.add)
                                last.then_inc(v_taken, 1)
                        dve.wait_ge(hi_done, 4 * n + j + 1)
                        wait(dve, lo_done, 4 * n + j - 1)
                        dve.scalar_tensor_tensor(RB[:, j % 2, :], bank(2 + j),
                                                 BQK[:, 2 * which + c:2 * which + c + 1], PT[:, j, 0, :],
                                                 ALU.add, ALU.subtract).then_inc(r_done, 1)
                        dve.wait_ge(r_done, 4 * n + j + 1)
                        dve.tensor_copy(PT[:, j, 1, :], RB[:, j % 2, :]).then_inc(mid_done, 1)

            def split_max(n, g):
                s, q = NG * n + g, g % 2
                dve.wait_ge(max_taken, 16 * (s + 1))
                wait(dve, max_turned, s)
                dve.tensor_copy(MP[:, :, 0, :], MX[:, q, :, :]).then_inc(max_link, 1)
                dve.wait_ge(max_link, 3 * s + 1)
                dve.tensor_tensor(MD[:, :, :], MX[:, q, :, :], MP[:, :, 0, :], ALU.subtract).then_inc(max_link, 1)
                dve.wait_ge(max_link, 3 * s + 2)
                dve.tensor_copy(MP[:, :, 1, :], MD[:, :, :]).then_inc(max_link, 1)
                dve.wait_ge(max_link, 3 * s + 3)
                dve.tensor_tensor(MP[:, :, 2, :], MD[:, :, :], MP[:, :, 1, :], ALU.subtract).then_inc(max_parts, 1)

            def maxima(n, g, some):
                for i in some:
                    dve.wait_ge(max_done, 16 * (NG * n + g) + i + 1)
                    dve.tensor_reduce(MX[:, g % 2, i % TB, i // TB:i // TB + 1], SM[i % 2], AX.X, ALU.max,
                                      negate=True).then_inc(max_taken, 1)

            def normalise(s, n, g):
                dve.wait_ge(ot_turned, s + 1)
                o = MISC.rearrange("p (t h d) -> p t h d", t=TB, h=G)
                dve.reciprocal(rden[:, :, :], o[:, :, :, DK]).then_inc(rden_ready, 1)
                dve.wait_ge(rden_ready, s + 1)
                to = BIG[:, bass.ds(24576 + n * (TB * D), TB * D)].rearrange("p (t n) -> p t n", t=TB)
                dve.tensor_tensor(to[:, :, g * G * DK:(g + 1) * G * DK].rearrange("p t (h d) -> p t h d", h=G),
                                  o[:, :, :, 0:DK], rden[:, :, :].unsqueeze(3).to_broadcast([P, TB, G, DK]),
                                  ALU.mult).then_inc(o_ready, 1)

            def attention(layer):
                dve.memset(PV, 0.0).then_inc(pv_zero, 1)
                n0 = B * layer
                for g in range(2):
                    maxima(n0, g, range(16))
                split_max(n0, 0)

                def batch(n, first, last):
                    for g in range(NG):
                        if not (last and g == NG - 1):
                            split_max(n + (g + 1) // NG, (g + 1) % NG)
                        ahead = not (last and g >= 2)
                        if ahead:
                            maxima(n + (g + 2) // NG, (g + 2) % NG, range(12))
                        if not (first and g == 0):
                            m = n if g else n - 1
                            normalise(NG * n + g - 1, m - n0, (g + 3) % NG)
                        if ahead:
                            maxima(n + (g + 2) // NG, (g + 2) % NG, range(12, 16))
                over_batches(dve, layer, batch)
                normalise(NG * (n0 + B) - 1, B - 1, NG - 1)

            def tail(layer):
                for i in range(NT):
                    t = NT * layer + i
                    dve.wait_ge(out_done, t + 1)
                    if layer:
                        dve.wait_ge(biased, NT + i + 1)
                    dve.scalar_tensor_tensor(X[:, i, :], bank(2 + i % 2)[:, 0:D], tg[:, layer:layer + 1], X[:, i, :],
                                             ALU.mult, ALU.add).then_inc(x_upd, 1)

            routing()
            norm(0, NT)
            prep(0)
            attention(0)
            tail(0)
            dve.wait_ge(x_upd, NT)
            norm(1, ROUTED)
            dve.wait_ge(tg_ready, 1)
            dve.tensor_scalar(bias_row[:, :], bias_row[:, :], tg[:, 2:3], None, ALU.mult).then_inc(tg_bias, 1)

            def turned(m, q):
                for half in range(2):
                    dve.wait_ge(ht_turned, 2 * (2 * m + q) + half + 1)
                    dve.tensor_copy(M["ht"][:, q, 4 * half:4 * half + 4, :].rearrange("p c n -> p (c n)"),
                                    bank(2 + half)).then_inc(ht_ready, 1)

            def slots_turned(m, q, ahead):
                dve.wait_ge(xs_turned, 2 * m + q + ahead + 1)
                dve.tensor_copy(M["xst"][:, (q + ahead) % 2, :],
                                bank(6 + (q + ahead) % 2)[:, 0:D]).then_inc(xst_ready, 1)

            slots_turned(0, 0, 0)
            slots_turned(0, 1, 0)

            def expert_tile(m, q, t):
                turned(m, q)
                if t is None or t + 2 < SLOT_TILES:
                    slots_turned(m, q, 2)
            over_tiles(dve, expert_tile)

            for i in range(ROUTED):
                dve.wait_ge(gathered[i], 16 * TOPK)
                dve.wait_ge(biased, NT)
                y0, y1 = M["got"][:, 0, i, :], M["got"][:, 1, i, :]
                link(dve, dve.tensor_scalar(y0, y0, ew[:, i, 0:1], None, ALU.mult))
                link(dve, dve.scalar_tensor_tensor(y0, y1, ew[:, i, 1:2], y0, ALU.mult, ALU.add))
                dve.scalar_tensor_tensor(X[:, i, :], y0, tg[:, 2:3], X[:, i, :],
                                         ALU.mult, ALU.add).then_inc(combined, 1)
            dve.wait_ge(combined, ROUTED)
            norm(2, NT)
            dve.wait_ge(aw_in, 64 * 2)
            dve.tensor_scalar(bias_row[:, :], TGBO, tg[:, 1:2], None, ALU.mult).then_inc(tg_bias, 1)
            prep(1)
            attention(1)
            tail(1)
            dve.wait_ge(x_upd, 2 * NT)
            norm(3, NT)

            def spread_max(r, count):
                dve.wait_ge(max_col_turned, r + 1)
                dve.tensor_reduce(one[0:1, 0:count], bank(5)[0:1, 0:count * P].rearrange("p (k n) -> p k n", k=count),
                                  AX.X, ALU.max).then_inc(max_one, 1)
                dve.wait_ge(max_spread, r + 1)
                link(dve, dve.tensor_copy(sc[:, A_MAX:A_MAX + count], bank(4)[:, 0:count]))

            def dequantise(first, chunks, blocks, k):
                w = Q["raw"][:, first:first + chunks * blocks * BLOCK]
                wb = w.rearrange("p (b n) -> p b n", n=BLOCK)
                nb = chunks * blocks
                link(dve, dve.tensor_reduce(ws[:, 0, 0:nb], wb, AX.X, ALU.max, apply_absolute_value=True))
                link(dve, dve.tensor_scalar(ws[:, 1, 0:nb], ws[:, 0, 0:nb], 1.0 / 7.0, TINY, ALU.mult, ALU.max))
                link(dve, dve.reciprocal(ws[:, 2, 0:nb], ws[:, 1, 0:nb]))
                link(dve, dve.tensor_tensor(wb, wb, ws[:, 2, 0:nb].unsqueeze(2).to_broadcast([P, nb, BLOCK]), ALU.mult))
                link(dve, dve.tensor_scalar(w, w, MAGIC, MAGIC, ALU.add, ALU.subtract))
                link(dve, dve.tensor_scalar(w, w, -8.0, 7.0, ALU.max, ALU.min))
                dve.tensor_tensor(wb, wb, ws[:, 1, 0:nb].unsqueeze(2).to_broadcast([P, nb, BLOCK]),
                                  ALU.mult).then_inc(qw_ready, 1)

            dve.wait_ge(qw_in, 48)
            for k in range(3):
                dequantise(k * QC * D, *((QC, D // BLOCK) if k < 2 else (KC, QF // BLOCK)), k)
            for k in range(3):
                for half in range(3):
                    dve.wait_ge(qwt_turned, 3 * k + half + 1)
                    dve.tensor_copy(Q["wt"][:, k * QC * D + half * 512:k * QC * D + half * 512 + 512],
                                    bank(half)).then_inc(qwt_ready, 1)

            dve.wait_ge(xn_ready, NORM_BASE[3] + NT)
            for i in range(4):
                last = dve.tensor_reduce(cmx[:, i:i + 1], Pt[:, i * 1024:(i + 1) * 1024], AX.X, ALU.max,
                                         apply_absolute_value=True)
            link(dve, last)
            dve.tensor_reduce(cm[:, 0:1], cmx[:, 0:4], AX.X, ALU.max).then_inc(col_max, 1)
            spread_max(0, 1)
            link(dve, dve.tensor_scalar(sc[:, S_X:S_X + 1], sc[:, A_MAX:A_MAX + 1], 1.0 / QMAX, TINY, ALU.mult, ALU.max))
            dve.reciprocal(sc[:, F_X:F_X + 1], sc[:, S_X:S_X + 1]).then_inc(scales, 1)
            for i in range(4):
                dve.wait_ge(q_clip, i + 1)
                ap = Pt[:, i * 1024:(i + 1) * 1024]
                dve.tensor_scalar(ap, ap, MAGIC, None, ALU.subtract).then_inc(nx_ready, 1)

            for k in range(2 * QC * B):
                dve.wait_ge(ug_copied, k + 1)
                last = dve.tensor_reduce(cmx[:, (k % 2) * 32 + k // 2:(k % 2) * 32 + k // 2 + 1], ug_place(k), AX.X,
                                         ALU.max, apply_absolute_value=True)
            link(dve, last)
            dve.tensor_reduce(cm[:, 0:2], cmx[:, :].rearrange("p (w k) -> p w k", w=2)[:, :, 0:QC * B], AX.X,
                              ALU.max).then_inc(col_max, 1)
            spread_max(1, 2)
            for w, (s_, f_) in enumerate(((S_U, F_U), (S_G, F_G))):
                link(dve, dve.tensor_tensor(sc[:, T0:T0 + 1], sc[:, A_MAX + w:A_MAX + w + 1], sc[:, S_X:S_X + 1], ALU.mult))
                link(dve, dve.tensor_scalar(sc[:, s_:s_ + 1], sc[:, T0:T0 + 1], 1.0 / QMAX, TINY, ALU.mult, ALU.max))
                link(dve, dve.reciprocal(sc[:, T1:T1 + 1], sc[:, s_:s_ + 1]))
                last = dve.tensor_tensor(sc[:, f_:f_ + 1], sc[:, T1:T1 + 1], sc[:, S_X:S_X + 1], ALU.mult)
                if w == 0:
                    link(dve, last)
            last.then_inc(scales, 1)

            for i in range(PIECES + 2):
                if i < PIECES:
                    ap = piece(Q["gate"], i)
                    dve.wait_ge(q_clip, clip_count("gate", i))
                    dve.tensor_scalar(ap, ap, MAGIC, None, ALU.subtract).then_inc(gate_int, 1)
                if 0 < i <= PIECES:
                    dve.wait_ge(sig_done, i)
                    sg = Q["sig"][:, (i - 1) % 2, :]
                    dve.tensor_scalar(sg, sg, 65536.0, MAGIC, ALU.mult, ALU.add).then_inc(m_magic, 1)
                if i > 1:
                    j = i - 2
                    dve.wait_ge(q_clip, clip_count("sig", j))
                    ap = piece(Q["gate"], j)
                    dve.scalar_tensor_tensor(ap, Q["sig"][:, j % 2, :], MAGIC, ap, ALU.subtract,
                                             ALU.mult).then_inc(prod_done, 1)
                    dve.wait_ge(prod_done, j + 1)
                    last = dve.tensor_reduce(cmx[:, j:j + 1], ap, AX.X, ALU.max, apply_absolute_value=True)
            link(dve, last)
            dve.tensor_reduce(cm[:, 0:1], cmx[:, 0:PIECES], AX.X, ALU.max).then_inc(col_max, 1)
            spread_max(2, 1)

            def next_scale(unit, s_, f_, r):
                link(dve, dve.tensor_tensor(sc[:, T0:T0 + 1], sc[:, A_MAX:A_MAX + 1], unit, ALU.mult))
                link(dve, dve.tensor_scalar(sc[:, s_:s_ + 1], sc[:, T0:T0 + 1], 1.0 / QMAX, TINY, ALU.mult, ALU.max))
                link(dve, dve.reciprocal(sc[:, T1:T1 + 1], sc[:, s_:s_ + 1]))
                dve.tensor_tensor(sc[:, f_:f_ + 1], sc[:, T1:T1 + 1], unit, ALU.mult).then_inc(scales, 1)

            link(dve, dve.tensor_scalar(sc[:, UNIT:UNIT + 1], sc[:, S_G:S_G + 1], 1.0 / 65536.0, None, ALU.mult))
            next_scale(sc[:, UNIT:UNIT + 1], S_2, F_2, 3)
            for i in range(PIECES):
                ap = piece(Q["gate"], i)
                dve.wait_ge(q_clip, 4 + 3 * PIECES + i + 1)
                link(dve, dve.tensor_scalar(ap, ap, MAGIC, None, ALU.subtract))
                link(dve, dve.scalar_tensor_tensor(ap, piece(Q["up"], i), MAGIC, ap, ALU.subtract, ALU.mult))
                last = dve.tensor_reduce(cmx[:, i:i + 1], ap, AX.X, ALU.max, apply_absolute_value=True)
            link(dve, last)
            dve.tensor_reduce(cm[:, 0:1], cmx[:, 0:PIECES], AX.X, ALU.max).then_inc(col_max, 1)
            spread_max(3, 1)
            link(dve, dve.tensor_tensor(sc[:, UNIT:UNIT + 1], sc[:, S_2:S_2 + 1], sc[:, S_U:S_U + 1], ALU.mult))
            next_scale(sc[:, UNIT:UNIT + 1], S_O, F_O, 4)
            link(dve, dve.tensor_tensor(sc[:, OUT_F:OUT_F + 1], sc[:, S_O:S_O + 1], tg[:, 3:4], ALU.mult))
            for i in range(PIECES):
                ap = piece(Q["gate"], PIECE_ORDER[i])
                dve.wait_ge(q_clip, 4 + 4 * PIECES + i + 1)
                dve.tensor_scalar(ap, ap, MAGIC, None, ALU.subtract).then_inc(o_int, 1)
            for i in range(NT):
                dve.wait_ge(dn_done, i + 1)
                dve.scalar_tensor_tensor(X[:, i, :], bank(i % 4)[:, 0:D], sc[:, OUT_F:OUT_F + 1], X[:, i, :],
                                         ALU.mult, ALU.add).then_inc(y_final, 1)

        @block.tensor
        def _(pe):
            pe.wait_ge(consts, 3)
            pe.wait_ge(gp_consts, 7)
            pe.wait_ge(onehots, 1)
            pe.matmul(bank(0)[:, 0:ROUTED * E], upper[:, :], slots[:, :, :].rearrange("p i e -> p (i e)"),
                      start=True, stop=True)
            pe.matmul(bank(1)[:, 0:ROUTED * E], ones[:, :], slots[:, :, :].rearrange("p i e -> p (i e)"),
                      start=True, stop=True).then_inc(ranks, 1)
            pe.wait_ge(routed, 1)

            def prep(layer):
                pe.wait_ge(aw_in, 64 * (layer + 1))
                pe.wait_ge(ct_in, 16 * KC * (layer + 1))
                for b in range(B):
                    n = B * layer + b
                    pe.wait_ge(xn_ready, NORM_BASE[2 * layer] + TB * (b + 1))
                    wait(pe, xnt_evac, KC * n)
                    for c in range(KC):
                        for t in range(TB):
                            last = pe.transpose(bank(c)[:, t * P:(t + 1) * P], XN[:, TB * b + t, c * P:(c + 1) * P],
                                                identf[:, :])
                        last.then_inc(tr_done, 1)
                    for j in range(4):
                        which, c = 1 - j // 2, j % 2
                        if j == 2:
                            for t in range(TB):
                                wait(pe, v_taken, 2 * (n - 1) + t // 2 + 1 if n > 0 else 0)
                                for kc in range(KC):
                                    last = pe.matmul(bank(6 + t // 2)[:, (t % 2) * D:(t % 2) * D + D],
                                                     CT[:, kc, (TB * b + t) * P:(TB * b + t + 1) * P],
                                                     AW[:, 2 * KC + kc, :], start=(kc == 0), stop=(kc == KC - 1))
                                if t % 2:
                                    last.then_inc(v_done, 1)
                            pe.wait_ge(xnt_evac, KC * (n + 1))
                        wait(pe, r_done, 4 * (n - 1) + j + 1 if n > 0 else 0)
                        for kc in range(KC):
                            rhs = CT[:, kc, b * S:(b + 1) * S] if which else XNT[:, kc, :]
                            last = pe.matmul(bank(2 + j), AW[:, which * KC + kc, c * P:(c + 1) * P], rhs,
                                             start=(kc == 0), stop=(kc == KC - 1))
                        last.then_inc(qk_done, 1)

            def max_scores(n, g, some):
                for i in some:
                    h, qc = i // TB, i % TB
                    if i == 0:
                        pe.wait_ge(q_stack[g], 96 * (n + 1))
                    wait(pe, max_taken, 16 * (NG * n + g) + i - 1)
                    pe.matmul(SM[i % 2], QS[0:ROWS, g, h, qc * P:(qc + 1) * P], KS[0:ROWS, g, h, :],
                              start=True, stop=True).then_inc(max_done, 1)

            def turn_max(n, g):
                s = NG * n + g
                pe.wait_ge(max_parts, s + 1)
                wait(pe, o_ready, s - 2)
                for t in range(TB):
                    last = pe.transpose(MISC[0:PARTS * G, t * P // 2:(t + 1) * P // 2].bitcast(BF16),
                                        MP[:, t, :, :].rearrange("p r h -> p (r h)"), identb[:, :])
                last.then_inc(max_turned, 1)

            def key_scores(s, n, g, kc):
                u = 4 * s + kc
                if kc == 0:
                    pe.wait_ge(max_rows[g], 16 * (n + 1))
                for half in range(2):
                    wait(pe, exp_done, 2 * u + half - 1)
                    for i in range(2):
                        h = 2 * half + i
                        last = pe.matmul(ST[half][:, i * S:(i + 1) * S], KS[0:ROWS + PARTS, g, h, kc * P:(kc + 1) * P],
                                         QS[0:ROWS + PARTS, g, h, :], start=True, stop=True)
                    last.then_inc(st_done, 1)

            def values(s, n, g, kc):
                pe.wait_ge(exp_done, 2 * (4 * s + kc + 1))
                if kc == 0:
                    pe.wait_ge(v_stack[g], 16 * (n + 1))
                    wait(pe, ot_ready, s)
                for h in range(G):
                    last = pe.matmul(PV[32 * h:32 * h + DK + 1, :], VS[:, g, kc, h, :],
                                     PP[:, 2 * (kc % 2) + h // 2, h % 2, :], start=(kc == 0), stop=(kc == TB - 1),
                                     tile_position=(0, 32 * h))
                last.then_inc(pv_done, 1)

            def turn_outputs(s, q, max_too):
                pe.wait_ge(ot_ready, s + 1)
                if max_too:
                    pe.wait_ge(max_copied, s + 3)
                else:
                    pe.wait_ge(o_ready, s)
                for t in range(TB):
                    last = pe.transpose(MISC[:, t * P:(t + 1) * P], OT[:, q, t * P:(t + 1) * P], identf[:, :])
                last.then_inc(ot_turned, 1)

            def attention(layer):
                n0 = B * layer
                pe.wait_ge(ones_rows, layer + 1)
                pe.wait_ge(pv_zero, layer + 1)
                pe.wait_ge(r_done, 4 * B * (layer + 1))
                pe.wait_ge(v_taken, 2 * B * (layer + 1))
                for g in range(2):
                    max_scores(n0, g, range(16))
                turn_max(n0, 0)

                def batch(n, first, last):
                    for g in range(NG):
                        s = NG * n + g
                        for kc in range(TB):
                            key_scores(s, n, g, kc)
                            if not (last and g >= 2):
                                max_scores(n + (g + 2) // NG, (g + 2) % NG, range(4 * kc, 4 * kc + 4))
                            if kc > 0:
                                values(s, n, g, kc - 1)
                            elif g > 0:
                                values(s - 1, n, g - 1, TB - 1)
                            elif not first:
                                values(s - 1, n - 1, NG - 1, TB - 1)
                            if kc == 1 and not (last and g == NG - 1):
                                turn_max(n + (g + 1) // NG, (g + 1) % NG)
                            if kc == 2 and not (first and g == 0):
                                turn_outputs(s - 1, (g + 1) % 2, not (last and g == NG - 1))
                over_batches(pe, layer, batch)
                n = n0 + B - 1
                s = NG * n + NG - 1
                values(s, n, NG - 1, TB - 1)
                turn_outputs(s, 1, False)

            def tail(layer):
                pe.wait_ge(wo_in, 16 * (layer + 1))
                pe.wait_ge(o_ready, NG * B * (layer + 1))
                pe.wait_ge(exp_done, 8 * NG * B * (layer + 1))
                for i in range(NT + 1):
                    t = NT * layer + i
                    if i < NT:
                        if i >= 2:
                            pe.wait_ge(on_evac, t - 1)
                        for c in range(KC):
                            last = pe.transpose(bank(i % 2)[:, c * P:(c + 1) * P], OALL[:, i, c * P:(c + 1) * P],
                                                identf[:, :])
                        last.then_inc(tro_done, 1)
                    if i > 0:
                        j = i - 1
                        pe.wait_ge(on_evac, t)
                        if j >= 2:
                            pe.wait_ge(x_upd, t - 2)
                        for c in range(KC):
                            last = pe.matmul(bank(2 + j % 2)[:, 0:D], OT[:, j % 2, c * P:(c + 1) * P], WO[:, c, :],
                                             start=(c == 0), stop=(c == KC - 1))
                        last.then_inc(out_done, 1)

            prep(0)
            attention(0)
            tail(0)

            def turn_slots(m, q, ahead):
                p = (q + ahead) % 2
                pe.wait_ge(xs_in[p], 16 * (m + (q + ahead) // 2 + 1))
                wait(pe, xst_ready, 2 * m + q + ahead - 1)
                for c in range(KC):
                    last = pe.transpose(bank(6 + p)[:, c * P:(c + 1) * P], M["xs"][:, p, c * P:(c + 1) * P], identf[:, :])
                last.then_inc(xs_turned, 1)

            def expert_of(m, q, ahead):
                t = 2 * m + q + ahead
                return pe.value_load(expert_i[0:1, bass.ds(t, 1)], min_val=0, max_val=E - 1)

            def hidden(m, q, ahead, e):
                t = 2 * m + q + ahead
                p = (q + ahead) % 2
                pe.wait_ge(xst_ready, t + 1)
                for half in range(2):
                    wait(pe, gelu_done, 2 * t + half - 1)
                    for c in range(KC):
                        last = pe.matmul(bank(half), M["xst"][:, p, c * P:(c + 1) * P],
                                         W1[:, bass.ds(e * (KC * FF) + (c * FF + half * 512), 512)],
                                         start=(c == 0), stop=(c == KC - 1))
                    last.then_inc(h_done, 1)

            def expert_tile(m, q, t):
                n = 2 * m + q
                for half in range(2):
                    pe.wait_ge(gelu_done, 2 * n + half + 1)
                    wait(pe, ht_ready, 2 * n + half - 1)
                    for c in range(4 * half, 4 * half + 4):
                        last = pe.transpose(bank(2 + half)[:, (c % 4) * P:(c % 4 + 1) * P],
                                            M["h"][:, q, c * P:(c + 1) * P], identf[:, :])
                    last.then_inc(ht_turned, 1)
                if t is None or t + 1 < SLOT_TILES:
                    hidden(m, q, 1, expert_of(m, q, 1))
                if t is None or t + 2 < SLOT_TILES:
                    turn_slots(m, q, 2)
                e = expert_of(m, q, 0)
                pe.wait_ge(ht_ready, 2 * n + 2)
                wait(pe, ys_ready, n - 1)
                for c in range(FC):
                    last = pe.matmul(bank(4 + q)[:, 0:D], M["ht"][:, q, c, :],
                                     W2[:, bass.ds(e * (FC * D) + c * D, D)], start=(c == 0), stop=(c == FC - 1))
                last.then_inc(y_done, 1)

            pe.wait_ge(x_upd, NT)
            pe.wait_ge(w_in, 16 * 2 * E)
            turn_slots(0, 0, 0)
            turn_slots(0, 1, 0)
            hidden(0, 0, 0, expert_of(0, 0, 0))
            expert_tile(0, 0, 0)
            expert_tile(0, 1, 1)
            with pe.Fori(1, (SLOT_TILES - 3) // 2) as m:
                for q in range(2):
                    expert_tile(m, q, None)
            for t in range(SLOT_TILES - 3, SLOT_TILES):
                expert_tile(t // 2, t % 2, t)

            pe.wait_ge(ys_ready, SLOT_TILES)
            prep(1)
            attention(1)
            tail(1)
            pe.wait_ge(x_upd, 2 * NT)

            for k in range(3):
                pe.wait_ge(qw_ready, k + 1)
                chunks, turned_chunks = (QC, KC) if k < 2 else (KC, QC)
                w = Q["raw"][:, k * QC * D:(k + 1) * QC * D].rearrange("p (c n) -> p c n", c=chunks)
                for a in range(12):
                    ci, co = a // chunks, a % chunks
                    if a % 4 == 0:
                        wait(pe, qwt_ready, 3 * k + a // 4 - 2)
                    last = pe.transpose(bank(a // 4)[:, (a % 4) * P:(a % 4 + 1) * P], w[:, co, ci * P:(ci + 1) * P],
                                        identf[:, :])
                    if a % 4 == 3:
                        last.then_inc(qwt_turned, 1)

            def spread_max(r, count):
                pe.wait_ge(col_max, r + 1)
                for k in range(count):
                    last = pe.transpose(bank(5)[0:1, k * P:(k + 1) * P], cm[:, k:k + 1], identf[:, :])
                last.then_inc(max_col_turned, 1)
                pe.wait_ge(max_one, r + 1)
                pe.matmul(bank(4)[:, 0:count], ones[0:1, :], one[0:1, 0:count], start=True, stop=True
                          ).then_inc(max_spread, 1)

            spread_max(0, 1)
            for i in range(NT // 4):
                pe.wait_ge(nx_ready, i + 1)
                for c in range(KC):
                    wait(pe, nxt_ready, 2 * (i - 1) + c + 1 if i else 0)
                    for t in range(4):
                        last = pe.transpose(bank(6 + c)[:, t * P:(t + 1) * P], XN[:, 4 * i + t, c * P:(c + 1) * P],
                                            identf[:, :])
                    last.then_inc(nx_turned, 1)
            pe.wait_ge(qwt_ready, 9)
            wt = Q["wt"]
            for k in range(2 * QC * B):
                b, c, w = k // (2 * QC), k // 2 % QC, k % 2
                pe.wait_ge(nxt_ready, 2 * (b + 1))
                if k >= 4:
                    pe.wait_ge(ug_copied, k - 3)
                for kc in range(KC):
                    at = (1 - w) * QC * D + kc * QF + c * P
                    last = pe.matmul(bank(k % 4), wt[:, at:at + P], Q["xt"][:, kc, b * S:(b + 1) * S],
                                     start=(kc == 0), stop=(kc == KC - 1))
                last.then_inc(ug_done, 1)
            spread_max(1, 2)
            spread_max(2, 1)
            spread_max(3, 1)
            for i in range(NT):
                if i % (NT // 2) == 0:
                    pe.wait_ge(o_int, QC * (i // (NT // 2) + 1))
                if i >= 4:
                    pe.wait_ge(y_final, i - 3)
                for c in range(QC):
                    at = 2 * QC * D + c * D
                    last = pe.matmul(bank(i % 4)[:, 0:D], Q["gate"][:, c, i * P:(i + 1) * P], wt[:, at:at + D],
                                     start=(c == 0), stop=(c == QC - 1))
                last.then_inc(dn_done, 1)


_NAMES = ("x", "ctx_t", "gates", "attn_w", "attn_bqk", "attn_bvo", "expert_indices", "expert_weights", "moe_bias", "w1", "w2",
          "w_gate", "w_up", "w_down")


def layout(inputs):
    a = {k: np.ascontiguousarray(v) for k, v in inputs.items()}

    def by_step(w):
        return np.ascontiguousarray(w.reshape(w.shape[:-1] + (NG, G, DK)).swapaxes(-1, -2)).reshape(w.shape)

    zero = np.zeros(D, a["x"].dtype)
    return {
        "x": a["x"],
        "ctx_t": np.ascontiguousarray(a["ctx_1024"].reshape(B * S, D).T),
        "gates": np.concatenate([a["g_xattn"], a["g_ffn"]]),
        "attn_w": np.stack([
            np.stack([by_step(a["L0_xattn_W_q"].T), by_step(a["L0_xattn_W_k"].T), a["L0_xattn_W_v"].T,
                      a["L0_xattn_W_o"].T]),
            np.stack([by_step(a["L1_xattn_Wq"]), by_step(a["L1_xattn_Wk"]), a["L1_xattn_Wv"], a["L1_xattn_Wo"]])]),
        "attn_bqk": np.stack([np.stack([zero] * 2).reshape(2 * KC, P).T, np.stack(
            [by_step(a["L1_xattn_bq"]), by_step(a["L1_xattn_bk"])]).reshape(2 * KC, P).T]),
        "attn_bvo": np.stack([np.stack([zero] * 2), np.stack([a["L1_xattn_bv"], a["L1_xattn_bo"]])]),
        "expert_indices": a["L0_ffn_expert_indices"],
        "expert_weights": a["L0_ffn_expert_weights"],
        "moe_bias": a["L0_ffn_bias"],
        "w1": a["L0_ffn_w1"],
        "w2": a["L0_ffn_w2"],
        "w_gate": a["L1_ffn_w_gate"],
        "w_up": a["L1_ffn_w_up"],
        "w_down": a["L1_ffn_w_down"],
    }


def kernel(**inputs):
    import concourse.bacc as bacc
    from concourse.bass_utils import run_bass_kernel_spmd

    nc = bacc.Bacc("TRN2", target_bir_lowering=False, num_devices=1)
    arrays = {f"in_{k}": v for k, v in layout(inputs).items()}
    io = {k: nc.dram_tensor(f"in_{k}", arrays[f"in_{k}"].shape, mybir.dt.from_np(arrays[f"in_{k}"].dtype),
                            kind="ExternalInput").ap() for k in _NAMES}
    out = nc.dram_tensor("out_x", (B, S, D), F32, kind="ExternalOutput").ap()
    build_program(nc, io, out)
    result = run_bass_kernel_spmd(nc, [arrays], core_ids=[0])
    return result.results[0]["out_x"]
```

```python
from contextlib import ExitStack

import numpy as np

import concourse.bass as bass
from concourse import mybir

F32 = mybir.dt.float32
BF16 = mybir.dt.bfloat16
I32 = mybir.dt.int32
U32 = mybir.dt.uint32
ALU = mybir.AluOpType
ACT = mybir.ActivationFunctionType
AX = mybir.AxisListType

P = 128
D = 256
KC = D // P
B, S = 4, 512
NT = B * S // P
TB = S // P
H, DK = 16, 16
G = 4
NG = H // G
E = 8
FF = 1024
FC = FF // P
ROUTED = 8
TOPK = 2
SLOT_TILES = ROUTED * TOPK + E - 1
QF = 768
QC = QF // P
BLOCK = 32
EPS = 1e-5
PARTS = 3
ROWS = 6 * DK
Q_RUNS = [(0, 3), (3, 2), (5, 1)]
K_RUNS = [(0, 3), (3, 2), (5, 1)]
MAGIC = 1.5 * 2.0 ** 23
QMAX = 32767.0
TINY = 1e-12
A_MAX, S_X, F_X, S_U, F_U, S_G, F_G, S_2, F_2, S_O, F_O, OUT_F, UNIT, T0, T1 = (0, *range(2, 16))
PIECES = QC * 2
SIG_MAX = 65535.0 / 65536.0
SIG_MAGIC = 1.5 * 2.0 ** 23 / 65536.0


def build_program(nc, io, out):
    with ExitStack() as ctx:
        def sb(name, shape, dt=F32):
            return ctx.enter_context(nc.sbuf_tensor(name, shape, dt))

        def sem(name):
            return ctx.enter_context(nc.semaphore(name))

        PS = ctx.enter_context(nc.psum_tensor("PS", [P, 8, 512], F32))
        BIG = sb("BIG", [P, 32768])
        KSt = sb("KSt", [P, 4 * G * S], BF16)
        Pt = sb("Pt", [P, 4096])
        X = sb("X", [P, NT, D])
        VS = sb("VS", [P, NG, TB, G, DK + 1])
        OT = sb("OT", [P, 2, S])
        WO = sb("WO", [P, KC, D])
        identf = sb("identf", [P, P])
        identb = sb("identb", [P, P], BF16)
        upper = sb("upper", [P, P])
        ones = sb("ones", [P, P])
        gates = sb("gates", [P, 4])
        tg = sb("tg", [P, 4])
        bias_row = sb("bias_row", [P, D])
        stats = sb("stats", [P, NT, 6])
        mv = sb("mv", [P, NT, 2])
        ve = sb("ve", [P, NT])
        sd = sb("sd", [P, NT])
        nw1 = sb("nw1", [P, NT])
        nw2 = sb("nw2", [P, NT])
        rstd = sb("rstd", [P, NT])
        MX = sb("MX", [P, 2, TB, G])
        MP = sb("MP", [P, TB, PARTS, G], BF16)
        MD = sb("MD", [P, TB, G])
        MR = sb("MR", [PARTS * G, 2, S], BF16)
        rden = sb("rden", [P, TB, G])
        pos_i = sb("pos_i", [P, TOPK, ROUTED], U32)
        ew = sb("ew", [P, ROUTED, TOPK])
        expert_i = sb("expert_i", [1, SLOT_TILES + 1], I32)
        zrow = sb("zrow", [P, D])
        magic = sb("magic", [P, 2])
        idx = sb("idx", [P, ROUTED, TOPK], I32)
        idxf = sb("idxf", [P, ROUTED, TOPK])
        hot = sb("hot", [P, ROUTED, TOPK, E])
        slots = sb("slots", [P, ROUTED, E])
        totals = sb("totals", [P, ROUTED, E])
        before = sb("before", [P, ROUTED, E])
        place = sb("place", [P, ROUTED, E])
        picked = sb("picked", [P, ROUTED, E])
        posf = sb("posf", [P, TOPK, ROUTED])
        rt = [sb(f"rt{i}", [P, E]) for i in range(4)]
        rti = [sb(f"rti{i}", [P, E], I32) for i in range(2)]
        upto = sb("upto", [P, E])
        ex = [sb(f"ex{i}", [1, SLOT_TILES + 1]) for i in range(2)]
        tile_no = sb("tile_no", [P, SLOT_TILES + 1], I32)
        tile_f = sb("tile_f", [P, SLOT_TILES + 1])
        sc = sb("sc", [P, 16])
        cm = sb("cm", [P, 2])
        cmx = sb("cmx", [P, 64])
        one = sb("one", [1, 2])
        ws = sb("ws", [P, 3, 3, QC * D // BLOCK])

        W1 = BIG[:, 0:E * KC * FF]
        W2 = BIG[:, E * KC * FF:2 * E * KC * FF]
        QS = BIG[:, 28672:32768].bitcast(BF16).rearrange("p (g h t) -> p g h t", g=NG, h=G)
        KS = KSt[:, :].rearrange("p (g h t) -> p g h t", g=NG, h=G)
        OALL = BIG[:, 24576:28672].rearrange("p (i n) -> p i n", i=NT)
        at = 4608
        CT = BIG[:, at:at + 4096].rearrange("p (c t) -> p c t", c=KC); at += 4096
        XNT = BIG[:, at:at + 1024].rearrange("p (c t) -> p c t", c=KC); at += 1024
        PT = BIG[:, at:at + 3072].bitcast(BF16).rearrange("p (j r t) -> p j r t", j=4, r=PARTS); at += 3072
        VB = BIG[:, at:at + TB * H * (DK + 1)].rearrange("p (t h d) -> p t h d", t=TB, h=H); at += TB * H * (DK + 1)
        RB = BIG[:, at:at + 1024].rearrange("p (j t) -> p j t", j=2); at += 1024
        AW = BIG[:, at:at + 1536].rearrange("p (c n) -> p c n", c=3 * KC); at += 1536
        BV = BIG[:, at:at + D]; at += D
        BQK = BIG[:, at:at + 4]; at += 4
        TGBO = BIG[:, at:at + D]; at += D
        assert at <= 24576 - 3 * QC * D
        XN = Pt[:, :].rearrange("p (i n) -> p i n", i=NT)
        PP = Pt[:, :].rearrange("p (q h t) -> p q h t", q=4, h=2)

        qk_dram = nc.dram_tensor("qk_parts", (2, 2, B, PARTS, D, S), BF16).ap()
        v_dram = nc.dram_tensor("v_rows", (2, B, NG, P, TB, G, DK + 1), F32).ap()
        xs_dram = nc.dram_tensor("slot_rows", ((SLOT_TILES + 1) * P, D), F32).ap()
        ys_dram = nc.dram_tensor("slot_results", ((SLOT_TILES + 1) * P, D), F32).ap()

        x_in = [sem(f"x_in{b}") for b in range(B)]
        gates_in = sem("gates_in")
        aw_in = sem("aw_in")
        wo_in = sem("wo_in")
        ct_in = sem("ct_in")
        consts = sem("consts")
        tg_ready = sem("tg_ready")
        ln_var = sem("ln_var")
        ln_sd = sem("ln_sd")
        xn_ready = sem("xn_ready")
        dve_link = sem("dve_link")
        tr_done = sem("tr_done")
        xnt_evac = sem("xnt_evac")
        qk_done = sem("qk_done")
        hi_done = sem("hi_done")
        r_done = sem("r_done")
        mid_done = sem("mid_done")
        lo_done = sem("lo_done")
        part_out = [sem(f"part_out{j}") for j in range(4)]
        v_done = sem("v_done")
        v_taken = sem("v_taken")
        v_out = sem("v_out")
        q_stack = [sem(f"q_stack{g}") for g in range(NG)]
        v_stack = [sem(f"v_stack{g}") for g in range(NG)]
        max_done = sem("max_done")
        max_taken = sem("max_taken")
        max_link = sem("max_link")
        max_parts = sem("max_parts")
        max_turned = sem("max_turned")
        max_copied = sem("max_copied")
        max_rows = [sem(f"max_rows{g}") for g in range(NG)]
        st_done = sem("st_done")
        exp_done = sem("exp_done")
        pv_done = sem("pv_done")
        ot_ready = sem("ot_ready")
        ot_turned = sem("ot_turned")
        rden_ready = sem("rden_ready")
        o_ready = sem("o_ready")
        pv_zero = sem("pv_zero")
        tro_done = sem("tro_done")
        on_evac = sem("on_evac")
        out_done = sem("out_done")
        x_upd = sem("x_upd")
        biased = sem("biased")
        idx_in = sem("idx_in")
        gp_consts = sem("gp_consts")
        ones_rows = sem("ones_rows")
        tg_bias = sem("tg_bias")
        gate_int = sem("gate_int")
        o_int = sem("o_int")
        onehots = sem("onehots")
        ranks = sem("ranks")
        routed = sem("routed")
        zeroed = sem("zeroed")
        scattered = sem("scattered")
        w1_in = sem("w1_in")
        w2_in = sem("w2_in")
        xs_in = [sem(f"xs_in{q}") for q in range(2)]
        xs_turned = sem("xs_turned")
        xst_ready = sem("xst_ready")
        h_done = sem("h_done")
        gelu_done = sem("gelu_done")
        ht_turned = sem("ht_turned")
        ht_ready = sem("ht_ready")
        y_done = sem("y_done")
        ys_ready = sem("ys_ready")
        ys_out = [sem(f"ys_out{q}") for q in range(2)]
        gathered = [sem(f"gathered{i}") for i in range(ROUTED)]
        combined = sem("combined")
        qw_in = sem("qw_in")
        qw_ready = sem("qw_ready")
        qwt_turned = sem("qwt_turned")
        qwt_ready = sem("qwt_ready")
        col_max = sem("col_max")
        max_col_turned = sem("max_col_turned")
        max_one = sem("max_one")
        max_spread = sem("max_spread")
        nx_ready = sem("nx_ready")
        nx_turned = sem("nx_turned")
        nxt_ready = sem("nxt_ready")
        ug_done = sem("ug_done")
        ug_copied = sem("ug_copied")
        ug_max = sem("ug_max")
        scales = sem("scales")
        q_magic = sem("q_magic")
        w_scales = sem("w_scales")
        qw_step = sem("qw_step")
        up_magic = sem("up_magic")
        up_int = sem("up_int")
        gate_magic = sem("gate_magic")
        sig_round = sem("sig_round")
        gate_scaled = sem("gate_scaled")
        o_scaled = sem("o_scaled")
        sig_done = sem("sig_done")
        prod_done = sem("prod_done")
        dn_done = sem("dn_done")
        y_final = sem("y_final")
        stored = sem("stored")

        block = ctx.enter_context(nc.Block())


        def moe_buffers():
            k32 = KSt[:, :].bitcast(F32)
            return dict(
                xs=k32[:, 0:512].rearrange("p (q n) -> p q n", q=2),
                xst=k32[:, 512:1024].rearrange("p (q n) -> p q n", q=2),
                ys=k32[:, 1024:1536].rearrange("p (q n) -> p q n", q=2),
                h=Pt[:, 0:2048].rearrange("p (q n) -> p q n", q=2),
                ht=Pt[:, 2048:4096].rearrange("p (q c n) -> p q c n", q=2, c=FC),
                got=Pt[:, :].rearrange("p (k i n) -> p k i n", k=TOPK, i=ROUTED),
            )

        def quant_buffers():
            return dict(
                raw=BIG[:, 24576 - 3 * QC * D:24576],
                wt=BIG[:, 0:3 * QC * D],
                up=BIG[:, 4608:16896].rearrange("p (c t) -> p c t", c=QC),
                gate=BIG[:, 16896:29184].rearrange("p (c t) -> p c t", c=QC),
                xt=KSt[:, :].bitcast(F32).rearrange("p (c t) -> p c t", c=KC),
                sig=Pt[:, 0:2048].rearrange("p (q n) -> p q n", q=2),
            )

        def quant_weight(k):
            w = Q["raw"][:, k * QC * D:(k + 1) * QC * D]
            return w, w.rearrange("p (b n) -> p b n", n=BLOCK), QC * D // BLOCK

        def some_gate(b, part):
            return Q["gate"][:, part * (QC // 2):(part + 1) * (QC // 2), b * S:(b + 1) * S]

        M = moe_buffers()
        Q = quant_buffers()

        def bank(i, k=1):
            return PS[:, i:i + k, :].rearrange("p a b -> p (a b)")

        ST = [bank(0, 2), bank(2, 2)]
        SM = [bank(4), bank(5)]
        PV = bank(6)
        MISC = bank(7)

        linked = [0]

        def link(eng, ins):
            linked[0] += 1
            ins.then_inc(dve_link, 1)
            eng.wait_ge(dve_link, linked[0])

        def wait(eng, s, value):
            if not isinstance(value, int) or value > 0:
                eng.wait_ge(s, value)

        def over_batches(eng, layer, body):
            body(B * layer, True, False)
            with eng.Fori(B * layer + 1, B * layer + B - 1) as n:
                body(n, False, False)
            body(B * layer + B - 1, False, True)

        def over_tiles(eng, body):
            with eng.Fori(0, (SLOT_TILES - 3) // 2) as m:
                for q in range(2):
                    body(m, q, None)
            for t in range(SLOT_TILES - 3, SLOT_TILES):
                body(t // 2, t % 2, t)

        assert SLOT_TILES % 2 == 1
        
        def piece(ap, i):
            return ap[:, i // 2, i % 2 * 1024:i % 2 * 1024 + 1024]

        def ug_place(k):
            return Q["gate" if k % 2 else "up"][:, k // 2 % QC, k // (2 * QC) * S:k // (2 * QC) * S + S]

        NORM_BASE = [0, NT, NT + ROUTED, 2 * NT + ROUTED]

        @block.sync
        def _(sp):
            def load_layer(layer):
                sp.dma_start(AW, io["attn_w"][layer, 0:3].rearrange("w (c p) n -> p (w c) n", p=P)).then_inc(aw_in, 16)
                sp.dma_start(BQK, io["attn_bqk"][layer]).then_inc(aw_in, 16)
                sp.dma_start(BV, io["attn_bvo"][layer, 0].partition_broadcast(P)).then_inc(aw_in, 16)
                sp.dma_start(TGBO, io["attn_bvo"][layer, 1].partition_broadcast(P)).then_inc(aw_in, 16)
                for c in range(KC):
                    sp.dma_start(CT[:, c, :], io["ctx_t"][c * P:(c + 1) * P, :]).then_inc(ct_in, 16)

            def prep(layer):
                for b in range(B):
                    n = B * layer + b
                    for j in range(4):
                        which, c = 1 - j // 2, j % 2
                        if j == 2:
                            sp.wait_ge(v_taken, 2 * (n + 1))
                            for g in range(NG):
                                sp.dma_start(v_dram[layer, b, g], VB[:, :, G * g:G * g + G, :]).then_inc(v_out, 16)
                        sp.wait_ge(lo_done, 4 * n + j + 1)
                        sp.dma_start(qk_dram[layer, which, b, :, c * P:(c + 1) * P, :].rearrange("r p t -> p r t"),
                                     PT[:, j, :, :]).then_inc(part_out[j], 16)

            def load_stack(layer, b, g):
                rows = slice(g * G * DK, (g + 1) * G * DK)
                for first, k, part in ((0, 3, 0), (3, 2, 1), (5, 1, 2)):
                    dst = slice(first * DK, (first + k) * DK)
                    q = qk_dram[layer, 0, b, part, rows, :].rearrange("(d h) t -> d (h t)", h=G)
                    sp.dma_start(QS[dst, g, :, :].rearrange("p h t -> p (h t)"),
                                 q.unsqueeze(0).to_broadcast([k, DK, G * S])).then_inc(q_stack[g], 16)
                    kk = qk_dram[layer, 1, b, 0:k, rows, :].rearrange("r (d h) t -> r d (h t)", h=G)
                    sp.dma_start(KS[dst, g, :, :].rearrange("p h t -> p (h t)"), kk).then_inc(q_stack[g], 16)

            def load_v(layer, b, g):
                sp.dma_start(VS[:, g], v_dram[layer, b, g]).then_inc(v_stack[g], 16)

            def load_max_rows(g):
                sp.dma_start(QS[ROWS:ROWS + PARTS, g, :, :], MR[:, g % 2, :]).then_inc(max_rows[g], 16)

            def attention(layer):
                for j in range(4):
                    sp.wait_ge(part_out[j], 16 * B * (layer + 1))
                sp.wait_ge(v_out, 16 * NG * B * (layer + 1))
                for g in range(NG):
                    load_stack(layer, 0, g)
                    load_v(layer, 0, g)
                sp.wait_ge(max_copied, NG * B * layer + 1)
                load_max_rows(0)

                def batch(n, first, last):
                    for g in range(NG):
                        s = NG * n + g
                        if not (last and g == NG - 1):
                            sp.wait_ge(max_copied, s + 2)
                            load_max_rows((g + 1) % NG)
                        if not last:
                            sp.wait_ge(st_done, 8 * (s + 1))
                            load_stack(layer, n + 1 - B * layer, g)
                            sp.wait_ge(pv_done, 4 * (s + 1))
                            load_v(layer, n + 1 - B * layer, g)
                over_batches(sp, layer, batch)

            sp.dma_start(gates[:, :], io["gates"].partition_broadcast(P)).then_inc(gates_in, 16)
            for b in range(B):
                sp.dma_start(X[:, TB * b:TB * b + TB, :],
                             io["x"][b].rearrange("(i p) n -> p i n", p=P)).then_inc(x_in[b], 16)
            load_layer(0)
            sp.dma_start(WO[:, :, :], io["attn_w"][0, 3].rearrange("(c p) n -> p c n", p=P)).then_inc(wo_in, 16)
            sp.dma_start(ew[:, :, :], io["expert_weights"].rearrange("(i p) k -> p i k", p=P)).then_inc(idx_in, 16)
            sp.dma_start(idx[:, :, :], io["expert_indices"].rearrange("(i p) k -> p i k", p=P)).then_inc(idx_in, 16)
            sp.dma_start(bias_row[:, :], io["moe_bias"].partition_broadcast(P)).then_inc(idx_in, 16)
            prep(0)
            attention(0)

            sp.wait_ge(out_done, NT)
            sp.dma_start(WO[:, :, :], io["attn_w"][1, 3].rearrange("(c p) n -> p c n", p=P)).then_inc(wo_in, 16)

            def load_slots(m, q, t):
                if t is None or t >= 2:
                    sp.wait_ge(xs_turned, 2 * m + q - 1)
                sp.dma_start(M["xs"][:, q, :], slot_tile(xs_dram, m, q)).then_inc(xs_in[q], 16)

            def store_results(m, q):
                sp.wait_ge(ys_ready, 2 * m + q + 1)
                sp.dma_start(slot_tile(ys_dram, m, q), M["ys"][:, q, :]).then_inc(ys_out[q], 16)

            def slot_tile(dram, m, q):
                return dram.rearrange("(m q p) n -> m q p n", q=2, p=P)[m, q]

            sp.wait_ge(scattered, 16 * TOPK * ROUTED)
            load_slots(0, 0, 0)
            load_slots(0, 1, 1)
            with sp.Fori(0, (SLOT_TILES - 3) // 2) as m:
                for q in range(2):
                    load_slots(m + 1, q, None)
                    store_results(m, q)
            t = SLOT_TILES - 1
            load_slots(t // 2, t % 2, t)
            for t in range(SLOT_TILES - 3, SLOT_TILES):
                store_results(t // 2, t % 2)

            sp.wait_ge(y_done, SLOT_TILES)
            load_layer(1)
            raw = Q["raw"]
            sp.dma_start(raw[:, 0:QC * D].rearrange("p (c n) -> p c n", c=QC),
                         io["w_gate"].rearrange("(c p) n -> p c n", p=P)).then_inc(qw_in, 16)
            sp.dma_start(raw[:, QC * D:2 * QC * D].rearrange("p (c n) -> p c n", c=QC),
                         io["w_up"].rearrange("(c p) n -> p c n", p=P)).then_inc(qw_in, 16)
            sp.dma_start(raw[:, 2 * QC * D:].rearrange("p (c n) -> p c n", c=KC),
                         io["w_down"].rearrange("(c p) n -> p c n", p=P)).then_inc(qw_in, 16)
            prep(1)
            attention(1)

            for i in range(NT):
                sp.wait_ge(y_final, i + 1)
                sp.dma_start(out[i // TB, (i % TB) * P:(i % TB + 1) * P, :], X[:, i, :]).then_inc(stored, 16)
            sp.wait_ge(stored, 16 * NT)

        @block.gpsimd
        def _(gp):
            gp.memset(identf[:, :], 0.0).then_inc(gp_consts, 1)
            gp.memset(upper[:, :], 1.0).then_inc(gp_consts, 1)
            gp.memset(ones[:, :], 1.0).then_inc(gp_consts, 1)
            gp.memset(zrow[:, :], 0.0).then_inc(gp_consts, 1)
            gp.memset(magic[:, 0:1], MAGIC).then_inc(gp_consts, 1)
            gp.memset(magic[:, 1:2], -MAGIC).then_inc(gp_consts, 1)
            gp.memset(VB[:, :, :, DK:DK + 1], 1.0).then_inc(gp_consts, 1)
            gp.iota(tile_no[:, :], pattern=[[1, SLOT_TILES + 1]], base=0, channel_multiplier=0).then_inc(gp_consts, 1)
            gp.wait_ge(gp_consts, 8)
            gp.affine_select(out=identf[:, :], in_=identf[:, :], compare_op=ALU.not_equal, fill=1.0, base=0,
                             pattern=[[-1, P]], channel_multiplier=1).then_inc(consts, 1)
            gp.affine_select(out=upper[:, :], in_=upper[:, :], compare_op=ALU.is_gt, fill=0.0, base=0,
                             pattern=[[1, P]], channel_multiplier=-1).then_inc(consts, 1)
            gp.wait_ge(consts, 1)
            gp.tensor_copy(identb[:, :], identf[:, :]).then_inc(consts, 1)
            gp.wait_ge(consts, 3)
            gp.memset(KS[ROWS:ROWS + PARTS, :, :, :], 1.0).then_inc(ones_rows, 1)
            gp.wait_ge(ones_rows, 1)

            def prep(layer):
                for n in range(B * layer, B * layer + B):
                    for j in range(4):
                        gp.wait_ge(mid_done, 4 * n + j + 1)
                        gp.tensor_tensor(PT[:, j, 2, :], RB[:, j % 2, :], PT[:, j, 1, :],
                                         ALU.subtract).then_inc(lo_done, 1)

            prep(0)

            def load_w1(e):
                gp.dma_start(W1[:, e * KC * FF:(e + 1) * KC * FF].rearrange("p (c n) -> p c n", c=KC),
                             io["w1"][e].rearrange("(c p) n -> p c n", p=P)).then_inc(w1_in, 16)

            def load_w2(e):
                gp.dma_start(W2[:, e * FC * D:(e + 1) * FC * D].rearrange("p (c n) -> p c n", c=FC),
                             io["w2"][e].rearrange("(c p) n -> p c n", p=P)).then_inc(w2_in, 16)

            gp.wait_ge(aw_in, 64)
            for j in range(4):
                gp.wait_ge(part_out[j], 16 * B)
            gp.wait_ge(v_out, 16 * NG * B)
            gp.wait_ge(qk_done, 4 * B)
            gp.wait_ge(st_done, 8)
            gp.dma_start(xs_dram.rearrange("(t p) n -> p t n", p=P),
                         zrow[:, :].unsqueeze(1).to_broadcast([P, SLOT_TILES + 1, D])).then_inc(zeroed, 16)
            for e in range(E):
                gp.wait_ge(st_done, 8 * (e + 2))
                load_w1(e)
            for e in range(4):
                gp.wait_ge(st_done, 8 * (e + E + 2))
                load_w2(e)
            gp.wait_ge(st_done, 8 * NG * B)
            for e in (6, 7):
                load_w2(e)
            gp.wait_ge(tro_done, NT)
            for e in (4, 5):
                load_w2(e)

            gp.wait_ge(routed, 1)
            gp.wait_ge(zeroed, 16)
            for i in range(ROUTED):
                gp.wait_ge(xn_ready, NORM_BASE[1] + i + 1)
                for k in range(TOPK):
                    gp.indirect_dma_start(out=xs_dram[:, :],
                                          out_offset=bass.IndirectOffsetOnAxis(ap=pos_i[:, k, i:i + 1], axis=0),
                                          in_=XN[:, i, :], in_offset=None).then_inc(scattered, 16)
            gp.wait_ge(tg_bias, 1)
            for i in range(NT):
                if i == 0:
                    gp.wait_ge(x_upd, NT)
                gp.tensor_tensor(X[:, i, :], X[:, i, :], bias_row[:, :], ALU.add).then_inc(biased, 1)
            gp.wait_ge(ys_out[0], 16 * ((SLOT_TILES + 1) // 2))
            gp.wait_ge(ys_out[1], 16 * (SLOT_TILES // 2))
            for i in range(ROUTED):
                for k in range(TOPK):
                    gp.indirect_dma_start(out=M["got"][:, k, i, :], out_offset=None, in_=ys_dram[0:SLOT_TILES * P, :],
                                          in_offset=bass.IndirectOffsetOnAxis(ap=pos_i[:, k, i:i + 1], axis=0),
                                          ).then_inc(gathered[i], 16)

            gp.wait_ge(y_done, SLOT_TILES)
            gp.wait_ge(ys_out[0], 16 * ((SLOT_TILES + 1) // 2))
            gp.memset(VB[:, :, :, DK:DK + 1], 1.0).then_inc(gp_consts, 1)
            gp.wait_ge(gp_consts, 9)
            gp.memset(KS[ROWS:ROWS + PARTS, :, :, :], 1.0).then_inc(ones_rows, 1)
            gp.wait_ge(ones_rows, 2)
            prep(1)
            gp.wait_ge(tg_bias, 2)
            gp.wait_ge(xn_ready, NORM_BASE[3])
            for i in range(NT):
                gp.tensor_tensor(X[:, i, :], X[:, i, :], bias_row[:, :], ALU.add).then_inc(biased, 1)

            steps = 0
            for k in range(3):
                gp.wait_ge(w_scales, k + 1)
                w, wb, nb = quant_weight(k)
                factor = ws[:, k, 2, 0:nb].unsqueeze(2).to_broadcast([P, nb, BLOCK])
                scale = ws[:, k, 1, 0:nb].unsqueeze(2).to_broadcast([P, nb, BLOCK])
                gp.tensor_tensor(wb, wb, factor, ALU.mult).then_inc(qw_step, 1)
                for first, op0, second, op1 in ((MAGIC, ALU.add, 1.0, ALU.mult),
                                                (MAGIC + 7.0, ALU.min, MAGIC - 8.0, ALU.max),
                                                (-MAGIC, ALU.add, 1.0, ALU.mult)):
                    steps += 1
                    gp.wait_ge(qw_step, steps)
                    gp.tensor_scalar(w, w, first, second, op0, op1).then_inc(qw_step, 1)
                steps += 1
                gp.wait_ge(qw_step, steps)
                gp.tensor_tensor(wb, wb, scale, ALU.mult).then_inc(qw_ready, 1)

            gp.wait_ge(scales, 2)
            for i in range(PIECES):
                ap = piece(Q["up"], i)
                gp.tensor_scalar(ap, ap, sc[:, F_U:F_U + 1], MAGIC, ALU.mult, ALU.add).then_inc(up_magic, 1)
                gp.wait_ge(up_magic, i + 1)
                gp.tensor_scalar(ap, ap, -MAGIC, 1.0, ALU.add, ALU.mult).then_inc(up_int, 1)

        @block.scalar
        def _(act):
            act.wait_ge(gates_in, 16)
            act.wait_ge(gp_consts, 8)
            act.activation(tg[:, :], gates[:, :], ACT.Tanh).then_inc(tg_ready, 1)

            def norm(k):
                act.wait_ge(ln_var, k + 1)
                act.activation(sd[:, :], ve[:, :], ACT.Sqrt).then_inc(ln_sd, 1)

            def prep(layer):
                act.wait_ge(aw_in, 64 * (layer + 1))
                for n in range(B * layer, B * layer + B):
                    for c in range(KC):
                        act.wait_ge(tr_done, KC * n + c + 1)
                        wait(act, qk_done, 4 * n)
                        act.activation(XNT[:, c, :], bank(c), ACT.Copy).then_inc(xnt_evac, 1)
                    for j in range(4):
                        which, c = 1 - j // 2, j % 2
                        act.wait_ge(qk_done, 4 * n + j + 1)
                        wait(act, part_out[j], 16 * n)
                        act.activation(PT[:, j, 0, :], bank(2 + j), ACT.Identity,
                                       bias=BQK[:, 2 * which + c:2 * which + c + 1]).then_inc(hi_done, 1)

            def copy_out(s, q):
                act.wait_ge(pv_done, 4 * (s + 1))
                wait(act, ot_turned, s - 1)
                act.activation(OT[:, q, :], PV, ACT.Copy).then_inc(ot_ready, 1)

            def copy_max(n, g):
                act.wait_ge(max_turned, NG * n + g + 1)
                wait(act, max_rows[(g + 2) % NG], 16 * (n + g // 2))
                act.activation(MR[:, g % 2, :], MISC[0:PARTS * G, 0:S // 2].bitcast(BF16),
                               ACT.Copy).then_inc(max_copied, 1)

            def attention(layer):
                copy_max(B * layer, 0)

                def batch(n, first, last):
                    for g in range(NG):
                        s = NG * n + g
                        for kc in range(TB):
                            u = 4 * s + kc
                            for half in range(2):
                                act.wait_ge(st_done, 2 * u + half + 1)
                                wait(act, pv_done, u - 1)
                                act.activation(PP[:, 2 * (kc % 2) + half, :, :].rearrange("p h t -> p (h t)"),
                                               ST[half], ACT.Exp, scale=DK ** -0.5).then_inc(exp_done, 1)
                            if kc == 0 and not (first and g == 0):
                                copy_out(s - 1, (g + 1) % 2)
                            if kc == 1 and not (last and g == NG - 1):
                                copy_max(n + (g + 1) // NG, (g + 1) % NG)
                over_batches(act, layer, batch)
                copy_out(NG * B * (layer + 1) - 1, 1)

            def tail(layer):
                for i in range(NT):
                    t = NT * layer + i
                    act.wait_ge(tro_done, t + 1)
                    wait(act, out_done, t - 1)
                    act.activation(OT[:, i % 2, 0:D], bank(i % 2)[:, 0:D], ACT.Copy).then_inc(on_evac, 1)

            norm(0)
            prep(0)
            attention(0)
            tail(0)
            norm(1)

            def expert_tile(m, q, t):
                if t is None or t + 1 < SLOT_TILES:
                    gelu(m, q, 1, t)
                act.wait_ge(y_done, 2 * m + q + 1)
                act.activation(M["ys"][:, q, :], bank(4 + q)[:, 0:D], ACT.Copy).then_inc(ys_ready, 1)

            def gelu(m, q, ahead, t):
                nq = (q + ahead) % 2
                for half in range(2):
                    act.wait_ge(h_done, 2 * (2 * m + q + ahead) + half + 1)
                    act.activation(M["h"][:, nq, half * 512:half * 512 + 512], bank(half),
                                   ACT.Gelu).then_inc(gelu_done, 1)

            gelu(0, 0, 0, 0)
            expert_tile(0, 0, 0)
            expert_tile(0, 1, 1)
            with act.Fori(1, (SLOT_TILES - 3) // 2) as m:
                for q in range(2):
                    act.wait_ge(ys_out[q], 16 * m)
                    expert_tile(m, q, None)
            for t in range(SLOT_TILES - 3, SLOT_TILES):
                act.wait_ge(ys_out[t % 2], 16 * (t // 2))
                expert_tile(t // 2, t % 2, t)

            norm(2)
            prep(1)
            attention(1)
            tail(1)

            for k in range(3):
                for a in range(3):
                    act.wait_ge(qwt_turned, 3 * k + a + 1)
                    act.activation(Q["wt"][:, k * QC * D + a * 512:k * QC * D + a * 512 + 512], bank(4 + a),
                                   ACT.Copy).then_inc(qwt_ready, 1)
            norm(3)
            for i in range(B):
                for c in range(KC):
                    act.wait_ge(nx_turned, 2 * i + c + 1)
                    act.activation(Q["xt"][:, c, i * S:(i + 1) * S], bank(i % 2 * 2 + c), ACT.Copy).then_inc(nxt_ready, 1)
            act.wait_ge(scales, 1)
            act.wait_ge(nxt_ready, 2 * B)
            for i in range(B):
                ap = Q["xt"][:, :, i * S:(i + 1) * S]
                act.activation(ap, ap, ACT.Identity, scale=sc[:, F_X:F_X + 1], bias=magic[:, 0:1]).then_inc(q_magic, 1)
            for k in range(2 * QC * B):
                act.wait_ge(ug_done, k + 1)
                act.activation(ug_place(k), bank(k % 4), ACT.Copy).then_inc(ug_copied, 1)
            act.wait_ge(scales, 2)
            for i in range(PIECES + 1):
                if i < PIECES:
                    ap = piece(Q["gate"], i)
                    act.activation(ap, ap, ACT.Identity, scale=sc[:, F_G:F_G + 1],
                                   bias=magic[:, 0:1]).then_inc(gate_magic, 1)
                if i > 0:
                    j = i - 1
                    act.wait_ge(gate_int, j + 1)
                    wait(act, prod_done, j - 1)
                    act.activation(Q["sig"][:, j % 2, :], piece(Q["gate"], j), ACT.Sigmoid,
                                   scale=sc[:, S_G:S_G + 1]).then_inc(sig_done, 1)
                if i < PIECES:
                    act.wait_ge(gate_magic, i + 1)
                    act.activation(ap, ap, ACT.Identity, bias=magic[:, 1:2]).then_inc(gate_int, 1)
            act.wait_ge(scales, 3)
            for i in range(PIECES):
                ap = piece(Q["gate"], i)
                act.activation(ap, ap, ACT.Identity, scale=sc[:, F_2:F_2 + 1],
                               bias=magic[:, 0:1]).then_inc(gate_scaled, 1)
            act.wait_ge(scales, 4)
            for b in range(B):
                for part in range(2):
                    ap = some_gate(b, part)
                    act.activation(ap, ap, ACT.Identity, scale=sc[:, F_O:F_O + 1],
                                   bias=magic[:, 0:1]).then_inc(o_scaled, 1)

        @block.vector
        def _(dve):
            def routing():
                dve.wait_ge(idx_in, 48)
                dve.wait_ge(gp_consts, 8)
                dve.tensor_copy(tile_f[:, :], tile_no[:, :])
                link(dve, dve.tensor_copy(idxf[:, :, :], idx[:, :, :]))
                for e in range(E):
                    last = dve.tensor_scalar(hot[:, :, :, e], idxf[:, :, :], float(e), None, ALU.is_equal)
                link(dve, last)
                dve.tensor_tensor(slots[:, :, :], hot[:, :, 0, :], hot[:, :, 1, :], ALU.add).then_inc(onehots, 1)
                dve.wait_ge(ranks, 1)
                dve.memset(before[:, 0, :], 0.0)
                link(dve, dve.tensor_copy(totals[:, :, :].rearrange("p i e -> p (i e)"), bank(1)[:, 0:ROUTED * E]))
                for i in range(1, ROUTED):
                    link(dve, dve.tensor_tensor(before[:, i, :], before[:, i - 1, :], totals[:, i - 1, :], ALU.add))
                link(dve, dve.tensor_tensor(rt[0][:, :], before[:, ROUTED - 1, :], totals[:, ROUTED - 1, :], ALU.add))
                link(dve, dve.tensor_scalar(rti[0][:, :], rt[0][:, :], float(P - 1), None, ALU.add))
                link(dve, dve.tensor_scalar(rti[1][:, :], rti[0][:, :], 7, None, ALU.arith_shift_right))
                link(dve, dve.tensor_copy(rt[1][:, :], rti[1][:, :]))
                link(dve, dve.tensor_copy(upto[:, 0:1], rt[1][:, 0:1]))
                for e in range(1, E):
                    link(dve, dve.tensor_tensor(upto[:, e:e + 1], upto[:, e - 1:e], rt[1][:, e:e + 1], ALU.add))
                link(dve, dve.tensor_tensor(rt[2][:, :], upto[:, :], rt[1][:, :], ALU.subtract))
                link(dve, dve.tensor_scalar(rt[3][:, :], rt[2][:, :], float(P), None, ALU.mult))
                link(dve, dve.tensor_tensor(place[:, :, :].rearrange("p i e -> p (i e)"), bank(0)[:, 0:ROUTED * E],
                                            before[:, :, :].rearrange("p i e -> p (i e)"), ALU.add))
                link(dve, dve.tensor_tensor(place[:, :, :], place[:, :, :],
                                            rt[3][:, :].unsqueeze(1).to_broadcast([P, ROUTED, E]), ALU.add))
                for k in range(TOPK):
                    link(dve, dve.tensor_tensor(picked[:, :, :], place[:, :, :], hot[:, :, k, :], ALU.mult))
                    link(dve, dve.tensor_reduce(posf[:, k, :], picked[:, :, :], AX.X, ALU.add))
                    if k == 0:
                        link(dve, dve.tensor_tensor(place[:, :, :], place[:, :, :], hot[:, :, 0, :], ALU.add))
                dve.tensor_copy(pos_i[:, :, :], posf[:, :, :])
                link(dve, dve.memset(ex[0][:, :], 0.0))
                for e in range(E):
                    link(dve, dve.scalar_tensor_tensor(ex[(e + 1) % 2][:, :], tile_f[0:1, :], upto[0:1, e:e + 1],
                                                       ex[e % 2][:, :], ALU.is_ge, ALU.add))
                link(dve, dve.tensor_scalar(ex[1][:, :], ex[0][:, :], float(E - 1), None, ALU.min))
                dve.tensor_copy(expert_i[:, :], ex[1][:, :]).then_inc(routed, 1)

            def norm(k, tiles):
                for i in range(tiles):
                    if k == 0 and i % TB == 0:
                        dve.wait_ge(x_in[i // TB], 16)
                    last = dve.bn_stats(stats[:, i, :], X[:, i, :])
                link(dve, last)
                for i in range(tiles):
                    last = dve.bn_aggr(mv[:, i, :], stats[:, i, :])
                link(dve, last)
                dve.tensor_scalar(ve[:, :], mv[:, :, 1], EPS, None, ALU.add).then_inc(ln_var, 1)
                dve.wait_ge(ln_sd, k + 1)
                link(dve, dve.reciprocal(nw1[:, :], sd[:, :]))
                link(dve, dve.tensor_tensor(nw2[:, :], ve[:, :], nw1[:, :], ALU.mult))
                link(dve, dve.tensor_tensor(nw1[:, :], nw2[:, :], sd[:, :], ALU.add))
                link(dve, dve.tensor_scalar(nw2[:, :], nw1[:, :], 0.5, None, ALU.mult))
                link(dve, dve.reciprocal(rstd[:, :], nw2[:, :]))
                for i in range(tiles):
                    dve.tensor_scalar(XN[:, i, :], X[:, i, :], mv[:, i, 0:1], rstd[:, i:i + 1],
                                      ALU.subtract, ALU.mult).then_inc(xn_ready, 1)

            def prep(layer):
                dve.wait_ge(aw_in, 64 * (layer + 1))
                dve.wait_ge(gp_consts, 8 + layer)
                for n in range(B * layer, B * layer + B):
                    for j in range(4):
                        which, c = 1 - j // 2, j % 2
                        if j == 2:
                            for t2 in range(2):
                                dve.wait_ge(v_done, 2 * n + t2 + 1)
                                wait(dve, v_out, 16 * NG * n)
                                for t in range(2):
                                    last = dve.tensor_tensor(
                                        VB[:, 2 * t2 + t, :, 0:DK],
                                        bank(6 + t2)[:, t * D:t * D + D].rearrange("p (h d) -> p h d", h=H),
                                        BV.rearrange("p (h d) -> p h d", h=H), ALU.add)
                                last.then_inc(v_taken, 1)
                        dve.wait_ge(hi_done, 4 * n + j + 1)
                        wait(dve, lo_done, 4 * n + j - 1)
                        dve.scalar_tensor_tensor(RB[:, j % 2, :], bank(2 + j),
                                                 BQK[:, 2 * which + c:2 * which + c + 1], PT[:, j, 0, :],
                                                 ALU.add, ALU.subtract).then_inc(r_done, 1)
                        dve.wait_ge(r_done, 4 * n + j + 1)
                        dve.tensor_copy(PT[:, j, 1, :], RB[:, j % 2, :]).then_inc(mid_done, 1)

            def split_max(n, g):
                s, q = NG * n + g, g % 2
                dve.wait_ge(max_taken, 16 * (s + 1))
                wait(dve, max_turned, s)
                dve.tensor_copy(MP[:, :, 0, :], MX[:, q, :, :]).then_inc(max_link, 1)
                dve.wait_ge(max_link, 3 * s + 1)
                dve.tensor_tensor(MD[:, :, :], MX[:, q, :, :], MP[:, :, 0, :], ALU.subtract).then_inc(max_link, 1)
                dve.wait_ge(max_link, 3 * s + 2)
                dve.tensor_copy(MP[:, :, 1, :], MD[:, :, :]).then_inc(max_link, 1)
                dve.wait_ge(max_link, 3 * s + 3)
                dve.tensor_tensor(MP[:, :, 2, :], MD[:, :, :], MP[:, :, 1, :], ALU.subtract).then_inc(max_parts, 1)

            def maxima(n, g, some):
                for i in some:
                    dve.wait_ge(max_done, 16 * (NG * n + g) + i + 1)
                    dve.tensor_reduce(MX[:, g % 2, i % TB, i // TB:i // TB + 1], SM[i % 2], AX.X, ALU.max,
                                      negate=True).then_inc(max_taken, 1)

            def normalise(s, n, g):
                dve.wait_ge(ot_turned, s + 1)
                o = MISC.rearrange("p (t h d) -> p t h d", t=TB, h=G)
                dve.reciprocal(rden[:, :, :], o[:, :, :, DK]).then_inc(rden_ready, 1)
                dve.wait_ge(rden_ready, s + 1)
                to = BIG[:, bass.ds(24576 + n * (TB * D), TB * D)].rearrange("p (t n) -> p t n", t=TB)
                dve.tensor_tensor(to[:, :, g * G * DK:(g + 1) * G * DK].rearrange("p t (h d) -> p t h d", h=G),
                                  o[:, :, :, 0:DK], rden[:, :, :].unsqueeze(3).to_broadcast([P, TB, G, DK]),
                                  ALU.mult).then_inc(o_ready, 1)

            def attention(layer):
                dve.memset(PV, 0.0).then_inc(pv_zero, 1)
                n0 = B * layer
                for g in range(2):
                    maxima(n0, g, range(16))
                split_max(n0, 0)

                def batch(n, first, last):
                    for g in range(NG):
                        if not (last and g == NG - 1):
                            split_max(n + (g + 1) // NG, (g + 1) % NG)
                        ahead = not (last and g >= 2)
                        if ahead:
                            maxima(n + (g + 2) // NG, (g + 2) % NG, range(12))
                        if not (first and g == 0):
                            m = n if g else n - 1
                            normalise(NG * n + g - 1, m - n0, (g + 3) % NG)
                        if ahead:
                            maxima(n + (g + 2) // NG, (g + 2) % NG, range(12, 16))
                over_batches(dve, layer, batch)
                normalise(NG * (n0 + B) - 1, B - 1, NG - 1)

            def tail(layer):
                for i in range(NT):
                    t = NT * layer + i
                    dve.wait_ge(out_done, t + 1)
                    if layer:
                        dve.wait_ge(biased, NT + i + 1)
                    dve.scalar_tensor_tensor(X[:, i, :], bank(2 + i % 2)[:, 0:D], tg[:, layer:layer + 1], X[:, i, :],
                                             ALU.mult, ALU.add).then_inc(x_upd, 1)

            def weight_scales():
                dve.wait_ge(qw_in, 48)
                for k in range(3):
                    w, wb, nb = quant_weight(k)
                    link(dve, dve.tensor_reduce(ws[:, k, 0, 0:nb], wb, AX.X, ALU.max, apply_absolute_value=True))
                    link(dve, dve.tensor_scalar(ws[:, k, 1, 0:nb], ws[:, k, 0, 0:nb], 1.0 / 7.0, TINY, ALU.mult, ALU.max))
                    dve.reciprocal(ws[:, k, 2, 0:nb], ws[:, k, 1, 0:nb]).then_inc(w_scales, 1)

            routing()
            norm(0, NT)
            prep(0)
            attention(0)
            tail(0)
            dve.wait_ge(x_upd, NT)
            norm(1, ROUTED)
            dve.wait_ge(tg_ready, 1)
            dve.tensor_scalar(bias_row[:, :], bias_row[:, :], tg[:, 2:3], None, ALU.mult).then_inc(tg_bias, 1)

            def turned(m, q):
                for half in range(2):
                    dve.wait_ge(ht_turned, 2 * (2 * m + q) + half + 1)
                    dve.tensor_copy(M["ht"][:, q, 4 * half:4 * half + 4, :].rearrange("p c n -> p (c n)"),
                                    bank(2 + half)).then_inc(ht_ready, 1)

            def slots_turned(m, q, ahead):
                dve.wait_ge(xs_turned, 2 * m + q + ahead + 1)
                dve.tensor_copy(M["xst"][:, (q + ahead) % 2, :],
                                bank(6 + (q + ahead) % 2)[:, 0:D]).then_inc(xst_ready, 1)

            slots_turned(0, 0, 0)
            slots_turned(0, 1, 0)

            def expert_tile(m, q, t):
                turned(m, q)
                if t is None or t + 2 < SLOT_TILES:
                    slots_turned(m, q, 2)
            over_tiles(dve, expert_tile)

            for i in range(ROUTED):
                dve.wait_ge(gathered[i], 16 * TOPK)
                dve.wait_ge(biased, NT)
                y0, y1 = M["got"][:, 0, i, :], M["got"][:, 1, i, :]
                link(dve, dve.tensor_scalar(y0, y0, ew[:, i, 0:1], None, ALU.mult))
                link(dve, dve.scalar_tensor_tensor(y0, y1, ew[:, i, 1:2], y0, ALU.mult, ALU.add))
                dve.scalar_tensor_tensor(X[:, i, :], y0, tg[:, 2:3], X[:, i, :],
                                         ALU.mult, ALU.add).then_inc(combined, 1)
            dve.wait_ge(combined, ROUTED)
            norm(2, NT)
            dve.wait_ge(aw_in, 64 * 2)
            dve.tensor_scalar(bias_row[:, :], TGBO, tg[:, 1:2], None, ALU.mult).then_inc(tg_bias, 1)
            prep(1)
            weight_scales()
            attention(1)
            tail(1)
            dve.wait_ge(x_upd, 2 * NT)
            norm(3, NT)

            def spread_max(r, count):
                dve.wait_ge(max_col_turned, r + 1)
                dve.tensor_reduce(one[0:1, 0:count], bank(5)[0:1, 0:count * P].rearrange("p (k n) -> p k n", k=count),
                                  AX.X, ALU.max).then_inc(max_one, 1)
                dve.wait_ge(max_spread, r + 1)
                link(dve, dve.tensor_copy(sc[:, A_MAX:A_MAX + count], bank(4)[:, 0:count]))

            dve.wait_ge(xn_ready, NORM_BASE[3] + NT)
            for i in range(4):
                last = dve.tensor_reduce(cmx[:, i:i + 1], Pt[:, i * 1024:(i + 1) * 1024], AX.X, ALU.max,
                                         apply_absolute_value=True)
            link(dve, last)
            dve.tensor_reduce(cm[:, 0:1], cmx[:, 0:4], AX.X, ALU.max).then_inc(col_max, 1)
            spread_max(0, 1)
            link(dve, dve.tensor_scalar(sc[:, S_X:S_X + 1], sc[:, A_MAX:A_MAX + 1], 1.0 / QMAX, TINY, ALU.mult, ALU.max))
            dve.reciprocal(sc[:, F_X:F_X + 1], sc[:, S_X:S_X + 1]).then_inc(scales, 1)
            for i in range(B):
                dve.wait_ge(q_magic, i + 1)
                ap = Q["xt"][:, :, i * S:(i + 1) * S]
                dve.tensor_scalar(ap, ap, MAGIC, None, ALU.subtract).then_inc(nx_ready, 1)

            for k in range(2 * QC * B):
                dve.wait_ge(ug_copied, k + 1)
                last = dve.tensor_reduce(cmx[:, (k % 2) * 32 + k // 2:(k % 2) * 32 + k // 2 + 1], ug_place(k), AX.X,
                                         ALU.max, apply_absolute_value=True)
            link(dve, last)
            dve.tensor_reduce(cm[:, 0:2], cmx[:, :].rearrange("p (w k) -> p w k", w=2)[:, :, 0:QC * B], AX.X,
                              ALU.max).then_inc(col_max, 1)
            spread_max(1, 2)
            for w, (s_, f_) in enumerate(((S_U, F_U), (S_G, F_G))):
                link(dve, dve.tensor_tensor(sc[:, T0:T0 + 1], sc[:, A_MAX + w:A_MAX + w + 1], sc[:, S_X:S_X + 1], ALU.mult))
                link(dve, dve.tensor_scalar(sc[:, s_:s_ + 1], sc[:, T0:T0 + 1], 1.0 / QMAX, TINY, ALU.mult, ALU.max))
                link(dve, dve.reciprocal(sc[:, T1:T1 + 1], sc[:, s_:s_ + 1]))
                last = dve.tensor_tensor(sc[:, f_:f_ + 1], sc[:, T1:T1 + 1], sc[:, S_X:S_X + 1], ALU.mult)
                if w == 0:
                    link(dve, last)
            last.then_inc(scales, 1)

            for i in range(PIECES + 1):
                if i < PIECES:
                    dve.wait_ge(sig_done, i + 1)
                    sg = Q["sig"][:, i % 2, :]
                    dve.tensor_scalar(sg, sg, SIG_MAX, SIG_MAGIC, ALU.min, ALU.add).then_inc(sig_round, 1)
                if i > 0:
                    dve.wait_ge(prod_done, i)
                    last = dve.tensor_reduce(cmx[:, i - 1:i], piece(Q["gate"], i - 1), AX.X, ALU.max,
                                             apply_absolute_value=True)
                if i < PIECES:
                    dve.wait_ge(sig_round, i + 1)
                    ap = piece(Q["gate"], i)
                    dve.scalar_tensor_tensor(ap, sg, SIG_MAGIC, ap, ALU.subtract, ALU.mult).then_inc(prod_done, 1)
            link(dve, last)
            dve.tensor_reduce(cm[:, 0:1], cmx[:, 0:PIECES], AX.X, ALU.max).then_inc(col_max, 1)
            spread_max(2, 1)

            def next_scale(unit, s_, f_, r):
                link(dve, dve.tensor_tensor(sc[:, T0:T0 + 1], sc[:, A_MAX:A_MAX + 1], unit, ALU.mult))
                link(dve, dve.tensor_scalar(sc[:, s_:s_ + 1], sc[:, T0:T0 + 1], 1.0 / QMAX, TINY, ALU.mult, ALU.max))
                link(dve, dve.reciprocal(sc[:, T1:T1 + 1], sc[:, s_:s_ + 1]))
                dve.tensor_tensor(sc[:, f_:f_ + 1], sc[:, T1:T1 + 1], unit, ALU.mult).then_inc(scales, 1)

            next_scale(sc[:, S_G:S_G + 1], S_2, F_2, 3)
            for i in range(PIECES + 1):
                if i < PIECES:
                    ap = piece(Q["gate"], i)
                    dve.wait_ge(gate_scaled, i + 1)
                    dve.wait_ge(up_int, i + 1)
                    dve.scalar_tensor_tensor(ap, ap, MAGIC, piece(Q["up"], i), ALU.subtract,
                                             ALU.mult).then_inc(prod_done, 1)
                if i > 0:
                    dve.wait_ge(prod_done, PIECES + i)
                    last = dve.tensor_reduce(cmx[:, i - 1:i], piece(Q["gate"], i - 1), AX.X, ALU.max,
                                             apply_absolute_value=True)
            link(dve, last)
            dve.tensor_reduce(cm[:, 0:1], cmx[:, 0:PIECES], AX.X, ALU.max).then_inc(col_max, 1)
            spread_max(3, 1)
            link(dve, dve.tensor_tensor(sc[:, UNIT:UNIT + 1], sc[:, S_2:S_2 + 1], sc[:, S_U:S_U + 1], ALU.mult))
            next_scale(sc[:, UNIT:UNIT + 1], S_O, F_O, 4)
            link(dve, dve.tensor_tensor(sc[:, OUT_F:OUT_F + 1], sc[:, S_O:S_O + 1], tg[:, 3:4], ALU.mult))
            for b in range(B + 1):
                if b < B:
                    for part in range(2):
                        ap = some_gate(b, part)
                        dve.wait_ge(o_scaled, 2 * b + part + 1)
                        dve.tensor_scalar(ap, ap, MAGIC, None, ALU.subtract).then_inc(o_int, 1)
                if b > 0:
                    for i in range(TB * (b - 1), TB * b):
                        dve.wait_ge(dn_done, i + 1)
                        dve.scalar_tensor_tensor(X[:, i, :], bank(i % 4)[:, 0:D], sc[:, OUT_F:OUT_F + 1], X[:, i, :],
                                                 ALU.mult, ALU.add).then_inc(y_final, 1)

        @block.tensor
        def _(pe):
            pe.wait_ge(consts, 3)
            pe.wait_ge(gp_consts, 8)
            pe.wait_ge(onehots, 1)
            pe.matmul(bank(0)[:, 0:ROUTED * E], upper[:, :], slots[:, :, :].rearrange("p i e -> p (i e)"),
                      start=True, stop=True)
            pe.matmul(bank(1)[:, 0:ROUTED * E], ones[:, :], slots[:, :, :].rearrange("p i e -> p (i e)"),
                      start=True, stop=True).then_inc(ranks, 1)
            pe.wait_ge(routed, 1)

            def prep(layer):
                pe.wait_ge(aw_in, 64 * (layer + 1))
                pe.wait_ge(ct_in, 16 * KC * (layer + 1))
                for b in range(B):
                    n = B * layer + b
                    pe.wait_ge(xn_ready, NORM_BASE[2 * layer] + TB * (b + 1))
                    wait(pe, xnt_evac, KC * n)
                    for c in range(KC):
                        for t in range(TB):
                            last = pe.transpose(bank(c)[:, t * P:(t + 1) * P], XN[:, TB * b + t, c * P:(c + 1) * P],
                                                identf[:, :])
                        last.then_inc(tr_done, 1)
                    for j in range(4):
                        which, c = 1 - j // 2, j % 2
                        if j == 2:
                            for t in range(TB):
                                wait(pe, v_taken, 2 * (n - 1) + t // 2 + 1 if n > 0 else 0)
                                for kc in range(KC):
                                    last = pe.matmul(bank(6 + t // 2)[:, (t % 2) * D:(t % 2) * D + D],
                                                     CT[:, kc, (TB * b + t) * P:(TB * b + t + 1) * P],
                                                     AW[:, 2 * KC + kc, :], start=(kc == 0), stop=(kc == KC - 1))
                                if t % 2:
                                    last.then_inc(v_done, 1)
                            pe.wait_ge(xnt_evac, KC * (n + 1))
                        wait(pe, r_done, 4 * (n - 1) + j + 1 if n > 0 else 0)
                        for kc in range(KC):
                            rhs = CT[:, kc, b * S:(b + 1) * S] if which else XNT[:, kc, :]
                            last = pe.matmul(bank(2 + j), AW[:, which * KC + kc, c * P:(c + 1) * P], rhs,
                                             start=(kc == 0), stop=(kc == KC - 1))
                        last.then_inc(qk_done, 1)

            def max_scores(n, g, some):
                for i in some:
                    h, qc = i // TB, i % TB
                    if i == 0:
                        pe.wait_ge(q_stack[g], 96 * (n + 1))
                    wait(pe, max_taken, 16 * (NG * n + g) + i - 1)
                    pe.matmul(SM[i % 2], QS[0:ROWS, g, h, qc * P:(qc + 1) * P], KS[0:ROWS, g, h, :],
                              start=True, stop=True).then_inc(max_done, 1)

            def turn_max(n, g):
                s = NG * n + g
                pe.wait_ge(max_parts, s + 1)
                wait(pe, o_ready, s - 2)
                for t in range(TB):
                    last = pe.transpose(MISC[0:PARTS * G, t * P // 2:(t + 1) * P // 2].bitcast(BF16),
                                        MP[:, t, :, :].rearrange("p r h -> p (r h)"), identb[:, :])
                last.then_inc(max_turned, 1)

            def key_scores(s, n, g, kc, half):
                if kc == 0 and half == 0:
                    pe.wait_ge(max_rows[g], 16 * (n + 1))
                wait(pe, exp_done, 2 * (4 * s + kc) + half - 1)
                for i in range(2):
                    h = 2 * half + i
                    last = pe.matmul(ST[half][:, i * S:(i + 1) * S], KS[0:ROWS + PARTS, g, h, kc * P:(kc + 1) * P],
                                     QS[0:ROWS + PARTS, g, h, :], start=True, stop=True)
                last.then_inc(st_done, 1)

            def values(s, n, g, kc, half):
                pe.wait_ge(exp_done, 2 * (4 * s + kc) + half + 1)
                if kc == 0 and half == 0:
                    pe.wait_ge(v_stack[g], 16 * (n + 1))
                    wait(pe, ot_ready, s)
                for h in (2 * half, 2 * half + 1):
                    last = pe.matmul(PV[32 * h:32 * h + DK + 1, :], VS[:, g, kc, h, :],
                                     PP[:, 2 * (kc % 2) + h // 2, h % 2, :], start=(kc == 0), stop=(kc == TB - 1),
                                     tile_position=(0, 32 * h))
                if half == 1:
                    last.then_inc(pv_done, 1)

            def turn_outputs(s, q, max_too):
                pe.wait_ge(ot_ready, s + 1)
                if max_too:
                    pe.wait_ge(max_copied, s + 3)
                else:
                    pe.wait_ge(o_ready, s)
                for t in range(TB):
                    last = pe.transpose(MISC[:, t * P:(t + 1) * P], OT[:, q, t * P:(t + 1) * P], identf[:, :])
                last.then_inc(ot_turned, 1)

            def attention(layer):
                n0 = B * layer
                pe.wait_ge(ones_rows, layer + 1)
                pe.wait_ge(pv_zero, layer + 1)
                pe.wait_ge(r_done, 4 * B * (layer + 1))
                pe.wait_ge(v_taken, 2 * B * (layer + 1))
                for g in range(2):
                    max_scores(n0, g, range(16))
                turn_max(n0, 0)

                def batch(n, first, last):
                    for g in range(NG):
                        s = NG * n + g
                        for kc in range(TB):
                            for i in range(4):
                                if i < 2:
                                    key_scores(s, n, g, kc, i)
                                elif kc > 0:
                                    values(s, n, g, kc - 1, i - 2)
                                elif g > 0:
                                    values(s - 1, n, g - 1, TB - 1, i - 2)
                                elif not first:
                                    values(s - 1, n - 1, NG - 1, TB - 1, i - 2)
                                if not (last and g >= 2):
                                    max_scores(n + (g + 2) // NG, (g + 2) % NG, range(4 * kc + i, 4 * kc + i + 1))
                            if kc == 1 and not (last and g == NG - 1):
                                turn_max(n + (g + 1) // NG, (g + 1) % NG)
                            if kc == 2 and not (first and g == 0):
                                turn_outputs(s - 1, (g + 1) % 2, not (last and g == NG - 1))
                over_batches(pe, layer, batch)
                n = n0 + B - 1
                s = NG * n + NG - 1
                for half in range(2):
                    values(s, n, NG - 1, TB - 1, half)
                turn_outputs(s, 1, False)

            def tail(layer):
                pe.wait_ge(wo_in, 16 * (layer + 1))
                pe.wait_ge(o_ready, NG * B * (layer + 1))
                pe.wait_ge(exp_done, 8 * NG * B * (layer + 1))
                for i in range(NT + 1):
                    t = NT * layer + i
                    if i < NT:
                        if i >= 2:
                            pe.wait_ge(on_evac, t - 1)
                        for c in range(KC):
                            last = pe.transpose(bank(i % 2)[:, c * P:(c + 1) * P], OALL[:, i, c * P:(c + 1) * P],
                                                identf[:, :])
                        last.then_inc(tro_done, 1)
                    if i > 0:
                        j = i - 1
                        pe.wait_ge(on_evac, t)
                        if j >= 2:
                            pe.wait_ge(x_upd, t - 2)
                        for c in range(KC):
                            last = pe.matmul(bank(2 + j % 2)[:, 0:D], OT[:, j % 2, c * P:(c + 1) * P], WO[:, c, :],
                                             start=(c == 0), stop=(c == KC - 1))
                        last.then_inc(out_done, 1)

            prep(0)
            attention(0)
            tail(0)

            def turn_slots(m, q, ahead):
                p = (q + ahead) % 2
                pe.wait_ge(xs_in[p], 16 * (m + (q + ahead) // 2 + 1))
                wait(pe, xst_ready, 2 * m + q + ahead - 1)
                for c in range(KC):
                    last = pe.transpose(bank(6 + p)[:, c * P:(c + 1) * P], M["xs"][:, p, c * P:(c + 1) * P], identf[:, :])
                last.then_inc(xs_turned, 1)

            def expert_of(m, q, ahead):
                t = 2 * m + q + ahead
                return pe.value_load(expert_i[0:1, bass.ds(t, 1)], min_val=0, max_val=E - 1)

            def hidden(m, q, ahead, e):
                t = 2 * m + q + ahead
                p = (q + ahead) % 2
                pe.wait_ge(xst_ready, t + 1)
                for half in range(2):
                    wait(pe, gelu_done, 2 * t + half - 1)
                    for c in range(KC):
                        last = pe.matmul(bank(half), M["xst"][:, p, c * P:(c + 1) * P],
                                         W1[:, bass.ds(e * (KC * FF) + (c * FF + half * 512), 512)],
                                         start=(c == 0), stop=(c == KC - 1))
                    last.then_inc(h_done, 1)

            def expert_tile(m, q, t):
                n = 2 * m + q
                for half in range(2):
                    pe.wait_ge(gelu_done, 2 * n + half + 1)
                    wait(pe, ht_ready, 2 * n + half - 1)
                    for c in range(4 * half, 4 * half + 4):
                        last = pe.transpose(bank(2 + half)[:, (c % 4) * P:(c % 4 + 1) * P],
                                            M["h"][:, q, c * P:(c + 1) * P], identf[:, :])
                    last.then_inc(ht_turned, 1)
                if t is None or t + 1 < SLOT_TILES:
                    hidden(m, q, 1, expert_of(m, q, 1))
                if t is None or t + 2 < SLOT_TILES:
                    turn_slots(m, q, 2)
                e = expert_of(m, q, 0)
                pe.wait_ge(ht_ready, 2 * n + 2)
                wait(pe, ys_ready, n - 1)
                for c in range(FC):
                    last = pe.matmul(bank(4 + q)[:, 0:D], M["ht"][:, q, c, :],
                                     W2[:, bass.ds(e * (FC * D) + c * D, D)], start=(c == 0), stop=(c == FC - 1))
                last.then_inc(y_done, 1)

            pe.wait_ge(x_upd, NT)
            turn_slots(0, 0, 0)
            turn_slots(0, 1, 0)
            pe.wait_ge(w1_in, 16 * E)
            hidden(0, 0, 0, expert_of(0, 0, 0))
            pe.wait_ge(w2_in, 16 * E)
            expert_tile(0, 0, 0)
            expert_tile(0, 1, 1)
            with pe.Fori(1, (SLOT_TILES - 3) // 2) as m:
                for q in range(2):
                    expert_tile(m, q, None)
            for t in range(SLOT_TILES - 3, SLOT_TILES):
                expert_tile(t // 2, t % 2, t)

            pe.wait_ge(ys_ready, SLOT_TILES)
            prep(1)
            attention(1)
            tail(1)

            for k in range(3):
                pe.wait_ge(qw_ready, k + 1)
                chunks = QC if k < 2 else KC
                w = Q["raw"][:, k * QC * D:(k + 1) * QC * D].rearrange("p (c n) -> p c n", c=chunks)
                for a in range(12):
                    ci, co = a // chunks, a % chunks
                    if a % 4 == 0:
                        wait(pe, qwt_ready, 3 * k + a // 4 - 2)
                    last = pe.transpose(bank(4 + a // 4)[:, (a % 4) * P:(a % 4 + 1) * P], w[:, co, ci * P:(ci + 1) * P],
                                        identf[:, :])
                    if a % 4 == 3:
                        last.then_inc(qwt_turned, 1)
            pe.wait_ge(x_upd, 2 * NT)
            for i in range(B):
                pe.wait_ge(xn_ready, NORM_BASE[3] + TB * (i + 1))
                for c in range(KC):
                    wait(pe, nxt_ready, 2 * (i - 2) + c + 1 if i > 1 else 0)
                    for t in range(TB):
                        last = pe.transpose(bank(i % 2 * 2 + c)[:, t * P:(t + 1) * P],
                                            XN[:, TB * i + t, c * P:(c + 1) * P], identf[:, :])
                    last.then_inc(nx_turned, 1)

            def spread_max(r, count):
                pe.wait_ge(col_max, r + 1)
                for k in range(count):
                    last = pe.transpose(bank(5)[0:1, k * P:(k + 1) * P], cm[:, k:k + 1], identf[:, :])
                last.then_inc(max_col_turned, 1)
                pe.wait_ge(max_one, r + 1)
                pe.matmul(bank(4)[:, 0:count], ones[0:1, :], one[0:1, 0:count], start=True, stop=True
                          ).then_inc(max_spread, 1)

            pe.wait_ge(qwt_ready, 9)
            spread_max(0, 1)
            pe.wait_ge(nxt_ready, 2 * B)
            wt = Q["wt"]
            for k in range(2 * QC * B):
                b, c, w = k // (2 * QC), k // 2 % QC, k % 2
                pe.wait_ge(nx_ready, b + 1)
                if k >= 4:
                    pe.wait_ge(ug_copied, k - 3)
                for kc in range(KC):
                    at = (1 - w) * QC * D + kc * QF + c * P
                    last = pe.matmul(bank(k % 4), wt[:, at:at + P], Q["xt"][:, kc, b * S:(b + 1) * S],
                                     start=(kc == 0), stop=(kc == KC - 1))
                last.then_inc(ug_done, 1)
            spread_max(1, 2)
            spread_max(2, 1)
            spread_max(3, 1)
            for i in range(NT):
                pe.wait_ge(o_int, 2 * (i // TB + 1))
                if i >= 4:
                    pe.wait_ge(y_final, i - 3)
                for c in range(QC):
                    at = 2 * QC * D + c * D
                    last = pe.matmul(bank(i % 4)[:, 0:D], Q["gate"][:, c, i * P:(i + 1) * P], wt[:, at:at + D],
                                     start=(c == 0), stop=(c == QC - 1))
                last.then_inc(dn_done, 1)


_NAMES = ("x", "ctx_t", "gates", "attn_w", "attn_bqk", "attn_bvo", "expert_indices", "expert_weights", "moe_bias", "w1", "w2",
          "w_gate", "w_up", "w_down")


def layout(inputs):
    a = {k: np.ascontiguousarray(v) for k, v in inputs.items()}

    def by_step(w):
        return np.ascontiguousarray(w.reshape(w.shape[:-1] + (NG, G, DK)).swapaxes(-1, -2)).reshape(w.shape)

    zero = np.zeros(D, a["x"].dtype)
    return {
        "x": a["x"],
        "ctx_t": np.ascontiguousarray(a["ctx_1024"].reshape(B * S, D).T),
        "gates": np.concatenate([a["g_xattn"], a["g_ffn"]]),
        "attn_w": np.stack([
            np.stack([by_step(a["L0_xattn_W_q"].T), by_step(a["L0_xattn_W_k"].T), a["L0_xattn_W_v"].T,
                      a["L0_xattn_W_o"].T]),
            np.stack([by_step(a["L1_xattn_Wq"]), by_step(a["L1_xattn_Wk"]), a["L1_xattn_Wv"], a["L1_xattn_Wo"]])]),
        "attn_bqk": np.stack([np.stack([zero] * 2).reshape(2 * KC, P).T, np.stack(
            [by_step(a["L1_xattn_bq"]), by_step(a["L1_xattn_bk"])]).reshape(2 * KC, P).T]),
        "attn_bvo": np.stack([np.stack([zero] * 2), np.stack([a["L1_xattn_bv"], a["L1_xattn_bo"]])]),
        "expert_indices": a["L0_ffn_expert_indices"],
        "expert_weights": a["L0_ffn_expert_weights"],
        "moe_bias": a["L0_ffn_bias"],
        "w1": a["L0_ffn_w1"],
        "w2": a["L0_ffn_w2"],
        "w_gate": a["L1_ffn_w_gate"],
        "w_up": a["L1_ffn_w_up"],
        "w_down": a["L1_ffn_w_down"],
    }


def kernel(**inputs):
    import concourse.bacc as bacc
    from concourse.bass_utils import run_bass_kernel_spmd

    nc = bacc.Bacc("TRN2", target_bir_lowering=False, num_devices=1)
    arrays = {f"in_{k}": v for k, v in layout(inputs).items()}
    io = {k: nc.dram_tensor(f"in_{k}", arrays[f"in_{k}"].shape, mybir.dt.from_np(arrays[f"in_{k}"].dtype),
                            kind="ExternalInput").ap() for k in _NAMES}
    out = nc.dram_tensor("out_x", (B, S, D), F32, kind="ExternalOutput").ap()
    build_program(nc, io, out)
    result = run_bass_kernel_spmd(nc, [arrays], core_ids=[0])
    return result.results[0]["out_x"]
```

```python
from contextlib import ExitStack

import numpy as np

import concourse.bass as bass
from concourse import mybir

F32 = mybir.dt.float32
BF16 = mybir.dt.bfloat16
I32 = mybir.dt.int32
U32 = mybir.dt.uint32
ALU = mybir.AluOpType
ACT = mybir.ActivationFunctionType
AX = mybir.AxisListType

P = 128
D = 256
KC = D // P
B, S = 4, 512
NT = B * S // P
TB = S // P
H, DK = 16, 16
G = 4
NG = H // G
E = 8
FF = 1024
FC = FF // P
ROUTED = 8
TOPK = 2
SLOT_TILES = ROUTED * TOPK + E - 1
QF = 768
QC = QF // P
BLOCK = 32
EPS = 1e-5
PARTS = 3
ROWS = 6 * DK
RUNS = ((0, 3, 0), (3, 2, 1), (5, 1, 2))
MAGIC = 1.5 * 2.0 ** 23
QMAX = 32767.0
TINY = 1e-12
A_MAX, S_X, F_X, S_U, F_U, S_G, F_G, S_2, F_2, S_O, F_O, OUT_F, UNIT, T0, T1 = (0, *range(2, 16))
PIECES = QC * 2
BANKS = QC * B
AHEAD = 2
SIGS = 4
SIG_MAX = 65535.0 / 65536.0
SIG_MAGIC = 1.5 * 2.0 ** 23 / 65536.0


def build_program(nc, io, out):
    with ExitStack() as ctx:
        def sb(name, shape, dt=F32):
            return ctx.enter_context(nc.sbuf_tensor(name, shape, dt))

        def sem(name):
            return ctx.enter_context(nc.semaphore(name))

        PS = ctx.enter_context(nc.psum_tensor("PS", [P, 8, 512], F32))
        BIG = sb("BIG", [P, 32768])
        KSt = sb("KSt", [P, 4 * G * S], BF16)
        Pt = sb("Pt", [P, 4096])
        X = sb("X", [P, NT, D])
        VS = sb("VS", [P, NG, TB, G, DK + 1])
        OT = sb("OT", [P, 2, S])
        TT = sb("TT", [P, 2, D])
        WO = sb("WO", [P, KC, D])
        identf = sb("identf", [P, P])
        identb = sb("identb", [P, P], BF16)
        upper = sb("upper", [P, P])
        ones = sb("ones", [P, P])
        gates = sb("gates", [P, 4])
        tg = sb("tg", [P, 4])
        bias_row = sb("bias_row", [P, D])
        stats = sb("stats", [P, NT, 6])
        mv = sb("mv", [P, NT, 2])
        ve = sb("ve", [P, NT])
        sd = sb("sd", [P, NT])
        nw1 = sb("nw1", [P, NT])
        nw2 = sb("nw2", [P, NT])
        rstd = sb("rstd", [P, NT])
        MX = sb("MX", [P, 2, TB, G])
        MP = sb("MP", [P, TB, PARTS, G], BF16)
        MD = sb("MD", [P, TB, G])
        MR = sb("MR", [PARTS * G, 2, S], BF16)
        rden = sb("rden", [P, TB, G])
        pos_i = sb("pos_i", [P, TOPK, ROUTED], U32)
        ew = sb("ew", [P, ROUTED, TOPK])
        expert_i = sb("expert_i", [1, SLOT_TILES + 1], I32)
        zrow = sb("zrow", [P, D])
        magic = sb("magic", [P, 2])
        idx = sb("idx", [P, ROUTED, TOPK], I32)
        idxf = sb("idxf", [P, ROUTED, TOPK])
        hot = sb("hot", [P, ROUTED, TOPK, E])
        slots = sb("slots", [P, ROUTED, E])
        totals = sb("totals", [P, ROUTED, E])
        before = sb("before", [P, ROUTED, E])
        place = sb("place", [P, ROUTED, E])
        picked = sb("picked", [P, ROUTED, E])
        posf = sb("posf", [P, TOPK, ROUTED])
        rt = [sb(f"rt{i}", [P, E]) for i in range(4)]
        rti = [sb(f"rti{i}", [P, E], I32) for i in range(2)]
        upto = sb("upto", [P, E])
        ex = [sb(f"ex{i}", [1, SLOT_TILES + 1]) for i in range(2)]
        tile_no = sb("tile_no", [P, SLOT_TILES + 1], I32)
        tile_f = sb("tile_f", [P, SLOT_TILES + 1])
        sc = sb("sc", [P, 16])
        cm = sb("cm", [P, 2])
        cmx = sb("cmx", [P, 64])
        one = sb("one", [1, 2])
        ws = sb("ws", [P, 3, 3, QC * D // BLOCK])

        W1 = BIG[:, 0:E * KC * FF]
        W2 = BIG[:, E * KC * FF:2 * E * KC * FF]
        QS = BIG[:, 28672:32768].bitcast(BF16).rearrange("p (g h t) -> p g h t", g=NG, h=G)
        KS = KSt[:, :].rearrange("p (g h t) -> p g h t", g=NG, h=G)
        OALL = BIG[:, 24576:28672].rearrange("p (i n) -> p i n", i=NT)
        at = 0
        CT = BIG[:, at:at + 4096].rearrange("p (c t) -> p c t", c=KC); at += 4096
        XNT = BIG[:, at:at + 1024].rearrange("p (c t) -> p c t", c=KC); at += 1024
        PT = BIG[:, at:at + 3072].bitcast(BF16).rearrange("p (j r t) -> p j r t", j=4, r=PARTS); at += 3072
        VB = BIG[:, at:at + TB * H * (DK + 1)].rearrange("p (t h d) -> p t h d", t=TB, h=H); at += TB * H * (DK + 1)
        RB = BIG[:, at:at + 1024].rearrange("p (j t) -> p j t", j=2); at += 1024
        AW = BIG[:, at:at + 1536].rearrange("p (c n) -> p c n", c=3 * KC); at += 1536
        BV = BIG[:, at:at + D]; at += D
        BQK = BIG[:, at:at + 4]; at += 4
        TGBO = BIG[:, at:at + D]; at += D
        assert at <= E * KC * FF
        assert E * KC * FF <= 24576 - 3 * QC * D
        XN = Pt[:, :].rearrange("p (i n) -> p i n", i=NT)
        PP = Pt[:, :].rearrange("p (q h t) -> p q h t", q=4, h=2)

        qk_dram = nc.dram_tensor("qk_parts", (2, 2, B, PARTS, D, S), BF16).ap()
        v_dram = nc.dram_tensor("v_rows", (2, B, P, TB, H, DK + 1), F32).ap()
        ones_dram = nc.dram_tensor("ones_rows_kept", (PARTS, NG, G, S), BF16).ap()
        xs_dram = nc.dram_tensor("slot_rows", ((SLOT_TILES + 1) * P, D), F32).ap()
        ys_dram = nc.dram_tensor("slot_results", ((SLOT_TILES + 1) * P, D), F32).ap()

        x_in = [sem(f"x_in{b}") for b in range(B)]
        gates_in = sem("gates_in")
        aw_in = sem("aw_in")
        ab_in = sem("ab_in")
        wo_in = sem("wo_in")
        ct_in = [sem(f"ct_in{b}") for b in range(B)]
        ranks_taken = sem("ranks_taken")
        consts = sem("consts")
        tg_ready = sem("tg_ready")
        ln_var = sem("ln_var")
        ln_sd = sem("ln_sd")
        xn_ready = sem("xn_ready")
        dve_link = sem("dve_link")
        tr_done = sem("tr_done")
        xnt_evac = sem("xnt_evac")
        qk_done = sem("qk_done")
        hi_done = sem("hi_done")
        r_done = sem("r_done")
        mid_done = sem("mid_done")
        lo_done = sem("lo_done")
        part_out = [sem(f"part_out{j}") for j in range(4)]
        v_done = sem("v_done")
        v_taken = sem("v_taken")
        v_out = sem("v_out")
        q_stack = [sem(f"q_stack{g}") for g in range(NG)]
        v_stack = [sem(f"v_stack{g}") for g in range(NG)]
        max_done = sem("max_done")
        max_taken = sem("max_taken")
        max_link = sem("max_link")
        max_parts = sem("max_parts")
        max_turned = sem("max_turned")
        max_copied = sem("max_copied")
        max_rows = [sem(f"max_rows{g}") for g in range(NG)]
        st_done = sem("st_done")
        exp_done = sem("exp_done")
        pv_done = sem("pv_done")
        ot_ready = sem("ot_ready")
        ot_turned = sem("ot_turned")
        rden_ready = sem("rden_ready")
        o_ready = sem("o_ready")
        pv_zero = sem("pv_zero")
        tro_done = sem("tro_done")
        on_evac = sem("on_evac")
        out_done = sem("out_done")
        x_upd = sem("x_upd")
        biased = sem("biased")
        idx_in = sem("idx_in")
        ew_in = sem("ew_in")
        gp_consts = sem("gp_consts")
        ones_rows = sem("ones_rows")
        ones_kept = sem("ones_kept")
        ones_back = sem("ones_back")
        tg_bias = sem("tg_bias")
        gate_int = sem("gate_int")
        o_int = sem("o_int")
        onehots = sem("onehots")
        ranks = sem("ranks")
        routed = sem("routed")
        zeroed = sem("zeroed")
        scattered = sem("scattered")
        w1_in = sem("w1_in")
        w2_in = sem("w2_in")
        w2_late = sem("w2_late")
        xs_in = [sem(f"xs_in{q}") for q in range(2)]
        xs_turned = sem("xs_turned")
        xst_ready = sem("xst_ready")
        h_done = sem("h_done")
        gelu_done = sem("gelu_done")
        ht_turned = sem("ht_turned")
        ht_ready = sem("ht_ready")
        y_done = sem("y_done")
        ys_ready = sem("ys_ready")
        ys_out = [sem(f"ys_out{q}") for q in range(2)]
        gathered = [sem(f"gathered{i}") for i in range(ROUTED)]
        combined = sem("combined")
        qw_in = sem("qw_in")
        qw_ready = sem("qw_ready")
        qwt_turned = sem("qwt_turned")
        qwt_ready = sem("qwt_ready")
        col_max = sem("col_max")
        max_col_turned = sem("max_col_turned")
        max_one = sem("max_one")
        max_spread = sem("max_spread")
        nx_ready = sem("nx_ready")
        nx_turned = sem("nx_turned")
        nxt_ready = sem("nxt_ready")
        ug_done = sem("ug_done")
        ug_copied = sem("ug_copied")
        scales = sem("scales")
        q_magic = sem("q_magic")
        w_scales = sem("w_scales")
        qw_step = sem("qw_step")
        up_magic = sem("up_magic")
        up_int = sem("up_int")
        gate_magic = sem("gate_magic")
        sig_round = sem("sig_round")
        gate_scaled = sem("gate_scaled")
        o_scaled = sem("o_scaled")
        sig_done = sem("sig_done")
        prod_done = sem("prod_done")
        dn_done = sem("dn_done")
        y_final = sem("y_final")
        stored = sem("stored")

        block = ctx.enter_context(nc.Block())


        def moe_buffers():
            k32 = KSt[:, :].bitcast(F32)
            return dict(
                xs=k32[:, 0:512].rearrange("p (q n) -> p q n", q=2),
                xst=k32[:, 512:1024].rearrange("p (q n) -> p q n", q=2),
                ys=k32[:, 1024:1536].rearrange("p (q n) -> p q n", q=2),
                h=Pt[:, 0:2048].rearrange("p (q n) -> p q n", q=2),
                ht=Pt[:, 2048:4096].rearrange("p (q c n) -> p q c n", q=2, c=FC),
                got=BIG[:, 24576:28672].rearrange("p (k i n) -> p k i n", k=TOPK, i=ROUTED),
            )

        def quant_buffers():
            return dict(
                raw=BIG[:, 24576 - 3 * QC * D:24576],
                wt=BIG[:, 0:3 * QC * D],
                up=BIG[:, 16896:29184].rearrange("p (c t) -> p c t", c=QC),
                gate=BIG[:, 4608:16896].rearrange("p (c t) -> p c t", c=QC),
                xt=KSt[:, :].bitcast(F32).rearrange("p (c t) -> p c t", c=KC),
                sig=Pt[:, :].rearrange("p (q n) -> p q n", q=SIGS),
            )

        def quant_weight(k):
            w = Q["raw"][:, k * QC * D:(k + 1) * QC * D]
            return w, w.rearrange("p (b n) -> p b n", n=BLOCK), QC * D // BLOCK

        def some_gate(b, part):
            return Q["gate"][:, part * (QC // 2):(part + 1) * (QC // 2), b * S:(b + 1) * S]

        M = moe_buffers()
        Q = quant_buffers()

        def bank(i, k=1):
            return PS[:, i:i + k, :].rearrange("p a b -> p (a b)")

        ST = [bank(0, 2), bank(2, 2)]
        SM = [bank(4), bank(5)]
        PV = bank(6)
        MISC = bank(7)

        linked = [0]

        def link(eng, ins):
            linked[0] += 1
            ins.then_inc(dve_link, 1)
            eng.wait_ge(dve_link, linked[0])

        def wait(eng, s, value):
            if not isinstance(value, int) or value > 0:
                eng.wait_ge(s, value)

        def over_batches(eng, layer, body):
            body(B * layer, True, False)
            with eng.Fori(B * layer + 1, B * layer + B - 1) as n:
                body(n, False, False)
            body(B * layer + B - 1, False, True)

        def over_tiles(eng, body):
            with eng.Fori(0, (SLOT_TILES - 3) // 2) as m:
                for q in range(2):
                    body(m, q, None)
            for t in range(SLOT_TILES - 3, SLOT_TILES):
                body(t // 2, t % 2, t)

        assert SLOT_TILES % 2 == 1

        def piece(ap, i):
            return ap[:, i // 2, i % 2 * 1024:i % 2 * 1024 + 1024]

        def ug_place(k):
            k, c = divmod(k, QC)
            w, b = divmod(k, B)
            return Q["up" if w else "gate"][:, c, b * S:(b + 1) * S]

        NORM_TILES = [range(NT), range(ROUTED), range(ROUTED, NT), range(TB), range(TB, ROUTED), range(NT)]
        NORM_BASE = [sum(len(t) for t in NORM_TILES[:k]) for k in range(len(NORM_TILES))]
        ORDER = [[0, 1, 2, 3], [2, 3, 0, 1]]
        assert B * TB == NT and ROUTED == 2 * TB

        def x_tile(layer, i):
            return TB * ORDER[layer][i // TB] + i % TB

        def load_w2(eng, e, done):
            eng.dma_start(W2[:, e * FC * D:(e + 1) * FC * D].rearrange("p (c n) -> p c n", c=FC),
                          io["w2"][e].rearrange("(c p) n -> p c n", p=P)).then_inc(done, 16)

        EARLY = 2 * TB

        def load_layer(eng, layer):
            eng.dma_start(AW, io["attn_w"][layer, 0:3].rearrange("w (c p) n -> p (w c) n", p=P)).then_inc(aw_in, 16)
            for b in ORDER[layer]:
                eng.dma_start(CT[:, :, b * S:(b + 1) * S],
                              io["ctx_t"][:, b * S:(b + 1) * S].rearrange("(c p) t -> p c t", p=P)).then_inc(ct_in[b], 16)
                if b == ORDER[layer][0]:
                    eng.dma_start(BQK, io["attn_bqk"][layer]).then_inc(ab_in, 16)
                    eng.dma_start(BV, io["attn_bvo"][layer, 0].partition_broadcast(P)).then_inc(ab_in, 16)
                    eng.dma_start(TGBO, io["attn_bvo"][layer, 1].partition_broadcast(P)).then_inc(ab_in, 16)

        @block.sync
        def _(sp):
            def prep(layer):
                for b in range(B):
                    n = B * layer + b
                    for j in range(4):
                        which, c = 1 - j // 2, j % 2
                        if j == 2:
                            sp.wait_ge(v_taken, 2 * (n + 1))
                            sp.dma_start(v_dram[layer, b], VB[:, :, :, :]).then_inc(v_out, 16)
                        sp.wait_ge(lo_done, 4 * n + j + 1)
                        sp.dma_start(qk_dram[layer, which, b, :, c * P:(c + 1) * P, :].rearrange("r p t -> p r t"),
                                     PT[:, j, :, :]).then_inc(part_out[j], 16)

                    if b > 0:
                        for j in range(4):
                            sp.wait_ge(part_out[j], 16 * n)
                        sp.wait_ge(v_out, 16 * n)
                        for g in ((0,), (1,), (2, 3))[b - 1]:
                            load_stack(layer, 0, g)
                            load_v(layer, 0, g)
                if layer:
                    load_quantised()

            def load_quantised():
                raw = Q["raw"]
                sp.dma_start(raw[:, 0:QC * D].rearrange("p (c n) -> p c n", c=QC),
                             io["w_gate"].rearrange("(c p) n -> p c n", p=P)).then_inc(qw_in, 16)
                sp.dma_start(raw[:, QC * D:2 * QC * D].rearrange("p (c n) -> p c n", c=QC),
                             io["w_up"].rearrange("(c p) n -> p c n", p=P)).then_inc(qw_in, 16)
                sp.dma_start(raw[:, 2 * QC * D:].rearrange("p (c n) -> p c n", c=KC),
                             io["w_down"].rearrange("(c p) n -> p c n", p=P)).then_inc(qw_in, 16)

            def load_stack(layer, b, g):
                rows = slice(g * G * DK, (g + 1) * G * DK)
                for first, k, part in RUNS:
                    dst = slice(first * DK, (first + k) * DK)
                    q = qk_dram[layer, 0, b, part, rows, :].rearrange("(d h) t -> d (h t)", h=G)
                    sp.dma_start(QS[dst, g, :, :].rearrange("p h t -> p (h t)"),
                                 q.unsqueeze(0).to_broadcast([k, DK, G * S])).then_inc(q_stack[g], 16)
                    kk = qk_dram[layer, 1, b, 0:k, rows, :].rearrange("r (d h) t -> r d (h t)", h=G)
                    sp.dma_start(KS[dst, g, :, :].rearrange("p h t -> p (h t)"), kk).then_inc(q_stack[g], 16)

            def load_v(layer, b, g):
                sp.dma_start(VS[:, g], v_dram[layer, b, :, :, G * g:G * g + G, :]).then_inc(v_stack[g], 16)

            def load_max_rows(g):
                sp.dma_start(QS[ROWS:ROWS + PARTS, g, :, :], MR[:, g % 2, :]).then_inc(max_rows[g], 16)

            def attention(layer):
                for j in range(4):
                    sp.wait_ge(part_out[j], 16 * B * (layer + 1))
                sp.wait_ge(v_out, 16 * B * (layer + 1))
                sp.wait_ge(max_copied, NG * B * layer + 1)
                load_max_rows(0)

                def batch(n, first, last):
                    for g in range(NG):
                        s = NG * n + g
                        if not (last and g == NG - 1):
                            sp.wait_ge(max_copied, s + 2)
                            load_max_rows((g + 1) % NG)
                        if not last:
                            sp.wait_ge(st_done, 8 * (s + 1))
                            load_stack(layer, n + 1 - B * layer, g)
                            sp.wait_ge(pv_done, 4 * (s + 1))
                            load_v(layer, n + 1 - B * layer, g)
                over_batches(sp, layer, batch)

            sp.dma_start(idx[:, :, :], io["expert_indices"].rearrange("(i p) k -> p i k", p=P)).then_inc(idx_in, 16)
            for b in range(B):
                sp.dma_start(X[:, TB * b:TB * b + TB, :],
                             io["x"][b].rearrange("(i p) n -> p i n", p=P)).then_inc(x_in[b], 16)
            sp.dma_start(gates[:, :], io["gates"].partition_broadcast(P)).then_inc(gates_in, 16)
            sp.dma_start(ew[:, :, :], io["expert_weights"].rearrange("(i p) k -> p i k", p=P)).then_inc(ew_in, 16)
            sp.dma_start(bias_row[:, :], io["moe_bias"].partition_broadcast(P)).then_inc(ew_in, 16)
            sp.dma_start(WO[:, :, :], io["attn_w"][0, 3].rearrange("(c p) n -> p c n", p=P)).then_inc(wo_in, 16)
            sp.wait_ge(ones_rows, 1)
            sp.dma_start(ones_dram, KS[ROWS:ROWS + PARTS, :, :, :]).then_inc(ones_kept, 16)
            prep(0)
            attention(0)

            sp.wait_ge(st_done, 8 * NG * B)
            for e in (6, 7):
                load_w2(sp, e, w2_late)
            sp.wait_ge(tro_done, NT)
            for e in (4, 5):
                load_w2(sp, e, w2_late)
            sp.wait_ge(out_done, NT)
            sp.dma_start(WO[:, :, :], io["attn_w"][1, 3].rearrange("(c p) n -> p c n", p=P)).then_inc(wo_in, 16)

            def load_slots(m, q, t):
                if t is None or t >= 2:
                    sp.wait_ge(xs_turned, 2 * m + q - 1)
                sp.dma_start(M["xs"][:, q, :], slot_tile(xs_dram, m, q)).then_inc(xs_in[q], 16)

            def store_results(m, q):
                sp.wait_ge(ys_ready, 2 * m + q + 1)
                sp.dma_start(slot_tile(ys_dram, m, q), M["ys"][:, q, :]).then_inc(ys_out[q], 16)

            def slot_tile(dram, m, q):
                return dram.rearrange("(m q p) n -> m q p n", q=2, p=P)[m, q]

            sp.wait_ge(scattered, 16 * TOPK * ROUTED)
            load_slots(0, 0, 0)
            load_slots(0, 1, 1)
            with sp.Fori(0, (SLOT_TILES - 3) // 2) as m:
                for q in range(2):
                    load_slots(m + 1, q, None)
                    store_results(m, q)
            t = SLOT_TILES - 1
            load_slots(t // 2, t % 2, t)
            for t in range(SLOT_TILES - 3, SLOT_TILES):
                if t == SLOT_TILES - 1:
                    sp.wait_ge(h_done, 2 * SLOT_TILES)
                    load_layer(sp, 1)
                store_results(t // 2, t % 2)
            sp.wait_ge(y_done, SLOT_TILES)
            sp.wait_ge(ys_out[0], 16 * ((SLOT_TILES + 1) // 2))
            sp.wait_ge(ys_out[1], 16 * (SLOT_TILES // 2))
            sp.wait_ge(ones_kept, 16)
            sp.dma_start(KS[ROWS:ROWS + PARTS, :, :, :], ones_dram).then_inc(ones_back, 16)
            prep(1)
            attention(1)

            for i in range(NT):
                sp.wait_ge(y_final, i + 1)
                sp.dma_start(out[i // TB, (i % TB) * P:(i % TB + 1) * P, :], X[:, i, :]).then_inc(stored, 16)
            sp.wait_ge(stored, 16 * NT)

        @block.gpsimd
        def _(gp):
            gp.memset(identf[:, :], 0.0).then_inc(gp_consts, 1)
            gp.memset(upper[:, :], 1.0).then_inc(gp_consts, 1)
            gp.memset(ones[:, :], 1.0).then_inc(gp_consts, 1)
            gp.memset(zrow[:, :], 0.0).then_inc(gp_consts, 1)
            gp.memset(magic[:, 0:1], MAGIC).then_inc(gp_consts, 1)
            gp.memset(magic[:, 1:2], -MAGIC).then_inc(gp_consts, 1)
            gp.memset(VB[:, :, :, DK:DK + 1], 1.0).then_inc(gp_consts, 1)
            gp.iota(tile_no[:, :], pattern=[[1, SLOT_TILES + 1]], base=0, channel_multiplier=0).then_inc(gp_consts, 1)
            gp.wait_ge(gp_consts, 8)
            gp.affine_select(out=identf[:, :], in_=identf[:, :], compare_op=ALU.not_equal, fill=1.0, base=0,
                             pattern=[[-1, P]], channel_multiplier=1).then_inc(consts, 1)
            gp.affine_select(out=upper[:, :], in_=upper[:, :], compare_op=ALU.is_gt, fill=0.0, base=0,
                             pattern=[[1, P]], channel_multiplier=-1).then_inc(consts, 1)
            gp.wait_ge(consts, 1)
            gp.tensor_copy(identb[:, :], identf[:, :]).then_inc(consts, 1)
            gp.wait_ge(consts, 3)
            gp.memset(KS[ROWS:ROWS + PARTS, :, :, :], 1.0).then_inc(ones_rows, 1)
            gp.wait_ge(ones_rows, 1)

            def gather(i):
                for k in range(TOPK):
                    gp.indirect_dma_start(out=M["got"][:, k, i, :], out_offset=None, in_=ys_dram[0:SLOT_TILES * P, :],
                                          in_offset=bass.IndirectOffsetOnAxis(ap=pos_i[:, k, i:i + 1], axis=0),
                                          ).then_inc(gathered[i], 16)

            def prep(layer):
                for n in range(B * layer, B * layer + B):
                    for j in range(4):
                        gp.wait_ge(mid_done, 4 * n + j + 1)
                        gp.tensor_tensor(PT[:, j, 2, :], RB[:, j % 2, :], PT[:, j, 1, :],
                                         ALU.subtract).then_inc(lo_done, 1)
                        if layer and n < B + 2:
                            gather(TB * (n - B) + j)

            prep(0)

            def split_max(n, g):
                zero = zrow[:, 0:TB * G].rearrange("p (t h) -> p t h", t=TB)
                s, q = NG * n + g, g % 2
                gp.wait_ge(max_taken, 16 * (s + 1))
                wait(gp, max_turned, s)
                gp.tensor_tensor(MP[:, :, 0, :], MX[:, q, :, :], zero, ALU.subtract).then_inc(max_link, 1)
                gp.wait_ge(max_link, 3 * s + 1)
                gp.tensor_tensor(MD[:, :, :], MX[:, q, :, :], MP[:, :, 0, :], ALU.subtract).then_inc(max_link, 1)
                gp.wait_ge(max_link, 3 * s + 2)
                gp.tensor_tensor(MP[:, :, 1, :], MD[:, :, :], zero, ALU.subtract).then_inc(max_link, 1)
                gp.wait_ge(max_link, 3 * s + 3)
                gp.tensor_tensor(MP[:, :, 2, :], MD[:, :, :], MP[:, :, 1, :], ALU.subtract).then_inc(max_parts, 1)

            def attention(layer, between):
                split_max(B * layer, 0)

                def batch(n, first, last):
                    for g in range(NG):
                        if not (last and g == NG - 1):
                            split_max(n + (g + 1) // NG, (g + 1) % NG)
                        between(n, g, first, last)
                over_batches(gp, layer, batch)

            def load_w1(e):
                gp.dma_start(W1[:, bass.ds(e * (KC * FF), KC * FF)].rearrange("p (c n) -> p c n", c=KC),
                             io["w1"].rearrange("e (c p) n -> e p c n", p=P)[e]).then_inc(w1_in, 16)

            def load_experts(n, g, first, last):
                if last:
                    load_w2(gp, g, w2_in)
                elif not first:
                    load_w1(NG * (n - 1) + g)
                elif g == 0:
                    gp.dma_start(xs_dram.rearrange("(t p) n -> p t n", p=P),
                                 zrow[:, :].unsqueeze(1).to_broadcast([P, SLOT_TILES + 1, D])).then_inc(zeroed, 16)

            assert B == 4 and E == 2 * NG
            gp.wait_ge(ab_in, 48)
            for j in range(4):
                gp.wait_ge(part_out[j], 16 * B)
            gp.wait_ge(v_out, 16 * B)
            gp.wait_ge(qk_done, 4 * B)
            attention(0, load_experts)
            gp.wait_ge(routed, 1)
            gp.wait_ge(zeroed, 16)
            for i in range(ROUTED):
                gp.wait_ge(xn_ready, NORM_BASE[1] + i + 1)
                for k in range(TOPK):
                    gp.indirect_dma_start(out=xs_dram[:, :],
                                          out_offset=bass.IndirectOffsetOnAxis(ap=pos_i[:, k, i:i + 1], axis=0),
                                          in_=XN[:, i, :], in_offset=None).then_inc(scattered, 16)
            gp.wait_ge(tg_bias, 1)
            for i in range(NT):
                if i == 0:
                    gp.wait_ge(x_upd, NT)
                gp.tensor_tensor(X[:, i, :], X[:, i, :], bias_row[:, :], ALU.add).then_inc(biased, 1)
            gp.wait_ge(h_done, 2 * SLOT_TILES)
            gp.memset(VB[:, :, :, DK:DK + 1], 1.0).then_inc(gp_consts, 1)
            gp.wait_ge(ys_out[0], 16 * ((SLOT_TILES + 1) // 2))
            gp.wait_ge(ys_out[1], 16 * (SLOT_TILES // 2))
            prep(1)
            gp.wait_ge(tg_bias, 2)
            gp.wait_ge(xn_ready, NORM_BASE[5])

            def add_bias(n, g, first, last):
                for i in range(TB * g, TB * g + TB) if first else ():
                    gp.tensor_tensor(X[:, i, :], X[:, i, :], bias_row[:, :], ALU.add).then_inc(biased, 1)

            attention(1, add_bias)

            steps = 0
            for k in range(3):
                gp.wait_ge(w_scales, k + 1)
                w, wb, nb = quant_weight(k)
                factor = ws[:, k, 2, 0:nb].unsqueeze(2).to_broadcast([P, nb, BLOCK])
                scale = ws[:, k, 1, 0:nb].unsqueeze(2).to_broadcast([P, nb, BLOCK])
                gp.tensor_tensor(wb, wb, factor, ALU.mult).then_inc(qw_step, 1)
                for first, op0, second, op1 in ((MAGIC, ALU.add, 1.0, ALU.mult),
                                                (MAGIC + 7.0, ALU.min, MAGIC - 8.0, ALU.max),
                                                (-MAGIC, ALU.add, 1.0, ALU.mult)):
                    steps += 1
                    gp.wait_ge(qw_step, steps)
                    gp.tensor_scalar(w, w, first, second, op0, op1).then_inc(qw_step, 1)
                steps += 1
                gp.wait_ge(qw_step, steps)
                gp.tensor_tensor(wb, wb, scale, ALU.mult).then_inc(qw_ready, 1)

            for i in range(PIECES):
                ap = piece(Q["gate"], i)
                gp.wait_ge(gate_magic, i + 1)
                gp.tensor_scalar(ap, ap, -MAGIC, 1.0, ALU.add, ALU.mult).then_inc(gate_int, 1)
            for i in range(PIECES):
                ap = piece(Q["up"], i)
                gp.wait_ge(up_magic, i + 1)
                gp.tensor_scalar(ap, ap, -MAGIC, 1.0, ALU.add, ALU.mult).then_inc(up_int, 1)

        @block.scalar
        def _(act):
            load_layer(act, 0)

            def norm(k):
                act.wait_ge(ln_var, k + 1)
                act.activation(sd[:, :], ve[:, :], ACT.Sqrt).then_inc(ln_sd, 1)

            def prep(layer, after):
                act.wait_ge(ab_in, 48 * (layer + 1))
                for n in range(B * layer, B * layer + B):
                    for j in range(4):
                        which, c = 1 - j // 2, j % 2
                        if j == 2:
                            for tc in range(KC):
                                act.wait_ge(tr_done, KC * n + tc + 1)
                                wait(act, qk_done, 4 * n)
                                act.activation(XNT[:, tc, :], bank(tc), ACT.Copy).then_inc(xnt_evac, 1)
                        act.wait_ge(qk_done, 4 * n + j + 1)
                        wait(act, part_out[j], 16 * n)
                        act.activation(PT[:, j, 0, :], bank(2 + j), ACT.Identity,
                                       bias=BQK[:, 2 * which + c:2 * which + c + 1]).then_inc(hi_done, 1)
                    after(n - B * layer)

            def copy_out(s, q):
                act.wait_ge(pv_done, 4 * (s + 1))
                wait(act, ot_turned, s - 1)
                act.activation(OT[:, q, :], PV, ACT.Copy).then_inc(ot_ready, 1)

            def copy_max(n, g):
                act.wait_ge(max_turned, NG * n + g + 1)
                wait(act, max_rows[(g + 2) % NG], 16 * (n + g // 2))
                act.activation(MR[:, g % 2, :], MISC[0:PARTS * G, 0:S // 2].bitcast(BF16),
                               ACT.Copy).then_inc(max_copied, 1)

            def attention(layer):
                copy_max(B * layer, 0)

                def batch(n, first, last):
                    for g in range(NG):
                        s = NG * n + g
                        for kc in range(TB):
                            u = 4 * s + kc
                            for half in range(2):
                                act.wait_ge(st_done, 2 * u + half + 1)
                                wait(act, pv_done, u - 1)
                                act.activation(PP[:, 2 * (kc % 2) + half, :, :].rearrange("p h t -> p (h t)"),
                                               ST[half], ACT.Exp, scale=DK ** -0.5).then_inc(exp_done, 1)
                            if kc == 0 and not (first and g == 0):
                                copy_out(s - 1, (g + 1) % 2)
                            if kc == 1 and not (last and g == NG - 1):
                                copy_max(n + (g + 1) // NG, (g + 1) % NG)
                            if last and g >= 2:
                                copy_turned(layer, TB * (g - 2) + kc, 4)
                over_batches(act, layer, batch)
                copy_out(NG * B * (layer + 1) - 1, 1)

            def copy_turned(layer, i, source):
                t = NT * layer + i
                act.wait_ge(tro_done, t + 1)
                wait(act, out_done, t - 1)
                act.activation(TT[:, i % 2, :], bank(source)[:, 0:D], ACT.Copy).then_inc(on_evac, 1)

            def tail(layer):
                for i in range(EARLY, NT):
                    copy_turned(layer, i, i % 2)

            norm(0)
            prep(0, lambda p: None)
            act.wait_ge(gates_in, 16)
            act.activation(tg[:, :], gates[:, :], ACT.Tanh).then_inc(tg_ready, 1)
            attention(0)
            norm(1)
            tail(0)

            def expert_tile(m, q, t):
                if t is None or t + 1 < SLOT_TILES:
                    gelu(m, q, 1, t)
                act.wait_ge(y_done, 2 * m + q + 1)
                act.activation(M["ys"][:, q, :], bank(4 + q)[:, 0:D], ACT.Copy).then_inc(ys_ready, 1)

            def gelu(m, q, ahead, t):
                nq = (q + ahead) % 2
                for half in range(2):
                    act.wait_ge(h_done, 2 * (2 * m + q + ahead) + half + 1)
                    act.activation(M["h"][:, nq, half * 512:half * 512 + 512], bank(half),
                                   ACT.Gelu).then_inc(gelu_done, 1)

            gelu(0, 0, 0, 0)
            expert_tile(0, 0, 0)
            expert_tile(0, 1, 1)
            with act.Fori(1, (SLOT_TILES - 3) // 2) as m:
                for q in range(2):
                    act.wait_ge(ys_out[q], 16 * m)
                    expert_tile(m, q, None)
            for t in range(SLOT_TILES - 3, SLOT_TILES):
                act.wait_ge(ys_out[t % 2], 16 * (t // 2))
                expert_tile(t // 2, t % 2, t)

            norm(2)

            def after(p):
                if p in (1, 2):
                    norm(2 + p)

            prep(1, after)
            attention(1)
            tail(1)

            def copy_weight(k, first_bank):
                for a in range(3):
                    act.wait_ge(qwt_turned, 3 * k + a + 1)
                    act.activation(Q["wt"][:, k * QC * D + a * 512:k * QC * D + a * 512 + 512], bank(first_bank + a),
                                   ACT.Copy).then_inc(qwt_ready, 1)

            copy_weight(0, 4)
            copy_weight(1, 4)
            norm(5)
            for i in range(B):
                for c in range(KC):
                    act.wait_ge(nx_turned, 2 * i + c + 1)
                    act.activation(Q["xt"][:, c, i * S:(i + 1) * S], bank(i % 2 * 2 + c), ACT.Copy).then_inc(nxt_ready, 1)
            act.wait_ge(scales, 1)
            act.wait_ge(nxt_ready, 2 * B)
            for i in range(B):
                ap = Q["xt"][:, :, i * S:(i + 1) * S]
                act.activation(ap, ap, ACT.Identity, scale=sc[:, F_X:F_X + 1], bias=magic[:, 0:1]).then_inc(q_magic, 1)

            def copy_banks(some):
                for k in some:
                    act.wait_ge(ug_done, k + 1)
                    act.activation(ug_place(k), bank(k % 4), ACT.Copy).then_inc(ug_copied, 1)

            copy_banks(range(BANKS))
            copy_weight(2, 0)
            copy_banks(range(BANKS, BANKS + AHEAD))
            act.wait_ge(scales, 2)
            for i in range(PIECES + 1):
                if i < PIECES:
                    ap = piece(Q["gate"], i)
                    act.activation(ap, ap, ACT.Identity, scale=sc[:, F_G:F_G + 1],
                                   bias=magic[:, 0:1]).then_inc(gate_magic, 1)
                    copy_banks(range(BANKS + AHEAD + 2 * i, min(BANKS + AHEAD + 2 * i + 2, 2 * BANKS)))
                if i > 0:
                    j = i - 1
                    act.wait_ge(gate_int, j + 1)
                    wait(act, prod_done, j - SIGS + 1)
                    act.activation(Q["sig"][:, j % SIGS, :], piece(Q["gate"], j), ACT.Sigmoid,
                                   scale=sc[:, S_G:S_G + 1]).then_inc(sig_done, 1)
            act.wait_ge(scales, 3)
            for i in range(PIECES):
                for which, f, done in (("up", F_U, up_magic), ("gate", F_2, gate_scaled)):
                    ap = piece(Q[which], i)
                    act.activation(ap, ap, ACT.Identity, scale=sc[:, f:f + 1], bias=magic[:, 0:1]).then_inc(done, 1)
            act.wait_ge(scales, 4)
            for b in range(B):
                for part in range(2):
                    ap = some_gate(b, part)
                    act.activation(ap, ap, ACT.Identity, scale=sc[:, F_O:F_O + 1],
                                   bias=magic[:, 0:1]).then_inc(o_scaled, 1)

        @block.vector
        def _(dve):
            def route_slots():
                dve.wait_ge(idx_in, 16)
                link(dve, dve.tensor_copy(idxf[:, :, :], idx[:, :, :]))
                for e in range(E):
                    last = dve.tensor_scalar(hot[:, :, :, e], idxf[:, :, :], float(e), None, ALU.is_equal)
                link(dve, last)
                dve.tensor_tensor(slots[:, :, :], hot[:, :, 0, :], hot[:, :, 1, :], ALU.add).then_inc(onehots, 1)
                dve.wait_ge(ranks, 1)
                dve.tensor_copy(totals[:, :, :].rearrange("p i e -> p (i e)"), bank(1)[:, 0:ROUTED * E])
                dve.tensor_copy(place[:, :, :].rearrange("p i e -> p (i e)"),
                                bank(0)[:, 0:ROUTED * E]).then_inc(ranks_taken, 1)

            def route_tiles():
                dve.wait_ge(ranks_taken, 1)
                link(dve, dve.memset(before[:, 0, :], 0.0))
                for i in range(1, ROUTED):
                    link(dve, dve.tensor_tensor(before[:, i, :], before[:, i - 1, :], totals[:, i - 1, :], ALU.add))
                link(dve, dve.tensor_tensor(rt[0][:, :], before[:, ROUTED - 1, :], totals[:, ROUTED - 1, :], ALU.add))
                link(dve, dve.tensor_scalar(rti[0][:, :], rt[0][:, :], float(P - 1), None, ALU.add))
                link(dve, dve.tensor_scalar(rti[1][:, :], rti[0][:, :], 7, None, ALU.arith_shift_right))
                link(dve, dve.tensor_copy(rt[1][:, :], rti[1][:, :]))
                link(dve, dve.tensor_copy(upto[:, 0:1], rt[1][:, 0:1]))
                for e in range(1, E):
                    link(dve, dve.tensor_tensor(upto[:, e:e + 1], upto[:, e - 1:e], rt[1][:, e:e + 1], ALU.add))

            def route_places():
                link(dve, dve.tensor_tensor(rt[2][:, :], upto[:, :], rt[1][:, :], ALU.subtract))
                link(dve, dve.tensor_scalar(rt[3][:, :], rt[2][:, :], float(P), None, ALU.mult))
                link(dve, dve.tensor_tensor(place[:, :, :], place[:, :, :], before[:, :, :], ALU.add))
                link(dve, dve.tensor_tensor(place[:, :, :], place[:, :, :],
                                            rt[3][:, :].unsqueeze(1).to_broadcast([P, ROUTED, E]), ALU.add))
                for k in range(TOPK):
                    link(dve, dve.tensor_tensor(picked[:, :, :], place[:, :, :], hot[:, :, k, :], ALU.mult))
                    link(dve, dve.tensor_reduce(posf[:, k, :], picked[:, :, :], AX.X, ALU.add))
                    if k == 0:
                        link(dve, dve.tensor_tensor(place[:, :, :], place[:, :, :], hot[:, :, 0, :], ALU.add))
                link(dve, dve.tensor_copy(pos_i[:, :, :], posf[:, :, :]))

            def route_experts():
                dve.tensor_copy(tile_f[:, :], tile_no[:, :])
                link(dve, dve.memset(ex[0][:, :], 0.0))
                for e in range(E):
                    link(dve, dve.scalar_tensor_tensor(ex[(e + 1) % 2][:, :], tile_f[0:1, :], upto[0:1, e:e + 1],
                                                       ex[e % 2][:, :], ALU.is_ge, ALU.add))
                link(dve, dve.tensor_scalar(ex[1][:, :], ex[0][:, :], float(E - 1), None, ALU.min))
                dve.tensor_copy(expert_i[:, :], ex[1][:, :]).then_inc(routed, 1)

            def norm_stats(tiles, k):
                for i in tiles:
                    if k == 0 and i % TB == 0:
                        dve.wait_ge(x_in[i // TB], 16)
                    last = dve.bn_stats(stats[:, i, :], X[:, i, :])
                return last

            def norm(k, left=None):
                tiles = NORM_TILES[k]
                last = norm_stats(tiles if left is None else left, k)
                link(dve, last)
                for i in tiles:
                    last = dve.bn_aggr(mv[:, i, :], stats[:, i, :])
                link(dve, last)
                dve.tensor_scalar(ve[:, :], mv[:, :, 1], EPS, None, ALU.add).then_inc(ln_var, 1)
                dve.wait_ge(ln_sd, k + 1)
                link(dve, dve.reciprocal(nw1[:, :], sd[:, :]))
                link(dve, dve.tensor_tensor(nw2[:, :], ve[:, :], nw1[:, :], ALU.mult))
                link(dve, dve.tensor_tensor(nw1[:, :], nw2[:, :], sd[:, :], ALU.add))
                link(dve, dve.tensor_scalar(nw2[:, :], nw1[:, :], 0.5, None, ALU.mult))
                link(dve, dve.reciprocal(rstd[:, :], nw2[:, :]))
                for i in tiles:
                    dve.tensor_scalar(XN[:, i, :], X[:, i, :], mv[:, i, 0:1], rstd[:, i:i + 1],
                                      ALU.subtract, ALU.mult).then_inc(xn_ready, 1)

            def prep(layer, after):
                dve.wait_ge(ab_in, 48 * (layer + 1))
                dve.wait_ge(gp_consts, 8 + layer)
                for n in range(B * layer, B * layer + B):
                    for j in range(4):
                        which, c = 1 - j // 2, j % 2
                        if j == 2:
                            for t2 in range(2):
                                dve.wait_ge(v_done, 2 * n + t2 + 1)
                                wait(dve, v_out, 16 * n)
                                for t in range(2):
                                    last = dve.tensor_tensor(
                                        VB[:, 2 * t2 + t, :, 0:DK],
                                        bank(6 + t2)[:, t * D:t * D + D].rearrange("p (h d) -> p h d", h=H),
                                        BV.rearrange("p (h d) -> p h d", h=H), ALU.add)
                                last.then_inc(v_taken, 1)
                        dve.wait_ge(hi_done, 4 * n + j + 1)
                        wait(dve, lo_done, 4 * n + j - 1)
                        dve.scalar_tensor_tensor(RB[:, j % 2, :], bank(2 + j),
                                                 BQK[:, 2 * which + c:2 * which + c + 1], PT[:, j, 0, :],
                                                 ALU.add, ALU.subtract).then_inc(r_done, 1)
                        dve.wait_ge(r_done, 4 * n + j + 1)
                        dve.tensor_copy(PT[:, j, 1, :], RB[:, j % 2, :]).then_inc(mid_done, 1)
                        after(n - B * layer, j)

            def maxima(n, g, some):
                wait(dve, max_parts, NG * n + g - 1)
                for i in some:
                    dve.wait_ge(max_done, 16 * (NG * n + g) + i + 1)
                    dve.tensor_reduce(MX[:, g % 2, i % TB, i // TB:i // TB + 1], SM[i % 2], AX.X, ALU.max,
                                      negate=True).then_inc(max_taken, 1)

            def normalise(s, n, g):
                dve.wait_ge(ot_turned, s + 1)
                o = MISC.rearrange("p (t h d) -> p t h d", t=TB, h=G)
                dve.reciprocal(rden[:, :, :], o[:, :, :, DK]).then_inc(rden_ready, 1)
                dve.wait_ge(rden_ready, s + 1)
                to = BIG[:, bass.ds(24576 + n * (TB * D), TB * D)].rearrange("p (t n) -> p t n", t=TB)
                dve.tensor_tensor(to[:, :, g * G * DK:(g + 1) * G * DK].rearrange("p t (h d) -> p t h d", h=G),
                                  o[:, :, :, 0:DK], rden[:, :, :].unsqueeze(3).to_broadcast([P, TB, G, DK]),
                                  ALU.mult).then_inc(o_ready, 1)

            def weight_scales(k):
                dve.wait_ge(qw_in, 48)
                w, wb, nb = quant_weight(k)
                link(dve, dve.tensor_reduce(ws[:, k, 0, 0:nb], wb, AX.X, ALU.max, apply_absolute_value=True))
                link(dve, dve.tensor_scalar(ws[:, k, 1, 0:nb], ws[:, k, 0, 0:nb], 1.0 / 7.0, TINY, ALU.mult, ALU.max))
                dve.reciprocal(ws[:, k, 2, 0:nb], ws[:, k, 1, 0:nb]).then_inc(w_scales, 1)

            def attention(layer):
                dve.memset(PV, 0.0).then_inc(pv_zero, 1)
                n0 = B * layer
                for g in range(2):
                    maxima(n0, g, range(16))

                def batch(n, first, last):
                    for g in range(NG):
                        ahead = not (last and g >= 2)
                        if ahead:
                            maxima(n + (g + 2) // NG, (g + 2) % NG, range(12))
                        early = last and g >= 2
                        if early and layer and g == 2:
                            weight_scales(0)
                        for i in range(TB * (g - 2) - 1, TB * (g - 2) + 2) if early else ():
                            if i >= 0:
                                update(layer, i, 5)
                        if not (first and g == 0):
                            m = n if g else n - 1
                            normalise(NG * n + g - 1, m - n0, (g + 3) % NG)
                        if ahead:
                            maxima(n + (g + 2) // NG, (g + 2) % NG, range(12, 16))
                        if early:
                            update(layer, TB * (g - 2) + 2, 5)
                            if layer and g == 2:
                                weight_scales(1)
                            elif layer == 0 and g == NG - 1:
                                dve.wait_ge(x_upd, EARLY - 2)
                                norm_stats(range(EARLY - 2), 1)
                over_batches(dve, layer, batch)
                update(layer, EARLY - 1, 5)
                normalise(NG * (n0 + B) - 1, B - 1, NG - 1)

            def update(layer, i, source):
                t, tile = NT * layer + i, x_tile(layer, i)
                dve.wait_ge(out_done, t + 1)
                if layer:
                    dve.wait_ge(biased, NT + tile + 1)
                dve.scalar_tensor_tensor(X[:, tile, :], bank(source)[:, 0:D], tg[:, layer:layer + 1], X[:, tile, :],
                                         ALU.mult, ALU.add).then_inc(x_upd, 1)

            def tail(layer):
                for i in range(EARLY, NT):
                    update(layer, i, 2 + i % 2)

            dve.wait_ge(gp_consts, 8)
            route_slots()
            norm(0)

            def after(p, j):
                if j == 3 and p < 3:
                    (route_tiles, route_places, route_experts)[p]()

            prep(0, after)
            attention(0)
            dve.wait_ge(x_upd, EARLY)
            norm(1, range(EARLY - 2, EARLY))
            dve.wait_ge(tg_ready, 1)
            dve.wait_ge(ew_in, 32)
            dve.tensor_scalar(bias_row[:, :], bias_row[:, :], tg[:, 2:3], None, ALU.mult).then_inc(tg_bias, 1)
            tail(0)

            def turned(m, q):
                for half in range(2):
                    dve.wait_ge(ht_turned, 2 * (2 * m + q) + half + 1)
                    dve.tensor_copy(M["ht"][:, q, 4 * half:4 * half + 4, :].rearrange("p c n -> p (c n)"),
                                    bank(2 + half)).then_inc(ht_ready, 1)

            def slots_turned(m, q, ahead):
                dve.wait_ge(xs_turned, 2 * m + q + ahead + 1)
                dve.tensor_copy(M["xst"][:, (q + ahead) % 2, :],
                                bank(6 + (q + ahead) % 2)[:, 0:D]).then_inc(xst_ready, 1)

            slots_turned(0, 0, 0)
            slots_turned(0, 1, 0)

            def expert_tile(m, q, t):
                turned(m, q)
                if t is None or t + 2 < SLOT_TILES:
                    slots_turned(m, q, 2)
            over_tiles(dve, expert_tile)

            def combine(i):
                dve.wait_ge(gathered[i], 16 * TOPK)
                y0, y1 = M["got"][:, 0, i, :], M["got"][:, 1, i, :]
                link(dve, dve.tensor_scalar(y0, y0, ew[:, i, 0:1], None, ALU.mult))
                link(dve, dve.scalar_tensor_tensor(y0, y1, ew[:, i, 1:2], y0, ALU.mult, ALU.add))
                dve.scalar_tensor_tensor(X[:, i, :], y0, tg[:, 2:3], X[:, i, :],
                                         ALU.mult, ALU.add).then_inc(combined, 1)

            dve.wait_ge(biased, NT)
            dve.wait_ge(y_done, SLOT_TILES)
            norm(2)
            dve.wait_ge(ab_in, 48 * 2)
            dve.tensor_scalar(bias_row[:, :], TGBO, tg[:, 1:2], None, ALU.mult).then_inc(tg_bias, 1)

            def after(p, j):
                if p in (1, 2):
                    combine(TB * (p - 1) + j)
                    if j == TB - 1:
                        dve.wait_ge(combined, TB * p)
                        norm(2 + p)

            prep(1, after)
            attention(1)
            dve.wait_ge(x_upd, NT + EARLY)
            norm_stats([x_tile(1, i) for i in range(EARLY)], 5)
            weight_scales(2)
            tail(1)
            dve.wait_ge(x_upd, 2 * NT)
            norm(5, [x_tile(1, i) for i in range(EARLY, NT)])

            def spread_max(r, count):
                dve.wait_ge(max_col_turned, r + 1)
                dve.tensor_reduce(one[0:1, 0:count], bank(5)[0:1, 0:count * P].rearrange("p (k n) -> p k n", k=count),
                                  AX.X, ALU.max).then_inc(max_one, 1)
                dve.wait_ge(max_spread, r + 1)
                link(dve, dve.tensor_copy(sc[:, A_MAX:A_MAX + count], bank(4)[:, 0:count]))

            dve.wait_ge(xn_ready, NORM_BASE[5] + NT)
            for i in range(4):
                last = dve.tensor_reduce(cmx[:, i:i + 1], Pt[:, i * 1024:(i + 1) * 1024], AX.X, ALU.max,
                                         apply_absolute_value=True)
            link(dve, last)
            dve.tensor_reduce(cm[:, 0:1], cmx[:, 0:4], AX.X, ALU.max).then_inc(col_max, 1)
            spread_max(0, 1)
            link(dve, dve.tensor_scalar(sc[:, S_X:S_X + 1], sc[:, A_MAX:A_MAX + 1], 1.0 / QMAX, TINY, ALU.mult, ALU.max))
            dve.reciprocal(sc[:, F_X:F_X + 1], sc[:, S_X:S_X + 1]).then_inc(scales, 1)
            for i in range(B):
                dve.wait_ge(q_magic, i + 1)
                ap = Q["xt"][:, :, i * S:(i + 1) * S]
                dve.tensor_scalar(ap, ap, MAGIC, None, ALU.subtract).then_inc(nx_ready, 1)

            def bank_max(k):
                dve.wait_ge(ug_copied, k + 1)
                return dve.tensor_reduce(cmx[:, k // BANKS * 32 + k % BANKS:k // BANKS * 32 + k % BANKS + 1], ug_place(k),
                                         AX.X, ALU.max, apply_absolute_value=True)

            def next_scale(col, unit, s_, f_):
                link(dve, dve.tensor_tensor(sc[:, T0:T0 + 1], sc[:, A_MAX + col:A_MAX + col + 1], unit, ALU.mult))
                link(dve, dve.tensor_scalar(sc[:, s_:s_ + 1], sc[:, T0:T0 + 1], 1.0 / QMAX, TINY, ALU.mult, ALU.max))
                link(dve, dve.reciprocal(sc[:, T1:T1 + 1], sc[:, s_:s_ + 1]))
                return dve.tensor_tensor(sc[:, f_:f_ + 1], sc[:, T1:T1 + 1], unit, ALU.mult)

            for k in range(BANKS):
                last = bank_max(k)
            link(dve, last)
            dve.tensor_reduce(cm[:, 0:1], cmx[:, 0:BANKS], AX.X, ALU.max).then_inc(col_max, 1)
            spread_max(1, 1)
            next_scale(0, sc[:, S_X:S_X + 1], S_G, F_G).then_inc(scales, 1)

            for k in range(BANKS, BANKS + AHEAD):
                last = bank_max(k)
            for i in range(PIECES + 2):
                for k in range(BANKS + AHEAD + 2 * i, min(BANKS + AHEAD + 2 * i + 2, 2 * BANKS)):
                    last = bank_max(k)
                if 0 < i <= PIECES:
                    sg = Q["sig"][:, (i - 1) % SIGS, :]
                    dve.wait_ge(sig_done, i)
                    dve.tensor_scalar(sg, sg, SIG_MAX, SIG_MAGIC, ALU.min, ALU.add).then_inc(sig_round, 1)
                if i > 1:
                    dve.wait_ge(prod_done, i - 1)
                    last = dve.tensor_reduce(cmx[:, i - 2:i - 1], piece(Q["gate"], i - 2), AX.X, ALU.max,
                                             apply_absolute_value=True)
                if 0 < i <= PIECES:
                    ap = piece(Q["gate"], i - 1)
                    dve.wait_ge(sig_round, i)
                    dve.scalar_tensor_tensor(ap, sg, SIG_MAGIC, ap, ALU.subtract, ALU.mult).then_inc(prod_done, 1)
            link(dve, last)
            dve.tensor_reduce(cm[:, 0:1], cmx[:, 0:PIECES], AX.X, ALU.max)
            dve.tensor_reduce(cm[:, 1:2], cmx[:, 32:32 + BANKS], AX.X, ALU.max).then_inc(col_max, 1)
            spread_max(2, 2)
            link(dve, next_scale(1, sc[:, S_X:S_X + 1], S_U, F_U))
            next_scale(0, sc[:, S_G:S_G + 1], S_2, F_2).then_inc(scales, 1)
            for i in range(PIECES + 1):
                if i < PIECES:
                    ap = piece(Q["gate"], i)
                    dve.wait_ge(gate_scaled, i + 1)
                    dve.wait_ge(up_int, i + 1)
                    dve.scalar_tensor_tensor(ap, ap, MAGIC, piece(Q["up"], i), ALU.subtract,
                                             ALU.mult).then_inc(prod_done, 1)
                if i > 0:
                    dve.wait_ge(prod_done, PIECES + i)
                    last = dve.tensor_reduce(cmx[:, i - 1:i], piece(Q["gate"], i - 1), AX.X, ALU.max,
                                             apply_absolute_value=True)
            link(dve, last)
            dve.tensor_reduce(cm[:, 0:1], cmx[:, 0:PIECES], AX.X, ALU.max).then_inc(col_max, 1)
            spread_max(3, 1)
            link(dve, dve.tensor_tensor(sc[:, UNIT:UNIT + 1], sc[:, S_2:S_2 + 1], sc[:, S_U:S_U + 1], ALU.mult))
            next_scale(0, sc[:, UNIT:UNIT + 1], S_O, F_O).then_inc(scales, 1)
            link(dve, dve.tensor_tensor(sc[:, OUT_F:OUT_F + 1], sc[:, S_O:S_O + 1], tg[:, 3:4], ALU.mult))
            for b in range(B + 1):
                if b < B:
                    for part in range(2):
                        ap = some_gate(b, part)
                        dve.wait_ge(o_scaled, 2 * b + part + 1)
                        dve.tensor_scalar(ap, ap, MAGIC, None, ALU.subtract).then_inc(o_int, 1)
                if b > 0:
                    for i in range(TB * (b - 1), TB * b):
                        dve.wait_ge(dn_done, i + 1)
                        dve.scalar_tensor_tensor(X[:, i, :], bank(i % 4)[:, 0:D], sc[:, OUT_F:OUT_F + 1], X[:, i, :],
                                                 ALU.mult, ALU.add).then_inc(y_final, 1)

        @block.tensor
        def _(pe):
            pe.wait_ge(consts, 3)
            pe.wait_ge(gp_consts, 8)
            pe.wait_ge(onehots, 1)
            pe.matmul(bank(0)[:, 0:ROUTED * E], upper[:, :], slots[:, :, :].rearrange("p i e -> p (i e)"),
                      start=True, stop=True)
            pe.matmul(bank(1)[:, 0:ROUTED * E], ones[:, :], slots[:, :, :].rearrange("p i e -> p (i e)"),
                      start=True, stop=True).then_inc(ranks, 1)

            def prep(layer):
                pe.wait_ge(aw_in, 16 * (layer + 1))
                for p in range(B):
                    b, n = ORDER[layer][p], B * layer + p
                    pe.wait_ge(ct_in[b], 16 * (layer + 1))
                    project(n, b, (0, 1))
                    late = p > 1 if layer else p == 0
                    if not late:
                        turn_x(n, b)
                    project_v(n, b)
                    if late:
                        turn_x(n, b)
                    pe.wait_ge(xnt_evac, KC * (n + 1))
                    project(n, b, (2, 3))

            def turn_x(n, b):
                pe.wait_ge(xn_ready, NORM_BASE[2 * (n // B)] + TB * (n % B + 1))
                pe.wait_ge(ranks_taken, 1)
                wait(pe, xnt_evac, KC * n)
                for c in range(KC):
                    for t in range(TB):
                        last = pe.transpose(bank(c)[:, t * P:(t + 1) * P], XN[:, TB * b + t, c * P:(c + 1) * P],
                                            identf[:, :])
                    last.then_inc(tr_done, 1)

            def project(n, b, some):
                for j in some:
                    which, c = 1 - j // 2, j % 2
                    wait(pe, r_done, 4 * (n - 1) + j + 1 if n > 0 else 0)
                    for kc in range(KC):
                        rhs = CT[:, kc, b * S:(b + 1) * S] if which else XNT[:, kc, :]
                        last = pe.matmul(bank(2 + j), AW[:, which * KC + kc, c * P:(c + 1) * P], rhs,
                                         start=(kc == 0), stop=(kc == KC - 1))
                    last.then_inc(qk_done, 1)

            def project_v(n, b):
                for t in range(TB):
                    wait(pe, v_taken, 2 * (n - 1) + t // 2 + 1 if n > 0 else 0)
                    for kc in range(KC):
                        last = pe.matmul(bank(6 + t // 2)[:, (t % 2) * D:(t % 2) * D + D],
                                         CT[:, kc, (TB * b + t) * P:(TB * b + t + 1) * P],
                                         AW[:, 2 * KC + kc, :], start=(kc == 0), stop=(kc == KC - 1))
                    if t % 2:
                        last.then_inc(v_done, 1)

            def max_scores(n, g, some):
                for i in some:
                    h, qc = i // TB, i % TB
                    if i == 0:
                        pe.wait_ge(q_stack[g], 96 * (n + 1))
                    wait(pe, max_taken, 16 * (NG * n + g) + i - 1)
                    pe.matmul(SM[i % 2], QS[0:ROWS, g, h, qc * P:(qc + 1) * P], KS[0:ROWS, g, h, :],
                              start=True, stop=True).then_inc(max_done, 1)

            def turn_max(n, g):
                s = NG * n + g
                pe.wait_ge(max_parts, s + 1)
                wait(pe, o_ready, s - 2)
                for t in range(TB):
                    last = pe.transpose(MISC[0:PARTS * G, t * P // 2:(t + 1) * P // 2].bitcast(BF16),
                                        MP[:, t, :, :].rearrange("p r h -> p (r h)"), identb[:, :])
                last.then_inc(max_turned, 1)

            def key_scores(s, n, g, kc, half):
                if kc == 0 and half == 0:
                    pe.wait_ge(max_rows[g], 16 * (n + 1))
                wait(pe, exp_done, 2 * (4 * s + kc) + half - 1)
                for i in range(2):
                    h = 2 * half + i
                    last = pe.matmul(ST[half][:, i * S:(i + 1) * S], KS[0:ROWS + PARTS, g, h, kc * P:(kc + 1) * P],
                                     QS[0:ROWS + PARTS, g, h, :], start=True, stop=True)
                last.then_inc(st_done, 1)

            def values(s, n, g, kc, half):
                pe.wait_ge(exp_done, 2 * (4 * s + kc) + half + 1)
                if kc == 0 and half == 0:
                    pe.wait_ge(v_stack[g], 16 * (n + 1))
                    wait(pe, ot_ready, s)
                for h in (2 * half, 2 * half + 1):
                    last = pe.matmul(PV[32 * h:32 * h + DK + 1, :], VS[:, g, kc, h, :],
                                     PP[:, 2 * (kc % 2) + h // 2, h % 2, :], start=(kc == 0), stop=(kc == TB - 1),
                                     tile_position=(0, 32 * h))
                if half == 1:
                    last.then_inc(pv_done, 1)

            def turn_outputs(s, q, max_too):
                pe.wait_ge(ot_ready, s + 1)
                if max_too:
                    pe.wait_ge(max_copied, s + 3)
                else:
                    pe.wait_ge(o_ready, s)
                for t in range(TB):
                    last = pe.transpose(MISC[:, t * P:(t + 1) * P], OT[:, q, t * P:(t + 1) * P], identf[:, :])
                last.then_inc(ot_turned, 1)

            def attention(layer):
                n0 = B * layer
                if layer:
                    pe.wait_ge(ones_back, 16)
                else:
                    pe.wait_ge(ones_rows, 1)
                pe.wait_ge(pv_zero, layer + 1)
                pe.wait_ge(r_done, 4 * B * (layer + 1))
                pe.wait_ge(v_taken, 2 * B * (layer + 1))
                for g in range(2):
                    max_scores(n0, g, range(16))
                turn_max(n0, 0)

                def batch(n, first, last):
                    for g in range(NG):
                        s = NG * n + g
                        for kc in range(TB):
                            early = last and g >= 2
                            for i in range(4):
                                if early and i == 3 and (g > 2 or kc > 0):
                                    project_out(layer, TB * (g - 2) + kc - 1, 5)
                                if early and i == 2:
                                    turn_tile(layer, TB * (g - 2) + kc, 4)
                                if i < 2:
                                    key_scores(s, n, g, kc, i)
                                elif kc > 0:
                                    values(s, n, g, kc - 1, i - 2)
                                elif g > 0:
                                    values(s - 1, n, g - 1, TB - 1, i - 2)
                                elif not first:
                                    values(s - 1, n - 1, NG - 1, TB - 1, i - 2)
                                if not (last and g >= 2):
                                    max_scores(n + (g + 2) // NG, (g + 2) % NG, range(4 * kc + i, 4 * kc + i + 1))
                            if kc == 1 and not (last and g == NG - 1):
                                turn_max(n + (g + 1) // NG, (g + 1) % NG)
                            if kc == 2 and not (first and g == 0):
                                turn_outputs(s - 1, (g + 1) % 2, not (last and g == NG - 1))
                over_batches(pe, layer, batch)
                n = n0 + B - 1
                s = NG * n + NG - 1
                for half in range(2):
                    values(s, n, NG - 1, TB - 1, half)
                project_out(layer, EARLY - 1, 5)
                turn_outputs(s, 1, False)

            def turn_tile(layer, i, to):
                t = NT * layer + i
                if i == 0:
                    pe.wait_ge(o_ready, NG * (B * layer + EARLY // TB))
                    pe.wait_ge(max_taken, 16 * NG * B * (layer + 1))
                elif to == 4:
                    pe.wait_ge(on_evac, t)
                elif i >= EARLY + 2:
                    pe.wait_ge(on_evac, t - 1)
                for c in range(KC):
                    last = pe.transpose(bank(to)[:, c * P:(c + 1) * P], OALL[:, i, c * P:(c + 1) * P], identf[:, :])
                last.then_inc(tro_done, 1)

            def project_out(layer, i, to):
                t = NT * layer + i
                pe.wait_ge(wo_in, 16 * (layer + 1))
                pe.wait_ge(on_evac, t + 1)
                if to == 5 and i > 0:
                    pe.wait_ge(x_upd, t)
                elif i >= EARLY + 2:
                    pe.wait_ge(x_upd, t - 1)
                for c in range(KC):
                    last = pe.matmul(bank(to)[:, 0:D], TT[:, i % 2, c * P:(c + 1) * P], WO[:, c, :],
                                     start=(c == 0), stop=(c == KC - 1))
                last.then_inc(out_done, 1)

            def tail(layer):
                pe.wait_ge(o_ready, NG * B * (layer + 1))
                pe.wait_ge(exp_done, 8 * NG * B * (layer + 1))
                for i in range(EARLY, NT + 1):
                    if i < NT:
                        turn_tile(layer, i, i % 2)
                    if i > EARLY:
                        project_out(layer, i - 1, 2 + (i - 1) % 2)

            prep(0)
            attention(0)
            tail(0)

            def turn_slots(m, q, ahead):
                p = (q + ahead) % 2
                pe.wait_ge(xs_in[p], 16 * (m + (q + ahead) // 2 + 1))
                wait(pe, xst_ready, 2 * m + q + ahead - 1)
                for c in range(KC):
                    last = pe.transpose(bank(6 + p)[:, c * P:(c + 1) * P], M["xs"][:, p, c * P:(c + 1) * P], identf[:, :])
                last.then_inc(xs_turned, 1)

            def expert_of(m, q, ahead):
                t = 2 * m + q + ahead
                return pe.value_load(expert_i[0:1, bass.ds(t, 1)], min_val=0, max_val=E - 1)

            def hidden(m, q, ahead, e):
                t = 2 * m + q + ahead
                p = (q + ahead) % 2
                pe.wait_ge(xst_ready, t + 1)
                for half in range(2):
                    wait(pe, gelu_done, 2 * t + half - 1)
                    for c in range(KC):
                        last = pe.matmul(bank(half), M["xst"][:, p, c * P:(c + 1) * P],
                                         W1[:, bass.ds(e * (KC * FF) + (c * FF + half * 512), 512)],
                                         start=(c == 0), stop=(c == KC - 1))
                    last.then_inc(h_done, 1)

            def expert_tile(m, q, t):
                n = 2 * m + q
                for half in range(2):
                    pe.wait_ge(gelu_done, 2 * n + half + 1)
                    wait(pe, ht_ready, 2 * n + half - 1)
                    for c in range(4 * half, 4 * half + 4):
                        last = pe.transpose(bank(2 + half)[:, (c % 4) * P:(c % 4 + 1) * P],
                                            M["h"][:, q, c * P:(c + 1) * P], identf[:, :])
                    last.then_inc(ht_turned, 1)
                if t is None or t + 1 < SLOT_TILES:
                    hidden(m, q, 1, expert_of(m, q, 1))
                if t is None or t + 2 < SLOT_TILES:
                    turn_slots(m, q, 2)
                e = expert_of(m, q, 0)
                pe.wait_ge(ht_ready, 2 * n + 2)
                wait(pe, ys_ready, n - 1)
                for c in range(FC):
                    last = pe.matmul(bank(4 + q)[:, 0:D], M["ht"][:, q, c, :],
                                     W2[:, bass.ds(e * (FC * D) + c * D, D)], start=(c == 0), stop=(c == FC - 1))
                last.then_inc(y_done, 1)

            turn_slots(0, 0, 0)
            turn_slots(0, 1, 0)
            pe.wait_ge(on_evac, NT)
            pe.wait_ge(x_upd, NT)
            pe.wait_ge(w1_in, 16 * E)
            hidden(0, 0, 0, expert_of(0, 0, 0))
            pe.wait_ge(w2_in, 16 * (E - 4))
            pe.wait_ge(w2_late, 16 * 4)
            expert_tile(0, 0, 0)
            expert_tile(0, 1, 1)
            with pe.Fori(1, (SLOT_TILES - 3) // 2) as m:
                for q in range(2):
                    expert_tile(m, q, None)
            for t in range(SLOT_TILES - 3, SLOT_TILES):
                expert_tile(t // 2, t % 2, t)

            pe.wait_ge(ys_ready, SLOT_TILES)
            prep(1)
            attention(1)
            tail(1)

            def turn_weight(k, first_bank):
                pe.wait_ge(qw_ready, k + 1)
                chunks = QC if k < 2 else KC
                w = Q["raw"][:, k * QC * D:(k + 1) * QC * D].rearrange("p (c n) -> p c n", c=chunks)
                for a in range(12):
                    ci, co = a // chunks, a % chunks
                    if a % 4 == 0 and k == 1:
                        pe.wait_ge(qwt_ready, a // 4 + 1)
                    last = pe.transpose(bank(first_bank + a // 4)[:, (a % 4) * P:(a % 4 + 1) * P],
                                        w[:, co, ci * P:(ci + 1) * P], identf[:, :])
                    if a % 4 == 3:
                        last.then_inc(qwt_turned, 1)

            turn_weight(0, 4)
            turn_weight(1, 4)
            pe.wait_ge(x_upd, 2 * NT)
            for i in range(B):
                pe.wait_ge(xn_ready, NORM_BASE[5] + TB * (i + 1))
                for c in range(KC):
                    wait(pe, nxt_ready, 2 * (i - 2) + c + 1 if i > 1 else 0)
                    for t in range(TB):
                        last = pe.transpose(bank(i % 2 * 2 + c)[:, t * P:(t + 1) * P],
                                            XN[:, TB * i + t, c * P:(c + 1) * P], identf[:, :])
                    last.then_inc(nx_turned, 1)

            def spread_max(r, count):
                pe.wait_ge(col_max, r + 1)
                for k in range(count):
                    last = pe.transpose(bank(5)[0:1, k * P:(k + 1) * P], cm[:, k:k + 1], identf[:, :])
                last.then_inc(max_col_turned, 1)
                pe.wait_ge(max_one, r + 1)
                pe.matmul(bank(4)[:, 0:count], ones[0:1, :], one[0:1, 0:count], start=True, stop=True
                          ).then_inc(max_spread, 1)

            pe.wait_ge(qwt_ready, 6)
            spread_max(0, 1)
            pe.wait_ge(nxt_ready, 2 * B)
            wt = Q["wt"]
            for k in range(2 * BANKS):
                c, b, w = k % QC, k // QC % B, k // BANKS
                pe.wait_ge(nx_ready, b + 1)
                if k >= 4:
                    pe.wait_ge(ug_copied, k - 3)
                if k == BANKS:
                    pe.wait_ge(qwt_ready, 9)
                for kc in range(KC):
                    at = w * QC * D + kc * QF + c * P
                    last = pe.matmul(bank(k % 4), wt[:, at:at + P], Q["xt"][:, kc, b * S:(b + 1) * S],
                                     start=(kc == 0), stop=(kc == KC - 1))
                last.then_inc(ug_done, 1)
                if k == BANKS - 1:
                    pe.wait_ge(ug_copied, BANKS)
                    turn_weight(2, 0)
                if k == BANKS + 1:
                    spread_max(1, 1)
            spread_max(2, 2)
            spread_max(3, 1)
            for i in range(NT):
                pe.wait_ge(o_int, 2 * (i // TB + 1))
                if i >= 4:
                    pe.wait_ge(y_final, i - 3)
                for c in range(QC):
                    at = 2 * QC * D + c * D
                    last = pe.matmul(bank(i % 4)[:, 0:D], Q["gate"][:, c, i * P:(i + 1) * P], wt[:, at:at + D],
                                     start=(c == 0), stop=(c == QC - 1))
                last.then_inc(dn_done, 1)


_NAMES = ("x", "ctx_t", "gates", "attn_w", "attn_bqk", "attn_bvo", "expert_indices", "expert_weights", "moe_bias",
          "w1", "w2", "w_gate", "w_up", "w_down")


def layout(inputs):
    a = {k: np.ascontiguousarray(v) for k, v in inputs.items()}

    def by_step(w):
        return np.ascontiguousarray(w.reshape(w.shape[:-1] + (NG, G, DK)).swapaxes(-1, -2)).reshape(w.shape)

    zero = np.zeros(D, a["x"].dtype)
    return {
        "x": a["x"],
        "ctx_t": np.ascontiguousarray(a["ctx_1024"].reshape(B * S, D).T),
        "gates": np.concatenate([a["g_xattn"], a["g_ffn"]]),
        "attn_w": np.stack([
            np.stack([by_step(a["L0_xattn_W_q"].T), by_step(a["L0_xattn_W_k"].T), a["L0_xattn_W_v"].T,
                      a["L0_xattn_W_o"].T]),
            np.stack([by_step(a["L1_xattn_Wq"]), by_step(a["L1_xattn_Wk"]), a["L1_xattn_Wv"], a["L1_xattn_Wo"]])]),
        "attn_bqk": np.stack([np.stack([zero] * 2).reshape(2 * KC, P).T, np.stack(
            [by_step(a["L1_xattn_bq"]), by_step(a["L1_xattn_bk"])]).reshape(2 * KC, P).T]),
        "attn_bvo": np.stack([np.stack([zero] * 2), np.stack([a["L1_xattn_bv"], a["L1_xattn_bo"]])]),
        "expert_indices": a["L0_ffn_expert_indices"],
        "expert_weights": a["L0_ffn_expert_weights"],
        "moe_bias": a["L0_ffn_bias"],
        "w1": a["L0_ffn_w1"],
        "w2": a["L0_ffn_w2"],
        "w_gate": a["L1_ffn_w_gate"],
        "w_up": a["L1_ffn_w_up"],
        "w_down": a["L1_ffn_w_down"],
    }


def kernel(**inputs):
    import concourse.bacc as bacc
    from concourse.bass_utils import run_bass_kernel_spmd

    nc = bacc.Bacc("TRN2", target_bir_lowering=False, num_devices=1)
    arrays = {f"in_{k}": v for k, v in layout(inputs).items()}
    io = {k: nc.dram_tensor(f"in_{k}", arrays[f"in_{k}"].shape, mybir.dt.from_np(arrays[f"in_{k}"].dtype),
                            kind="ExternalInput").ap() for k in _NAMES}
    out = nc.dram_tensor("out_x", (B, S, D), F32, kind="ExternalOutput").ap()
    build_program(nc, io, out)
    result = run_bass_kernel_spmd(nc, [arrays], core_ids=[0])
    return result.results[0]["out_x"]
```
